# Optimizing a Trainium2 kernel written in Bass

```python
import numpy as np
import jax
import jax.numpy as jnp

def _softmax(x, axis=-1):
    return jax.nn.softmax(x, axis=axis)

def _gelu(x):
    return jax.nn.gelu(x, approximate=True)

def _silu(x):
    return jax.nn.silu(x)

def _sigmoid(x):
    return jax.nn.sigmoid(x)

def _layernorm(x, axis=-1, eps=1e-05):
    m = jnp.mean(x, axis=axis, keepdims=True)
    v = jnp.var(x, axis=axis, keepdims=True)
    return (x - m) / jnp.sqrt(v + eps)

def _scatter_add(tgt, idx, src, axis=0):
    return tgt.at[idx].add(src)

def _segment_sum(src, seg, n):
    return jax.ops.segment_sum(src, seg, n)
kernel_name = 'mk_lm_tower_d2_tok_ids2048_r4_e3a833'

def setup_inputs(seed: int=0):
    np.random.seed(seed)
    _w = jnp.asarray

    def _rec_inputs():
        import jax
        import jax.numpy as jnp
        _rk = jax.random.key(seed)
        x = jax.random.randint(jax.random.fold_in(_rk, 1), (8, 512), 0, 12564, jnp.int32)
        return x
    x = _rec_inputs()

    def _L0_tok_setup():
        import jax, jax.numpy as jnp
        import numpy as np
        VOCAB = 50257
        EMBED_DIM = 512
        N_LAYERS = 2
        LOCAL_D = EMBED_DIM // 2 // N_LAYERS
        EMBD_D = EMBED_DIM - LOCAL_D * (2 * N_LAYERS - 1)
        KERNEL = 3
        B, T = (16, 512)

        def positional_encoding(max_len, d_model):
            depth = d_model // 2
            positions = jnp.arange(max_len, dtype=jnp.float32)[:, None]
            depths = jnp.arange(depth, dtype=jnp.float32)[None, :] / depth
            angle_rads = positions * (1.0 / 10000.0 ** depths)
            return jnp.concatenate([jnp.sin(angle_rads), jnp.cos(angle_rads)], axis=-1)

        def softpos_axis1(x, spos):
            n_subpos = spos.shape[0]
            m = x[:, :n_subpos, :]
            sel = jax.nn.softmax(m, axis=1)
            ext = jnp.einsum('bjt,jk->bkt', sel, spos)
            return jnp.concatenate([x, ext], axis=1)
        key = jax.random.key(seed)
        ks = jax.random.split(key, 6)
        return {'sequences': jax.random.randint(ks[0], (B, T), 0, VOCAB), 'emb_table': jax.random.normal(ks[1], (VOCAB, EMBD_D), dtype=jnp.float32), 'conv_w': jax.random.normal(ks[2], (LOCAL_D, EMBD_D, KERNEL), dtype=jnp.float32) * 0.05, 'conv_b': jax.random.normal(ks[3], (LOCAL_D,), dtype=jnp.float32) * 0.05, 'spos0': jax.random.normal(ks[4], (LOCAL_D, LOCAL_D), dtype=jnp.float32) * 0.05, 'spos1': jax.random.normal(ks[5], (LOCAL_D, LOCAL_D), dtype=jnp.float32) * 0.05}
    _L0_tok_all = _L0_tok_setup()
    _L0_tok_in = {k: v for k, v in _L0_tok_all.items() if k in ('emb_table', 'conv_w', 'conv_b', 'spos0', 'spos1')}
    del _L0_tok_all

    def _L0_attn_setup():
        import jax, jax.numpy as jnp
        import numpy as np
        D_MODEL = 512
        NHEAD = 32
        N_KV = 8
        HEAD_DIM = D_MODEL // NHEAD
        EPS = 1e-05

        def weight_quant(w):
            scale = jnp.maximum(jnp.mean(jnp.abs(w)), EPS)
            return jax.lax.stop_gradient(jnp.sign(w) * scale - w) + w

        def bitlinear(x, w):
            return x @ weight_quant(w).T
        key = jax.random.key(seed)
        k1, k2, k3, k4, k5 = jax.random.split(key, 5)
        B, S = (2, 512)
        return {'x': jax.random.normal(k1, (B, S, D_MODEL), dtype=jnp.float32), 'wq': jax.random.normal(k2, (D_MODEL, D_MODEL), dtype=jnp.float32) * 0.02, 'wk': jax.random.normal(k3, (N_KV * HEAD_DIM, D_MODEL), dtype=jnp.float32) * 0.02, 'wv': jax.random.normal(k4, (N_KV * HEAD_DIM, D_MODEL), dtype=jnp.float32) * 0.02, 'wo': jax.random.normal(k5, (D_MODEL, D_MODEL), dtype=jnp.float32) * 0.02}
    _L0_attn_all = _L0_attn_setup()
    _L0_attn_in = {k: v for k, v in _L0_attn_all.items() if k in ('wq', 'wk', 'wv', 'wo')}
    del _L0_attn_all

    def _L0_ffn_setup():
        import jax, jax.numpy as jnp
        import numpy as np
        D_MODEL = 512
        NUM_TILES = 64
        D_SLICE = D_MODEL // NUM_TILES
        TILES_PER_CLUSTER = 8
        NUM_CLUSTERS = NUM_TILES // TILES_PER_CLUSTER
        GRID = 16
        LN_EPS = 1e-05
        DIMS = (np.arange(NUM_TILES)[:, None] * D_SLICE + np.arange(D_SLICE)[None, :]) % D_MODEL
        DIMS = jnp.asarray(DIMS, dtype=jnp.int32)

        def _forward(x, ln_gamma, ln_beta, spline_bases, spline_slopes, output_scale):
            B, S, D = x.shape
            N = B * S
            mu = jnp.mean(x, axis=-1, keepdims=True)
            var = jnp.mean(jnp.square(x - mu), axis=-1, keepdims=True)
            xn = (x - mu) * jax.lax.rsqrt(var + LN_EPS) * ln_gamma + ln_beta
            xf = xn.reshape(N, D)
            slope_sign = jnp.sign(jnp.mean(spline_slopes, axis=-1))
            tile_sigs = jnp.zeros((NUM_TILES, D), dtype=x.dtype)
            tile_sigs = tile_sigs.at[jnp.arange(NUM_TILES)[:, None], DIMS].set(slope_sign)
            cluster_sigs = jnp.sign(tile_sigs.reshape(NUM_CLUSTERS, TILES_PER_CLUSTER, D).mean(axis=1))
            cluster_assign = jnp.arange(NUM_TILES, dtype=jnp.int32) // TILES_PER_CLUSTER
            input_sigs = jnp.sign(xf)
            cluster_scores = input_sigs @ cluster_sigs.T
            best_cluster = jnp.argmax(cluster_scores, axis=-1)
            tile_scores = input_sigs @ tile_sigs.T
            in_cluster = cluster_assign[None, :] == best_cluster[:, None]
            tile_idx = jnp.argmax(jnp.where(in_cluster, tile_scores, -jnp.inf), axis=-1)
            tok_dims = DIMS[tile_idx]
            x_slice = jnp.take_along_axis(xf, tok_dims, axis=1)
            tok_min = x_slice.min(axis=1)
            tok_max = x_slice.max(axis=1)
            onehot = tile_idx[None, :] == jnp.arange(NUM_TILES)[:, None]
            tile_min = jnp.where(onehot, tok_min[None, :], jnp.inf).min(axis=1)
            tile_max = jnp.where(onehot, tok_max[None, :], -jnp.inf).max(axis=1)
            mn = tile_min[tile_idx][:, None]
            mx = tile_max[tile_idx][:, None]
            u = jnp.clip((x_slice - mn) / (mx - mn + 1e-08), 0.0, 1.0 - 1e-06)
            gi = jnp.clip((u * GRID).astype(jnp.int32), 0, GRID - 1)
            j = jnp.arange(D_SLICE)[None, :]
            b = spline_bases[tile_idx[:, None], j, gi]
            s = spline_slopes[tile_idx[:, None], j, gi]
            x_local = (u - gi.astype(u.dtype) / GRID) * GRID
            delta = (b + s * x_local) * output_scale[tile_idx][:, None]
            out = jnp.zeros_like(xf).at[jnp.arange(N)[:, None], tok_dims].set(delta)
            return x + out.reshape(B, S, D)
        key = jax.random.key(seed)
        k1, k2, k3, k4, k5, k6 = jax.random.split(key, 6)
        x = jax.random.normal(k1, (4, 1024, D_MODEL), dtype=jnp.float32)
        ln_gamma = 1.0 + 0.1 * jax.random.normal(k2, (D_MODEL,), dtype=jnp.float32)
        ln_beta = 0.1 * jax.random.normal(k3, (D_MODEL,), dtype=jnp.float32)
        spline_bases = 0.1 * jax.random.normal(k4, (NUM_TILES, D_SLICE, GRID), dtype=jnp.float32)
        spline_slopes = 0.1 + 0.1 * jax.random.normal(k5, (NUM_TILES, D_SLICE, GRID), dtype=jnp.float32)
        output_scale = 1.0 + 0.1 * jax.random.normal(k6, (NUM_TILES,), dtype=jnp.float32)
        return {'x': x, 'ln_gamma': ln_gamma, 'ln_beta': ln_beta, 'spline_bases': spline_bases, 'spline_slopes': spline_slopes, 'output_scale': output_scale}
    _L0_ffn_all = _L0_ffn_setup()
    _L0_ffn_in = {k: v for k, v in _L0_ffn_all.items() if k in ('ln_gamma', 'ln_beta', 'spline_bases', 'spline_slopes', 'output_scale')}
    del _L0_ffn_all

    def _L1_attn_setup():
        import jax, jax.numpy as jnp
        import numpy as np
        N_HEADS = 16
        D_ROPE = 32
        ROPE_BASE = 10000.0
        MASK_FILL = -10000.0

        def _rope(x):
            S = x.shape[1]
            theta = 1.0 / ROPE_BASE ** (jnp.arange(0, D_ROPE, 2, dtype=jnp.float32) / D_ROPE)
            idx_theta = jnp.arange(S, dtype=jnp.float32)[:, None] * theta[None, :]
            idx_theta2 = jnp.concatenate([idx_theta, idx_theta], axis=-1)
            cos = jnp.cos(idx_theta2)[:, None, :].astype(x.dtype)
            sin = jnp.sin(idx_theta2)[:, None, :].astype(x.dtype)
            x_rope, x_pass = (x[..., :D_ROPE], x[..., D_ROPE:])
            half = D_ROPE // 2
            rot = jnp.concatenate([-x_rope[..., half:], x_rope[..., :half]], axis=-1)
            x_rope = x_rope * cos + rot * sin
            return jnp.concatenate([x_rope, x_pass], axis=-1)
        key = jax.random.key(seed)
        k1, k2, k3, k4, k5 = jax.random.split(key, 5)
        B, S, D = (2, 512, 512)
        sc = 0.02
        return {'x': jax.random.normal(k1, (B, S, D), jnp.float32), 'W_qkv': jax.random.normal(k2, (3 * D, D), jnp.float32) * sc, 'b_qkv': jax.random.normal(k3, (3 * D,), jnp.float32) * sc, 'W_out': jax.random.normal(k4, (D, D), jnp.float32) * sc, 'b_out': jax.random.normal(k5, (D,), jnp.float32) * sc}
    _L1_attn_all = _L1_attn_setup()
    _L1_attn_in = {k: v for k, v in _L1_attn_all.items() if k in ('W_qkv', 'b_qkv', 'W_out', 'b_out')}
    del _L1_attn_all

    def _L1_ffn_setup():
        import jax, jax.numpy as jnp
        import numpy as np
        K = 2

        def gelu(v):
            return jax.nn.gelu(v, approximate=False)
        key = jax.random.key(seed)
        ks = jax.random.split(key, 10)
        B, S, D, H, E = (4, 512, 512, 256, 8)
        SH = 2 * H
        u = lambda k_, shape, b: jax.random.uniform(k_, shape, jnp.float32, -b, b)
        return {'x': jax.random.normal(ks[0], (B, S, D), jnp.float32), 'gate_w': u(ks[1], (D, E), 1.0 / D), 'w1': u(ks[2], (E, D, H), 1.0 / D), 'b1': u(ks[3], (E, H), 1.0 / np.sqrt(D)), 'w2': u(ks[4], (E, H, D), 1.0 / H), 'b2': u(ks[5], (E, D), 1.0 / np.sqrt(H)), 'shared_w1': u(ks[6], (D, SH), 1.0 / D), 'shared_b1': u(ks[7], (SH,), 1.0 / np.sqrt(D)), 'shared_w2': u(ks[8], (SH, D), 1.0 / SH), 'shared_b2': u(ks[9], (D,), 1.0 / np.sqrt(SH))}
    _L1_ffn_all = _L1_ffn_setup()
    _L1_ffn_in = {k: v for k, v in _L1_ffn_all.items() if k in ('gate_w', 'w1', 'b1', 'w2', 'b2', 'shared_w1', 'shared_b1', 'shared_w2', 'shared_b2')}
    del _L1_ffn_all
    return {'x': x, 'L0_tok_emb_table': _L0_tok_in['emb_table'], 'L0_tok_conv_w': _L0_tok_in['conv_w'], 'L0_tok_conv_b': _L0_tok_in['conv_b'], 'L0_tok_spos0': _L0_tok_in['spos0'], 'L0_tok_spos1': _L0_tok_in['spos1'], 'L0_attn_wq': _L0_attn_in['wq'], 'L0_attn_wk': _L0_attn_in['wk'], 'L0_attn_wv': _L0_attn_in['wv'], 'L0_attn_wo': _L0_attn_in['wo'], 'L0_ffn_ln_gamma': _L0_ffn_in['ln_gamma'], 'L0_ffn_ln_beta': _L0_ffn_in['ln_beta'], 'L0_ffn_spline_bases': _L0_ffn_in['spline_bases'], 'L0_ffn_spline_slopes': _L0_ffn_in['spline_slopes'], 'L0_ffn_output_scale': _L0_ffn_in['output_scale'], 'L1_attn_W_qkv': _L1_attn_in['W_qkv'], 'L1_attn_b_qkv': _L1_attn_in['b_qkv'], 'L1_attn_W_out': _L1_attn_in['W_out'], 'L1_attn_b_out': _L1_attn_in['b_out'], 'L1_ffn_gate_w': _L1_ffn_in['gate_w'], 'L1_ffn_w1': _L1_ffn_in['w1'], 'L1_ffn_b1': _L1_ffn_in['b1'], 'L1_ffn_w2': _L1_ffn_in['w2'], 'L1_ffn_b2': _L1_ffn_in['b2'], 'L1_ffn_shared_w1': _L1_ffn_in['shared_w1'], 'L1_ffn_shared_b1': _L1_ffn_in['shared_b1'], 'L1_ffn_shared_w2': _L1_ffn_in['shared_w2'], 'L1_ffn_shared_b2': _L1_ffn_in['shared_b2']}

def reference(x, L0_tok_emb_table, L0_tok_conv_w, L0_tok_conv_b, L0_tok_spos0, L0_tok_spos1, L0_attn_wq, L0_attn_wk, L0_attn_wv, L0_attn_wo, L0_ffn_ln_gamma, L0_ffn_ln_beta, L0_ffn_spline_bases, L0_ffn_spline_slopes, L0_ffn_output_scale, L1_attn_W_qkv, L1_attn_b_qkv, L1_attn_W_out, L1_attn_b_out, L1_ffn_gate_w, L1_ffn_w1, L1_ffn_b1, L1_ffn_w2, L1_ffn_b2, L1_ffn_shared_w1, L1_ffn_shared_b1, L1_ffn_shared_w2, L1_ffn_shared_b2):
    import jax
    import jax.numpy as jnp

    def _L0_tok_ref(sequences, emb_table, conv_w, conv_b, spos0, spos1):
        import jax, jax.numpy as jnp
        import numpy as np
        VOCAB = 50257
        EMBED_DIM = 512
        N_LAYERS = 2
        LOCAL_D = EMBED_DIM // 2 // N_LAYERS
        EMBD_D = EMBED_DIM - LOCAL_D * (2 * N_LAYERS - 1)
        KERNEL = 3
        B, T = (16, 512)

        def positional_encoding(max_len, d_model):
            depth = d_model // 2
            positions = jnp.arange(max_len, dtype=jnp.float32)[:, None]
            depths = jnp.arange(depth, dtype=jnp.float32)[None, :] / depth
            angle_rads = positions * (1.0 / 10000.0 ** depths)
            return jnp.concatenate([jnp.sin(angle_rads), jnp.cos(angle_rads)], axis=-1)

        def softpos_axis1(x, spos):
            n_subpos = spos.shape[0]
            m = x[:, :n_subpos, :]
            sel = jax.nn.softmax(m, axis=1)
            ext = jnp.einsum('bjt,jk->bkt', sel, spos)
            return jnp.concatenate([x, ext], axis=1)
        seq_len = sequences.shape[1]
        x = emb_table[sequences] * jnp.sqrt(jnp.float32(EMBD_D))
        x = x + positional_encoding(seq_len, EMBD_D)[None]
        x = jnp.transpose(x, (0, 2, 1))
        dilation = 1
        x_pad = jnp.pad(x, ((0, 0), (0, 0), ((KERNEL - 1) * dilation, 0)))
        xc = jax.lax.conv_general_dilated(x_pad, conv_w, window_strides=(1,), padding='VALID', rhs_dilation=(dilation,), dimension_numbers=('NCH', 'OIH', 'NCH'))
        xc = xc + conv_b[None, :, None]
        y0 = softpos_axis1(x, spos0)
        y1 = softpos_axis1(xc, spos1)
        return jnp.concatenate([y0, y1], axis=1)

    def _L0_attn_ref(x, wq, wk, wv, wo):
        import jax, jax.numpy as jnp
        import numpy as np
        D_MODEL = 512
        NHEAD = 32
        N_KV = 8
        HEAD_DIM = D_MODEL // NHEAD
        EPS = 1e-05

        def weight_quant(w):
            scale = jnp.maximum(jnp.mean(jnp.abs(w)), EPS)
            return jax.lax.stop_gradient(jnp.sign(w) * scale - w) + w

        def bitlinear(x, w):
            return x @ weight_quant(w).T
        B, S, _ = x.shape
        G = NHEAD // N_KV
        q = bitlinear(x, wq).reshape(B, S, N_KV, G, HEAD_DIM)
        k = bitlinear(x, wk).reshape(B, S, N_KV, HEAD_DIM)
        v = bitlinear(x, wv).reshape(B, S, N_KV, HEAD_DIM)
        sm_scale = 1.0 / jnp.sqrt(jnp.asarray(HEAD_DIM, dtype=x.dtype))
        scores = jnp.einsum('bskgd,btkd->bkgst', q, k) * sm_scale
        causal = jnp.tril(jnp.ones((S, S), dtype=bool))
        scores = jnp.where(causal, scores, jnp.asarray(-jnp.inf, dtype=scores.dtype))
        probs = jax.nn.softmax(scores, axis=-1)
        out = jnp.einsum('bkgst,btkd->bskgd', probs, v)
        out = out.reshape(B, S, D_MODEL)
        return bitlinear(out, wo)

    def _L0_ffn_ref(x, ln_gamma, ln_beta, spline_bases, spline_slopes, output_scale):
        import jax, jax.numpy as jnp
        import numpy as np
        D_MODEL = 512
        NUM_TILES = 64
        D_SLICE = D_MODEL // NUM_TILES
        TILES_PER_CLUSTER = 8
        NUM_CLUSTERS = NUM_TILES // TILES_PER_CLUSTER
        GRID = 16
        LN_EPS = 1e-05
        DIMS = (np.arange(NUM_TILES)[:, None] * D_SLICE + np.arange(D_SLICE)[None, :]) % D_MODEL
        DIMS = jnp.asarray(DIMS, dtype=jnp.int32)

        def _forward(x, ln_gamma, ln_beta, spline_bases, spline_slopes, output_scale):
            B, S, D = x.shape
            N = B * S
            mu = jnp.mean(x, axis=-1, keepdims=True)
            var = jnp.mean(jnp.square(x - mu), axis=-1, keepdims=True)
            xn = (x - mu) * jax.lax.rsqrt(var + LN_EPS) * ln_gamma + ln_beta
            xf = xn.reshape(N, D)
            slope_sign = jnp.sign(jnp.mean(spline_slopes, axis=-1))
            tile_sigs = jnp.zeros((NUM_TILES, D), dtype=x.dtype)
            tile_sigs = tile_sigs.at[jnp.arange(NUM_TILES)[:, None], DIMS].set(slope_sign)
            cluster_sigs = jnp.sign(tile_sigs.reshape(NUM_CLUSTERS, TILES_PER_CLUSTER, D).mean(axis=1))
            cluster_assign = jnp.arange(NUM_TILES, dtype=jnp.int32) // TILES_PER_CLUSTER
            input_sigs = jnp.sign(xf)
            cluster_scores = input_sigs @ cluster_sigs.T
            best_cluster = jnp.argmax(cluster_scores, axis=-1)
            tile_scores = input_sigs @ tile_sigs.T
            in_cluster = cluster_assign[None, :] == best_cluster[:, None]
            tile_idx = jnp.argmax(jnp.where(in_cluster, tile_scores, -jnp.inf), axis=-1)
            tok_dims = DIMS[tile_idx]
            x_slice = jnp.take_along_axis(xf, tok_dims, axis=1)
            tok_min = x_slice.min(axis=1)
            tok_max = x_slice.max(axis=1)
            onehot = tile_idx[None, :] == jnp.arange(NUM_TILES)[:, None]
            tile_min = jnp.where(onehot, tok_min[None, :], jnp.inf).min(axis=1)
            tile_max = jnp.where(onehot, tok_max[None, :], -jnp.inf).max(axis=1)
            mn = tile_min[tile_idx][:, None]
            mx = tile_max[tile_idx][:, None]
            u = jnp.clip((x_slice - mn) / (mx - mn + 1e-08), 0.0, 1.0 - 1e-06)
            gi = jnp.clip((u * GRID).astype(jnp.int32), 0, GRID - 1)
            j = jnp.arange(D_SLICE)[None, :]
            b = spline_bases[tile_idx[:, None], j, gi]
            s = spline_slopes[tile_idx[:, None], j, gi]
            x_local = (u - gi.astype(u.dtype) / GRID) * GRID
            delta = (b + s * x_local) * output_scale[tile_idx][:, None]
            out = jnp.zeros_like(xf).at[jnp.arange(N)[:, None], tok_dims].set(delta)
            return x + out.reshape(B, S, D)
        return _forward(x, ln_gamma, ln_beta, spline_bases, spline_slopes, output_scale)

    def _L1_attn_ref(x, W_qkv, b_qkv, W_out, b_out):
        import jax, jax.numpy as jnp
        import numpy as np
        N_HEADS = 16
        D_ROPE = 32
        ROPE_BASE = 10000.0
        MASK_FILL = -10000.0

        def _rope(x):
            S = x.shape[1]
            theta = 1.0 / ROPE_BASE ** (jnp.arange(0, D_ROPE, 2, dtype=jnp.float32) / D_ROPE)
            idx_theta = jnp.arange(S, dtype=jnp.float32)[:, None] * theta[None, :]
            idx_theta2 = jnp.concatenate([idx_theta, idx_theta], axis=-1)
            cos = jnp.cos(idx_theta2)[:, None, :].astype(x.dtype)
            sin = jnp.sin(idx_theta2)[:, None, :].astype(x.dtype)
            x_rope, x_pass = (x[..., :D_ROPE], x[..., D_ROPE:])
            half = D_ROPE // 2
            rot = jnp.concatenate([-x_rope[..., half:], x_rope[..., :half]], axis=-1)
            x_rope = x_rope * cos + rot * sin
            return jnp.concatenate([x_rope, x_pass], axis=-1)
        B, S, D = x.shape
        d_k = D // N_HEADS
        scale = 1.0 / jnp.sqrt(jnp.asarray(d_k, x.dtype))
        qkv = x @ W_qkv.T + b_qkv
        qkv = qkv.reshape(B, S, N_HEADS, 3 * d_k)
        q, k, v = jnp.split(qkv, 3, axis=-1)
        q = _rope(q)
        k = _rope(k)
        attn = jnp.einsum('bihk,bjhk->bijh', q, k) * scale
        causal = jnp.triu(jnp.ones((S, S), dtype=bool), 1)
        attn = jnp.where(causal[None, :, :, None], MASK_FILL, attn)
        attn = jax.nn.softmax(attn, axis=2)
        out = jnp.einsum('bijh,bjhk->bihk', attn, v)
        out = out.reshape(B, S, D)
        return out @ W_out.T + b_out

    def _L1_ffn_ref(x, gate_w, w1, b1, w2, b2, shared_w1, shared_b1, shared_w2, shared_b2):
        import jax, jax.numpy as jnp
        import numpy as np
        K = 2

        def gelu(v):
            return jax.nn.gelu(v, approximate=False)
        B, S, D = x.shape
        E = gate_w.shape[1]
        xf = x.reshape(-1, D)
        logits = xf @ gate_w
        top_logits, top_idx = jax.lax.top_k(logits, K)
        top_gates = jax.nn.softmax(top_logits, axis=-1)
        gates = jnp.sum(jax.nn.one_hot(top_idx, E, dtype=xf.dtype) * top_gates[..., None], axis=1)
        h = gelu(jnp.einsum('nd,edh->neh', xf, w1) + b1)
        out_e = jnp.einsum('neh,ehd->ned', h, w2) + b2
        routed = jnp.einsum('ne,ned->nd', gates, out_e)
        shared = gelu(xf @ shared_w1 + shared_b1) @ shared_w2 + shared_b2
        return (routed + shared).reshape(B, S, D)
    h = _L0_tok_ref(x, L0_tok_emb_table, L0_tok_conv_w, L0_tok_conv_b, L0_tok_spos0, L0_tok_spos1)
    h = h + _L0_attn_ref(_layernorm(h, axis=-1), L0_attn_wq, L0_attn_wk, L0_attn_wv, L0_attn_wo)
    h = h + _L0_ffn_ref(_layernorm(h, axis=-1), L0_ffn_ln_gamma, L0_ffn_ln_beta, L0_ffn_spline_bases, L0_ffn_spline_slopes, L0_ffn_output_scale)
    h = h + _L1_attn_ref(_layernorm(h, axis=-1), L1_attn_W_qkv, L1_attn_b_qkv, L1_attn_W_out, L1_attn_b_out)
    h = h + _L1_ffn_ref(_layernorm(h, axis=-1), L1_ffn_gate_w, L1_ffn_w1, L1_ffn_b1, L1_ffn_w2, L1_ffn_b2, L1_ffn_shared_w1, L1_ffn_shared_b1, L1_ffn_shared_w2, L1_ffn_shared_b2)
    return h

_drawn_inputs = setup_inputs


def setup_inputs(seed=0):
    import zlib

    import numpy as np

    out = dict(_drawn_inputs(seed))
    spreads = {}
    factors = {'L0_tok_conv_b': 8.0,
     'L0_attn_wq': 8.0,
     'L0_attn_wk': 8.0,
     'L0_attn_wv': 3.52,
     'L0_attn_wo': 3.628,
     'L0_ffn_ln_gamma': 8.0,
     'L0_ffn_ln_beta': 8.0,
     'L0_ffn_spline_bases': 8.0,
     'L0_ffn_spline_slopes': 8.0,
     'L0_ffn_output_scale': 8.0,
     'L1_attn_W_qkv': 8.0,
     'L1_attn_b_qkv': 8.0,
     'L1_attn_W_out': 8.0,
     'L1_attn_b_out': 42.185,
     'L1_ffn_gate_w': 37.51,
     'L1_ffn_w1': 64.0,
     'L1_ffn_b1': 64.0,
     'L1_ffn_w2': 64.0,
     'L1_ffn_b2': 31.508,
     'L1_ffn_shared_w1': 64.0,
     'L1_ffn_shared_b1': 64.0,
     'L1_ffn_shared_w2': 64.0,
     'L1_ffn_shared_b2': 32.829}
    for name, (base, spread) in spreads.items():
        noise = np.random.default_rng([zlib.crc32(name.encode()), seed]).standard_normal(out[name].shape)
        drawn = base * np.exp(spread * noise) if base else spread * noise
        out[name] = jnp.asarray(drawn.astype(out[name].dtype))
    for name, factor in factors.items():
        out[name] = (out[name] * factor).astype(out[name].dtype)
    return out
```

```python
from contextlib import ExitStack

import numpy as np

import concourse.bass as bass
from concourse import mybir

F32 = mybir.dt.float32
F32R = mybir.dt.float32r
BF16 = mybir.dt.bfloat16
U32 = mybir.dt.uint32
ALU = mybir.AluOpType
ACT = mybir.ActivationFunctionType
AX = mybir.AxisListType
ds = bass.ds

P = 128
B = 8
T = 512
D = T
NT = T // P
E_CH = 128
TAPS = 3
EPS = 1e-5
NTILE, SLICE, GRID = 64, 8, 16
NCLUSTER = 8
BIG = 1e30
H0, G0, DH0 = 32, 4, 16
H1, DH1 = 16, 32
E, HID = 8, 256
LOOKUP = 2 * SLICE * GRID + 3


def host_constants():
    f = np.float32
    ident = np.eye(P, dtype=f)
    causal = np.where(np.arange(P)[None, :] > np.arange(P)[:, None], f(-BIG), f(0)).astype(f)
    depth = E_CH // 2
    angle = np.arange(T, dtype=f)[:, None] * (f(1) / f(10000.0) ** (np.arange(depth, dtype=f)[None] / f(depth)))
    pe = np.concatenate([np.sin(angle), np.cos(angle)], -1).astype(f)
    pe = pe.reshape(NT, P, E_CH).transpose(1, 0, 2)
    n = np.arange(NTILE)
    order = ((7 - n // NCLUSTER) * 256 + (7 - n % NCLUSTER)).astype(f)
    small = np.concatenate([order, np.arange(GRID, dtype=f), np.arange(1, GRID + 1, dtype=f)])
    theta = f(1) / f(10000.0) ** (np.arange(0, DH1, 2, dtype=f) / f(DH1))
    it = np.arange(T, dtype=f)[:, None] * theta[None]
    cos = np.concatenate([np.cos(it), np.cos(it)], -1)
    sin = np.concatenate([-np.sin(it), np.sin(it)], -1)
    rope = np.stack([cos, sin]).astype(f).reshape(2, NT, P, DH1).transpose(2, 0, 1, 3)
    pick = np.zeros((E, E, P), f)
    for e in range(E):
        pick[e, e] = 1
    earlier = (np.arange(E)[None, :] < np.arange(E)[:, None]).astype(f)
    return {
        "c_square": np.stack([ident, causal, np.ones((P, P), f)], 1),
        "c_pe": pe,
        "c_small": small,
        "c_rope": rope,
        "c_pick": pick.reshape(E, E * P),
        "c_earlier": earlier.reshape(-1),
    }


def flat(ap):
    return ap.rearrange("p a n -> p (a n)")


class Attention:

    def __init__(self, nc, ctx, name, heads, dh, shared_keys, q_planes, k_planes):
        self.dh, self.shared = dh, shared_keys
        self.rows = 3 * dh
        self.pairs = heads // 8
        self.q_planes, self.k_planes = q_planes, k_planes
        self.nk = 1 if shared_keys else 4

        def sem(n):
            return ctx.enter_context(nc.semaphore(f"{name}_{n}"))

        self.stored = sem("qk_stored")
        self.loaded = [sem("qk_loaded0"), sem("qk_loaded1")]
        self.qk_free = sem("qk_free")
        self.scores = sem("scores")
        self.max = sem("row_max")
        self.probs = sem("probs")
        self.probs_t = sem("probs_t")
        self.copied_v = sem("probs_t_copied_v")
        self.copied_a = sem("probs_t_copied_a")
        self.pv = sem("pv")
        self.rsums_ready = sem("rsums_ready")
        self.normed = sem("normed")

    def buffers(self, sb, name):
        self.q = [sb(f"{name}_q{i}", [self.rows, 4, T], F32R) for i in range(2)]
        self.k = [sb(f"{name}_k{i}", [self.rows, self.nk, T], F32R) for i in range(2)]
        self.p = [sb(f"{name}_p{i}", [P, T]) for i in range(4)]
        self.pt = [sb(f"{name}_pt{i}", [P, T]) for i in range(4)]
        self.mx = sb(f"{name}_mx", [P, 8])
        self.sums = sb(f"{name}_sums", [P, 2, NT, 4])
        self.rsums = sb(f"{name}_rsums", [P, 2, NT, 4])

    def units(self, b, gp, x):
        return (b * self.pairs + gp) * 32 + x + 1

    def copies(self, b, gp, x):
        return (b * self.pairs + gp) * 16 + x // 4 * 2 + x % 2 + 1

    def groups(self, b, gp, x):
        return (b * self.pairs + gp) * 2 + x // 16 + 1

    def copied(self, x):
        return self.copied_v if x % 4 >= 2 else self.copied_a


def load_heads(sp, at, b, gp):
    for g2 in range(2):
        it = b * at.pairs + gp
        sp.wait_ge(at.qk_free, it * 2 + g2 + 1)
        for n, (qp, kp) in enumerate(((0, 0), (0, 1), (1, 0))):
            rows = slice(n * at.dh, (n + 1) * at.dh)
            heads = (gp * 2 + g2) * 4
            sp.dma_start(at.q[g2][rows].bitcast(F32), at.q_planes[ds(b * 2 + qp, 1), ds(heads, 4)]
                         .rearrange("a h d s -> d (a h) s")).then_inc(at.loaded[g2], 16)
            keys = gp * 2 + g2 if at.shared else heads
            sp.dma_start(at.k[g2][rows].bitcast(F32), at.k_planes[ds(b * 2 + kp, 1), ds(keys, at.nk)]
                         .rearrange("a h d s -> d (a h) s")).then_inc(at.loaded[g2], 16)


def attend_pe(pe, at, ps, v, ident, ident_b, mask_b, b, gp, first, steps):
    dh = at.dh
    for s in steps:
        x = s
        if x < 32:
            g2, j, i = x // 16, x % 16 // 4, x % 4
            if x % 16 == 0:
                pe.wait_ge(at.loaded[g2], (b * at.pairs + gp + 1) * 96)
            if not first or x >= 4:
                pe.wait_ge(at.probs, at.units(b, gp, x - 4))
            keys = (i + 1) * P
            scores = pe.matmul(ps[i][:, 0:keys], at.q[g2][:, j, i * P:(i + 1) * P],
                               at.k[g2][:, 0 if at.shared else j, 0:keys], start=True, stop=False)
            if x % 16 == 15:
                scores.then_inc(at.qk_free, 1)
            pe.matmul(ps[i][:, i * P:keys], ident_b, mask_b, start=False, stop=True).then_inc(at.scores, 1)
        x = s - 3
        if x < 32 and (not first or x >= 0):
            i = x % 4
            pe.wait_ge(at.probs, at.units(b, gp, x))
            if not first or x >= 2:
                pe.wait_ge(at.copied(x - 2), at.copies(b, gp, x - 2))
            for kt in range(i + 1):
                turned = pe.transpose(ps[4 + x % 2][:, kt * P:(kt + 1) * P], at.p[i][:, kt * P:(kt + 1) * P], ident)
            turned.then_inc(at.probs_t, 1)
        x = s - 5
        if x < 32 and (not first or x >= 0):
            g2, j, i = x % 32 // 16, x % 16 // 4, x % 4
            pe.wait_ge(at.copied(x), at.copies(b, gp, x))
            if x % 16 == 0 and not first:
                pe.wait_ge(at.normed, at.groups(b, gp, x - 32))
            group = gp * 2 + (g2 if x >= 0 else g2 - 2)
            head = group if at.shared else group * 4 + j
            col = (i * 4 + j) * dh
            for kt in range(i + 1):
                product = pe.matmul(ps[6 + g2][:, col:col + dh], at.pt[i][:, kt * P:(kt + 1) * P],
                                    v[:, kt, ds(head * dh, dh)], start=(kt == 0), stop=(kt == i))
            product.then_inc(at.pv, 1)


def attend_dve(dve, at, ps, out, b, gp, first, steps):
    dh = at.dh
    for s in steps:
        x = s
        if x < 32:
            dve.wait_ge(at.scores, at.units(b, gp, x))
            dve.tensor_reduce(at.mx[:, x % 8:x % 8 + 1], ps[x % 4][:, 0:(x % 4 + 1) * P], AX.X, ALU.max,
                              negate=True).then_inc(at.max, 1)
        x = s - 4
        if x < 32 and x % 4 >= 2 and (not first or x >= 0):
            dve.wait_ge(at.probs_t, at.units(b, gp, x))
            if not first or x >= 4:
                dve.wait_ge(at.pv, at.units(b, gp, x - 4))
            dve.tensor_copy(at.pt[x % 4][:, 0:(x % 4 + 1) * P],
                            ps[4 + x % 2][:, 0:(x % 4 + 1) * P]).then_inc(at.copied_v, 1)
        x = s - 8
        if x % 16 == 15 and (not first or x >= 0):
            g2 = x % 32 // 16
            dve.wait_ge(at.pv, at.units(b, gp, x))
            dve.reciprocal(at.rsums[:, g2], at.sums[:, g2]).then_inc(at.rsums_ready, 1)
            dve.wait_ge(at.rsums_ready, at.groups(b, gp, x))
            group = gp * 2 + (g2 if x >= 0 else g2 - 2)
            dve.tensor_tensor(
                out[:, :, ds(group * 4 * dh, 4 * dh)].rearrange("p i (j d) -> p i j d", d=dh),
                ps[6 + g2][:, 0:16 * dh].rearrange("p (i j d) -> p i j d", i=NT, j=4),
                at.rsums[:, g2].unsqueeze(3).to_broadcast([P, NT, 4, dh]), ALU.mult).then_inc(at.normed, 1)


def attend_act(act, at, ps, b, gp, first, steps):
    for s in steps:
        x = s
        if x < 32:
            g2, j, i = x // 16, x % 16 // 4, x % 4
            act.wait_ge(at.max, at.units(b, gp, x))
            if not first or x >= 4:
                act.wait_ge(at.probs_t, at.units(b, gp, x - 4))
            act.activation(at.p[i][:, 0:(i + 1) * P], ps[i][:, 0:(i + 1) * P], ACT.Exp,
                           bias=at.mx[:, x % 8:x % 8 + 1], scale=1.0,
                           accum_out=at.sums[:, g2, i, j:j + 1]).then_inc(at.probs, 1)
        x = s - 4
        if x < 32 and x % 4 < 2 and (not first or x >= 0):
            act.wait_ge(at.probs_t, at.units(b, gp, x))
            if not first or x >= 4:
                act.wait_ge(at.pv, at.units(b, gp, x - 4))
            act.copy(at.pt[x % 4][:, 0:(x % 4 + 1) * P],
                     ps[4 + x % 2][:, 0:(x % 4 + 1) * P]).then_inc(at.copied_a, 1)


def over_pairs(eng, at, steps):
    steps(0, True, range(32))
    if at.pairs > 2:
        with eng.Fori(1, at.pairs) as gp:
            steps(gp, False, range(32))
    else:
        steps(1, False, range(32))
    steps(at.pairs - 1, False, range(32, 40))


def carry_wait(eng, carried):
    eng.sem_inc(carried, 1)


class Norm:

    def __init__(self, ctx, nc, name, per):
        self.per = per
        self.carried = ctx.enter_context(nc.semaphore(f"{name}_carried"))
        self.var = ctx.enter_context(nc.semaphore(f"{name}_var"))
        self.rstd = ctx.enter_context(nc.semaphore(f"{name}_rstd"))

    def buffers(self, sb, name):
        self.stats = sb(f"{name}_stats", [P, NT, 6])
        self.mv = sb(f"{name}_mv", [P, NT, 2])
        self.ve = sb(f"{name}_ve", [P, NT])
        self.r = sb(f"{name}_r", [P, NT])


def norm_dve(dve, link, nm, x, out, b, k):
    for t in range(NT):
        last = dve.bn_stats(nm.stats[:, t], x[:, t])
    link(last)
    carry_wait(dve, nm.carried)
    for t in range(NT):
        last = dve.bn_aggr(nm.mv[:, t], nm.stats[:, t])
    link(last)
    dve.tensor_scalar(nm.ve[:], nm.mv[:, :, 1], EPS, None, ALU.add).then_inc(nm.var, 1)
    dve.wait_ge(nm.rstd, b * nm.per + k + 1)
    for t in range(NT):
        last = dve.tensor_scalar(out[:, t], x[:, t], nm.mv[:, t, 0:1], nm.r[:, t:t + 1], ALU.subtract, ALU.mult)
    return last


def norm_pool(pool, nm, power, b, k):
    pool.wait_ge(nm.var, b * nm.per + k + 1)
    pool.tensor_tensor(nm.r[:], nm.ve[:], power[:, 0:NT], ALU.pow).then_inc(nm.rstd, 1)


def chain(eng, sem, base, done):
    def link(ins):
        done[0] += 1
        ins.then_inc(sem, 1)
        eng.wait_ge(sem, base + done[0])
    return link


def phase_one(nc, keep, a, scratch):
    with ExitStack() as ctx:
        def sb(name, shape, dt=F32):
            return ctx.enter_context(nc.sbuf_tensor("a_" + name, shape, dt))

        def sem(name):
            return ctx.enter_context(nc.semaphore("a_" + name))

        ps = [ctx.enter_context(nc.psum_tensor(f"a_ps{i}", [P, T], F32)) for i in range(8)]
        at = Attention(nc, ctx, "a_at", H0, DH0, True, scratch["q0"], scratch["k0"])
        at.buffers(sb, "at")
        nm = Norm(ctx, nc, "a_ln", 3)
        nm.buffers(sb, "ln")

        square = sb("square", [P, 3, P])
        ident, causal, ones = square[:, 0], square[:, 1], square[:, 2]
        ident_b = sb("ident_b", [P, P], BF16)
        mask_b = sb("mask_b", [P, P], BF16)
        pe_t = sb("pe", [P, NT, E_CH])
        small = sb("small", [P, NTILE + 2 * GRID])
        convw = sb("convw", [P, TAPS, P])
        convb = sb("convb", [P, P])
        spos = sb("spos", [P, 2, P])
        gamma = sb("gamma", [P, D])
        beta = sb("beta", [P, D])
        power = sb("power", [P, NT])
        ids = sb("ids", [P, B * NT], U32)
        ids_now = sb("ids_now", [P, NT], U32)
        raw = sb("raw", [P, NT, 2 * D + 2 * P])
        wq = sb("wq", [P, NT, D], F32R)
        wk = sb("wk", [P, NT, P], F32R)
        wv = sb("wv", [P, NT, P], F32R)
        wo = sb("wo", [P, NT, D], F32R)
        wparts = [(wq, 0, D), (wk, D, P), (wv, D + P, P), (wo, D + 2 * P, D)]
        asum = sb("asum", [P, 4])
        mean_abs = sb("mean_abs", [P, 4])
        wscale = sb("wscale", [P, 5])
        slopes = sb("slopes", [P, NT, GRID])
        ssum = sb("ssum", [P, NT])
        ssign = sb("ssign", [P, NT])
        sdiag = sb("sdiag", [P, NT, P])
        slope_sign = sb("slope_sign", [P, D])

        emb = sb("emb", [P, NT, E_CH])
        tok = [sb("tok0", [P, NT, E_CH]), sb("tok1", [P, NT, E_CH])]
        tmx = sb("tmx", [P, NT])
        texp = sb("texp", [P, NT, E_CH])
        tsum = sb("tsum", [P, NT])
        trs = sb("trs", [P, NT])
        sel = sb("sel", [P, NT, E_CH])
        sel_t = sb("sel_t", [P, T])
        xpad = sb("xpad", [P, T + TAPS - 1])
        h = sb("h", [P, NT, D])
        hn = sb("hn", [P, NT, D])
        x = sb("x", [P, NT, D])
        xh = sb("xh", [P, NT, T], F32R)
        xl = sb("xl", [P, NT, T], F32R)
        qh = sb("qh", [P, NT + 1, T], F32R)
        ql = sb("ql", [P, NT + 1, T], F32R)
        v = sb("v", [P, NT, P])
        sg = sb("sg", [P, NT, D])
        xf = sb("xf", [P, NT, D])
        ts = sb("ts", [P, NT, NTILE])
        cs = sb("cs", [P, NT * NCLUSTER])
        key = sb("key", [P, NT, NTILE])
        kmax = sb("kmax", [P, NT])
        oh = sb("oh", [P, NT, NTILE])
        pen = sb("pen", [P, NT, NTILE])
        xs = sb("xs", [P, NT, SLICE])
        ext = sb("ext", [P, 2, NT])
        cand = sb("cand", [P, 2, NT, NTILE])
        cmax = sb("cmax", [P, 2, NTILE])

        consts = sem("consts")
        raw_in = sem("raw_in")
        ids_in = sem("ids_in")
        bf_ready = sem("bf_ready")
        pool_set = sem("pool_set")
        asum_ready = sem("asum_ready")
        mean_psum = sem("mean_psum")
        w_ready = sem("w_ready")
        sdiag_ready = sem("sdiag_ready")
        sign_psum = sem("sign_psum")
        ssum_ready = sem("ssum_ready")
        ssign_ready = sem("ssign_ready")
        pool_carried = sem("pool_carried")
        ids_set = sem("ids_set")
        emb_in = sem("emb_in")
        tok_ready = sem("tok_ready")
        tmx_ready = sem("tmx_ready")
        texp_ready = sem("texp_ready")
        sel_ready = sem("sel_ready")
        tok_t = sem("tok_t")
        selt_psum = sem("selt_psum")
        selt_ready = sem("selt_ready")
        xpad_ready = sem("xpad_ready")
        ext_psum = sem("ext_psum")
        conv_psum = sem("conv_psum")
        h_built = sem("h_built")
        x_ready = sem("x_ready")
        xt_psum = sem("xt_psum")
        hi_ready = sem("hi_ready")
        lo_ready = sem("lo_ready")
        q_psum = sem("q_psum")
        qhi_ready = sem("qhi_ready")
        qlo_ready = sem("qlo_ready")
        v_psum = sem("v_psum")
        v_ready = sem("v_ready")
        o_psum = sem("o_psum")
        xn_ready = sem("xn_ready")
        hn_ready = sem("hn_ready")
        hn_out = sem("hn_out")
        xn2_ready = sem("xn2_ready")
        xf_ready = sem("xf_ready")
        sg_ready = sem("sg_ready")
        h_used = sem("h_used")
        dve_chain = sem("dve_chain")
        DVE_STEPS = 24

        with nc.Block() as block:
            @block.sync
            def _(sp):
                sp.sem_inc(at.stored, 1)
                sp.sem_inc(hn_out, 1)
                sp.dma_start(ids[:], a["ids"]).then_inc(ids_in, 16)
                for n, (_, c, w) in enumerate(wparts):
                    sp.dma_start(raw[:, :, c:c + w], a[("wq", "wk", "wv", "wo")[n]]).then_inc(raw_in, 16)
                loads = [(square, a["c_square"]), (pe_t, a["c_pe"]), (convw, a["convw"]), (spos, a["spos"]),
                         (slopes, a["slopes_rows"]),
                         (small, a["c_small"].partition_broadcast(P)), (convb, a["convb"].partition_broadcast(P)),
                         (gamma, a["gamma"].partition_broadcast(P)), (beta, a["beta"].partition_broadcast(P))]
                for to, of in loads:
                    sp.dma_start(to[:], of).then_inc(consts, 16)
                assert len(loads) == 9
                with sp.Fori(0, B) as b:
                    for m in range(NT + 1):
                        sp.wait_ge(qlo_ready, b * 5 + m + 1)
                        for plane, half in enumerate((qh, ql)):
                            to = (scratch["q0"][ds(b * 2 + plane, 1), m * 8:(m + 1) * 8] if m < NT
                                  else scratch["k0"][ds(b * 2 + plane, 1)])
                            sp.dma_start(to.rearrange("a h d s -> (a h d) s"), half[:, m].bitcast(F32)).then_inc(at.stored, 16)
                    sp.wait_ge(at.stored, b * 160 + 160 + 1)
                    load_heads(sp, at, b, 0)
                    with sp.Fori(1, at.pairs) as gp:
                        load_heads(sp, at, b, gp)
                    sp.wait_ge(hn_ready, b + 1)
                    sp.dma_start(scratch["h1"][ds(b, 1)].rearrange("a p n -> (a p) n"),
                                 hn[:].rearrange("p t n -> p (t n)")).then_inc(hn_out, 16)
                sp.wait_ge(hn_out, B * 16 + 1)

            @block.gpsimd
            def _(pool):
                pool.memset(power[:], -0.5).then_inc(pool_set, 1)
                pool.wait_ge(pool_set, 1)
                pool.wait_ge(ids_in, 16)
                pool.wait_ge(consts, 9 * 16)
                with pool.Fori(0, B) as b:
                    pool.wait_ge(tok_ready, b * 2 + 1)
                    pool.tensor_copy(ids_now[:], ids[:, ds(b * NT, NT)]).then_inc(ids_set, 1)
                    pool.wait_ge(ids_set, b + 1)
                    carry_wait(pool, pool_carried)
                    for t in range(NT):
                        pool.indirect_dma_start(
                            out=emb[:, t], out_offset=None, in_=a["table"],
                            in_offset=bass.IndirectOffsetOnAxis(ap=ids_now[:, t:t + 1], axis=0)).then_inc(emb_in, 16)
                    for k in range(2):
                        norm_pool(pool, nm, power, b, k)
                    pool.wait_ge(xn_ready, b + 1)
                    pool.wait_ge(hn_out, b * 16 + 1)
                    pool.tensor_tensor(hn[:], h[:], x[:], ALU.add).then_inc(hn_ready, 1)
                    norm_pool(pool, nm, power, b, 2)
                    pool.wait_ge(xn2_ready, b + 1)
                    pool.tensor_tensor(xf[:], xf[:], gamma[:].unsqueeze(1).to_broadcast([P, NT, D]), ALU.mult).then_inc(xf_ready, 1)
                    pool.wait_ge(xf_ready, b * 2 + 1)
                    pool.tensor_tensor(xf[:], xf[:], beta[:].unsqueeze(1).to_broadcast([P, NT, D]), ALU.add).then_inc(xf_ready, 1)

            @block.scalar
            def _(act):
                act.wait_ge(raw_in, 64)
                for w, c, n in wparts:
                    act.activation(w[:], raw[:, :, c:c + n], ACT.Sign).then_inc(w_ready, 1)
                act.wait_ge(ssum_ready, 1)
                act.activation(ssign[:], ssum[:], ACT.Sign).then_inc(ssign_ready, 1)
                act.wait_ge(bf_ready, 5)
                with act.Fori(0, B) as b:
                    for z in range(2):
                        act.wait_ge(tmx_ready, b * 2 + z + 1)
                        if z == 0:
                            act.wait_ge(h_used, b + 1)
                        for t in range(NT):
                            last = act.activation(texp[:, t], tok[z][:, t], ACT.Exp, bias=tmx[:, t:t + 1], scale=1.0,
                                                  accum_out=tsum[:, t:t + 1])
                        last.then_inc(texp_ready, 1)
                        act.wait_ge(tok_t, b * 2 + z + 1)
                        if z == 0:
                            act.copy(xpad[:, TAPS - 1:], ps[0][:]).then_inc(xpad_ready, 1)
                        act.copy(h[:, 2 * z], ps[0][:]).then_inc(h_built, 1)
                        act.wait_ge(ext_psum, b * 2 + z + 1)
                        act.copy(h[:, 2 * z + 1], ps[2][:]).then_inc(h_built, 1)

                    def upper(k):
                        for c in range(NT):
                            act.wait_ge(xt_psum, b * 8 + k * 4 + c + 1)
                            act.copy(xh[:, c], ps[c][:]).then_inc(hi_ready, 1)

                    upper(0)
                    act.wait_ge(at.stored, b * 160 + 1)
                    for m in range(NT + 1):
                        act.wait_ge(q_psum, b * 5 + m + 1)
                        act.activation(qh[:, m], ps[(4 + m) % 8][:], ACT.Copy,
                                       scale=wscale[:, 4:5] if m < NT else wscale[:, 1:2]).then_inc(qhi_ready, 1)
                    over_pairs(act, at, lambda gp, first, steps: attend_act(act, at, ps, b, gp, first, steps))
                    upper(1)
                    act.wait_ge(xf_ready, b * 2 + 2)
                    act.activation(sg[:], xf[:], ACT.Sign).then_inc(sg_ready, 1)

            @block.vector
            def _(dve):
                dve.sem_inc(tok_ready, 1)
                dve.sem_inc(h_used, 1)
                dve.memset(xpad[:, 0:TAPS - 1], 0.0).then_inc(bf_ready, 1)
                dve.memset(keep["best"][:], -BIG).then_inc(bf_ready, 1)
                dve.wait_ge(consts, 9 * 16)
                dve.tensor_copy(ident_b[:], ident).then_inc(bf_ready, 1)
                dve.tensor_copy(mask_b[:], causal).then_inc(bf_ready, 1)
                dve.wait_ge(raw_in, 64)
                for n, (_, c, w) in enumerate(wparts):
                    last = dve.tensor_reduce(asum[:, n:n + 1], raw[:, :, c:c + w], AX.XY, ALU.add, apply_absolute_value=True)
                last.then_inc(asum_ready, 1)
                dve.tensor_reduce(ssum[:], slopes[:], AX.X, ALU.add).then_inc(ssum_ready, 1)
                dve.wait_ge(mean_psum, 1)
                for n, (_, _, w) in enumerate(wparts):
                    last = dve.tensor_scalar(wscale[:, n:n + 1], ps[0][:, n:n + 1], 1.0 / (w * D), EPS, ALU.mult, ALU.max)
                last.then_inc(mean_psum, 1)
                dve.wait_ge(mean_psum, 2)
                dve.tensor_scalar(wscale[:, 4:5], wscale[:, 0:1], DH0 ** -0.5, None, ALU.mult).then_inc(bf_ready, 1)
                dve.wait_ge(bf_ready, 5)
                dve.wait_ge(ssign_ready, 1)
                for c in range(NT):
                    dve.tensor_scalar(sdiag[:, c], ident, ssign[:, c:c + 1], None, ALU.mult).then_inc(sdiag_ready, 1)
                dve.wait_ge(sign_psum, 1)
                dve.tensor_copy(slope_sign[:], ps[1][:]).then_inc(sign_psum, 1)
                dve.wait_ge(sign_psum, 2)
                with dve.Fori(0, B) as b:
                    steps = [0]
                    link = chain(dve, dve_chain, b * DVE_STEPS, steps)
                    for z in range(2):
                        if z == 0:
                            dve.wait_ge(emb_in, b * 64 + 64)
                            dve.scalar_tensor_tensor(tok[0][:], emb[:], float(np.sqrt(np.float32(E_CH))), pe_t[:],
                                                     ALU.mult, ALU.add).then_inc(tok_ready, 1)
                        else:
                            dve.wait_ge(conv_psum, b + 1)
                            dve.tensor_tensor(tok[1][:], ps[3][:].rearrange("p (t c) -> p t c", t=NT),
                                              convb[:].unsqueeze(1).to_broadcast([P, NT, P]), ALU.add).then_inc(tok_ready, 1)
                        dve.wait_ge(tok_ready, b * 2 + z + 1 + 1)
                        dve.tensor_reduce(tmx[:], tok[z][:], AX.X, ALU.max, negate=True).then_inc(tmx_ready, 1)
                        dve.wait_ge(texp_ready, b * 2 + z + 1)
                        link(dve.reciprocal(trs[:], tsum[:]))
                        dve.tensor_tensor(sel[:], texp[:], trs[:].unsqueeze(2).to_broadcast([P, NT, E_CH]),
                                          ALU.mult).then_inc(sel_ready, 1)
                        dve.wait_ge(selt_psum, b * 2 + z + 1)
                        dve.tensor_copy(sel_t[:], ps[1][:]).then_inc(selt_ready, 1)
                    dve.wait_ge(h_built, b * 4 + 4)
                    norm_dve(dve, link, nm, h, x, b, 0).then_inc(x_ready, 1)

                    def lower(k):
                        for c in range(NT):
                            dve.wait_ge(hi_ready, b * 8 + k * 4 + c + 1)
                            dve.tensor_tensor(xl[:, c], ps[c][:], xh[:, c].bitcast(F32), ALU.subtract).then_inc(lo_ready, 1)

                    lower(0)
                    for m in range(NT + 1):
                        dve.wait_ge(qhi_ready, b * 5 + m + 1)
                        dve.scalar_tensor_tensor(ql[:, m], ps[(4 + m) % 8][:], wscale[:, 4:5] if m < NT else wscale[:, 1:2],
                                                 qh[:, m].bitcast(F32), ALU.mult, ALU.subtract).then_inc(qlo_ready, 1)
                    dve.wait_ge(v_psum, b + 1)
                    dve.tensor_scalar(v[:], ps[1][:].rearrange("p (t n) -> p t n", t=NT), wscale[:, 2:3], None,
                                      ALU.mult).then_inc(v_ready, 1)
                    over_pairs(dve, at, lambda gp, first, steps: attend_dve(dve, at, ps, x, b, gp, first, steps))
                    lower(1)
                    for t in range(NT):
                        dve.wait_ge(o_psum, b * 4 + t + 1)
                        last = dve.scalar_tensor_tensor(h[:, t], ps[4 + t][:], wscale[:, 3:4], h[:, t], ALU.mult, ALU.add)
                    link(last)
                    norm_dve(dve, link, nm, h, x, b, 1).then_inc(xn_ready, 1)
                    dve.wait_ge(xn_ready, b + 1)
                    norm_dve(dve, link, nm, x, xf, b, 2).then_inc(xn2_ready, 1)
                    dve.wait_ge(sg_ready, b + 1)
                    link(dve.tensor_tensor(sg[:], sg[:], slope_sign[:].unsqueeze(1).to_broadcast([P, NT, D]), ALU.mult))
                    link(dve.tensor_reduce(ts[:], sg[:].rearrange("p t (n s) -> p (t n) s", s=SLICE), AX.X, ALU.add))
                    link(dve.tensor_reduce(cs[:], ts[:].rearrange("p t (c n) -> p (t c) n", c=NCLUSTER), AX.X, ALU.add))
                    link(dve.tensor_scalar(cs[:], cs[:], 2048.0, None, ALU.mult))
                    link(dve.scalar_tensor_tensor(key[:], ts[:], 8.0, small[:, 0:NTILE].unsqueeze(1).to_broadcast([P, NT, NTILE]),
                                                  ALU.mult, ALU.add))
                    keyc = key[:].rearrange("p t (c n) -> p (t c) n", c=NCLUSTER)
                    link(dve.tensor_tensor(keyc, keyc, cs[:].unsqueeze(2).to_broadcast([P, NT * NCLUSTER, 8]), ALU.add))
                    link(dve.tensor_reduce(kmax[:], key[:], AX.X, ALU.max))
                    link(dve.tensor_tensor(oh[:], key[:], kmax[:].unsqueeze(2).to_broadcast([P, NT, NTILE]), ALU.is_equal))
                    dve.tensor_copy(keep["onehot"][:, ds(b * NT, NT)], oh[:])
                    link(dve.tensor_scalar(pen[:], oh[:], 1.0, BIG, ALU.subtract, ALU.mult))
                    link(dve.tensor_tensor(sg[:].rearrange("p t (n s) -> p (t n) s", s=SLICE),
                                           xf[:].rearrange("p t (n s) -> p (t n) s", s=SLICE),
                                           oh[:].rearrange("p t n -> p (t n)").unsqueeze(2).to_broadcast([P, NT * NTILE, SLICE]),
                                           ALU.mult))
                    link(dve.tensor_reduce(xs[:], sg[:].rearrange("p t (n s) -> p t s n", s=SLICE), AX.X, ALU.add))
                    dve.tensor_copy(keep["slice"][:, ds(b * NT, NT)], xs[:])
                    dve.tensor_reduce(ext[:, 0], xs[:], AX.X, ALU.max)
                    link(dve.tensor_reduce(ext[:, 1], xs[:], AX.X, ALU.min, negate=True))
                    for k in range(2):
                        last = dve.tensor_tensor(cand[:, k], oh[:], ext[:, k].unsqueeze(2).to_broadcast([P, NT, NTILE]), ALU.mult)
                    link(last)
                    for k in range(2):
                        last = dve.tensor_tensor(cand[:, k], cand[:, k], pen[:], ALU.add)
                    link(last)
                    for k in range(2):
                        last = dve.tensor_reduce(cmax[:, k], cand[:, k].rearrange("p t n -> p n t"), AX.X, ALU.max)
                    link(last)
                    dve.tensor_tensor(keep["best"][:], keep["best"][:], cmax[:], ALU.max).then_inc(h_used, 1)
                    dve.wait_ge(h_used, b + 1 + 1)
                    assert steps[0] == DVE_STEPS

            @block.tensor
            def _(pe):
                pe.wait_ge(asum_ready, 1)
                pe.wait_ge(consts, 9 * 16)
                pe.matmul(ps[0][:, 0:4], ones, asum[:], start=True, stop=True).then_inc(mean_psum, 1)
                for c in range(NT):
                    pe.wait_ge(sdiag_ready, c + 1)
                    last = pe.matmul(ps[1][:, c * P:(c + 1) * P], ones, sdiag[:, c], start=True, stop=True)
                last.then_inc(sign_psum, 1)
                pe.wait_ge(sign_psum, 2)
                pe.wait_ge(bf_ready, 5)
                pe.wait_ge(w_ready, 4)
                pe.sem_inc(at.qk_free, 2)
                with pe.Fori(0, B) as b:
                    def turn(to, of, ready):
                        for t in range(NT):
                            last = pe.transpose(to[:, t * P:(t + 1) * P], of[:, t], ident)
                        last.then_inc(ready, 1)

                    pe.wait_ge(h_used, b + 1)
                    for z in range(2):
                        pe.wait_ge(tok_ready, b * 2 + z + 1 + 1)
                        if z == 1:
                            pe.wait_ge(h_built, b * 4 + 2)
                        turn(ps[0], tok[z], tok_t)
                        if z == 0:
                            pe.wait_ge(xpad_ready, b + 1)
                            for t in range(NT):
                                for k in range(TAPS):
                                    last = pe.matmul(ps[3][:, t * P:(t + 1) * P], xpad[:, t * P + k:t * P + k + P],
                                                     convw[:, k], start=(k == 0), stop=(k == TAPS - 1))
                            last.then_inc(conv_psum, 1)
                        pe.wait_ge(sel_ready, b * 2 + z + 1)
                        turn(ps[1], sel, selt_psum)
                        pe.wait_ge(selt_ready, b * 2 + z + 1)
                        pe.matmul(ps[2][:], spos[:, z], sel_t[:], start=True, stop=True).then_inc(ext_psum, 1)

                    def turn_rows():
                        for c in range(NT):
                            for t in range(NT):
                                last = pe.transpose(ps[c][:, t * P:(t + 1) * P], x[:, t, c * P:(c + 1) * P], ident)
                            last.then_inc(xt_psum, 1)

                    def product(out, left, right, k):
                        for c in range(NT):
                            pe.wait_ge(lo_ready, b * 8 + k * 4 + c + 1)
                            for half, hf in enumerate((xh, xl)):
                                last = pe.matmul(out, left(hf, c), right(hf, c), start=(c + half == 0), stop=(c == NT - 1 and half == 1))
                        return last

                    pe.wait_ge(x_ready, b + 1)
                    turn_rows()
                    for m in range(NT):
                        product(ps[4 + m][:], lambda hf, c: wq[:, c, m * P:(m + 1) * P],
                                lambda hf, c: hf[:, c], 0).then_inc(q_psum, 1)
                    product(ps[0][:], lambda hf, c: wk[:, c], lambda hf, c: hf[:, c], 0).then_inc(q_psum, 1)
                    for t in range(NT):
                        last = product(ps[1][:, t * P:(t + 1) * P], lambda hf, c: hf[:, c, t * P:(t + 1) * P],
                                       lambda hf, c: wv[:, c], 0)
                    last.then_inc(v_psum, 1)
                    pe.wait_ge(qlo_ready, b * 5 + 5)
                    pe.wait_ge(v_ready, b + 1)
                    over_pairs(pe, at, lambda gp, first, steps: attend_pe(pe, at, ps, v, ident, ident_b[:], mask_b[:], b, gp, first, steps))
                    pe.wait_ge(at.normed, b * at.pairs * 2 + at.pairs * 2)
                    turn_rows()
                    for t in range(NT):
                        product(ps[4 + t][:], lambda hf, c: hf[:, c, t * P:(t + 1) * P],
                                lambda hf, c: wo[:, c], 1).then_inc(o_psum, 1)


def phase_two(nc, keep, a, scratch):
    with ExitStack() as ctx:
        def sb(name, shape, dt=F32):
            return ctx.enter_context(nc.sbuf_tensor("b_" + name, shape, dt))

        def sem(name):
            return ctx.enter_context(nc.semaphore("b_" + name))

        ps = [ctx.enter_context(nc.psum_tensor(f"b_ps{i}", [P, T], F32)) for i in range(8)]
        at = Attention(nc, ctx, "b_at", H1, DH1, False, scratch["q1"], scratch["k1"])
        at.buffers(sb, "at")
        nm = Norm(ctx, nc, "b_ln", 1)
        nm.buffers(sb, "ln")
        NCELL = SLICE * GRID
        QK_SCALE = [float(DH1) ** -0.5, 1.0]

        square = sb("square", [P, 3, P])
        ident, causal = square[:, 0], square[:, 1]
        ident_b = sb("ident_b", [P, P], BF16)
        mask_b = sb("mask_b", [P, P], BF16)
        small = sb("small", [P, NTILE + 2 * GRID])
        rope = sb("rope", [P, 2, NT, DH1])
        power = sb("power", [P, NT])
        wqkv = sb("wqkv", [P, NT, 3 * D])
        wout = sb("wout", [P, NT, D])
        bqkv = sb("bqkv", [P, 3 * D])
        bout = sb("bout", [P, D])
        lookup = sb("lookup", [NTILE, LOOKUP])
        h = sb("h", [P, NT, D])
        h2 = sb("h2", [P, NT, D])
        x = sb("x", [P, NT, D])
        xt = sb("xt", [P, NT, T])
        oh = sb("oh", [P, NT, NTILE])
        oht = sb("oht", [NTILE, T])
        look = sb("look", [P, NT, LOOKUP])
        xs = sb("xs", [P, NT, SLICE])
        den = sb("den", [P, NT])
        rden = sb("rden", [P, NT])
        u = sb("u", [P, NT, SLICE])
        u16 = sb("u16", [P, NT * SLICE])
        cell = sb("cell", [P, NT * SLICE])
        cells = sb("cells", [P, NT * SLICE, GRID])
        picked = sb("picked", [P, NT * SLICE, GRID])
        picked2 = sb("picked2", [P, NT * SLICE, GRID])
        bs = sb("bs", [P, 2, NT * SLICE])
        delta = sb("delta", [P, NT, SLICE])
        v = sb("v", [P, NT, D])
        qk = sb("qk", [P, 2 * D])
        qk_cos = sb("qk_cos", [P, 2 * D])
        qk_sin = sb("qk_sin", [P, 2 * D])
        half_h = [sb(f"half_h{i}", [P, NT, P], F32R) for i in range(2)]
        half_l = [sb(f"half_l{i}", [P, NT, P], F32R) for i in range(2)]

        consts = sem("consts")
        pe_carried = sem("pe_carried")
        ready = sem("ready")
        pool_set = sem("pool_set")
        best_t = sem("best_t")
        lookup_ready = sem("lookup_ready")
        h_in = sem("h_in")
        oh_ready = sem("oh_ready")
        oht_psum = sem("oht_psum")
        oht_ready = sem("oht_ready")
        look_psum = sem("look_psum")
        look_ready = sem("look_ready")
        delta_ready = sem("delta_ready")
        spread = sem("spread")
        x_ready = sem("x_ready")
        xt_psum = sem("xt_psum")
        xt_even = sem("xt_even")
        xt_odd = sem("xt_odd")
        qkv_psum = sem("qkv_psum")
        qkv_taken = sem("qkv_taken")
        rot_ready = sem("rot_ready")
        rope_ready = sem("rope_ready")
        qkt_psum = sem("qkt_psum")
        qhi_ready = sem("qhi_ready")
        qlo_ready = sem("qlo_ready")
        o_psum = sem("o_psum")
        h2_ready = sem("h2_ready")
        h2_out = sem("h2_out")
        tile_stored = sem("tile_stored")
        dve_chain = sem("dve_chain")
        DVE_STEPS = 28

        with nc.Block() as block:
            @block.sync
            def _(sp):
                for credited in (at.stored, h2_out, tile_stored):
                    sp.sem_inc(credited, 1)
                loads = [(square[:], a["c_square"]), (rope[:], a["c_rope"]), (wqkv[:], a["wqkv"]), (wout[:], a["wout"]),
                         (lookup[:, 0:2 * NCELL], a["splines"]), (lookup[:, 2 * NCELL + 2:], a["output_scale"]),
                         (small[:], a["c_small"].partition_broadcast(P)), (bqkv[:], a["bqkv"].partition_broadcast(P)),
                         (bout[:], a["bout"].partition_broadcast(P))]
                for to, of in loads:
                    sp.dma_start(to, of).then_inc(consts, 16)
                assert len(loads) == 9
                with sp.Fori(0, B) as b:
                    sp.wait_ge(h2_ready, b * 4 + 1)
                    sp.dma_start(h[:].rearrange("p t n -> p (t n)"),
                                 scratch["h1"][ds(b, 1)].rearrange("a p n -> (a p) n")).then_inc(h_in, 16)
                    for t in range(NT):
                        for s in range(2):
                            sp.wait_ge(qlo_ready, b * 8 + t * 2 + s + 1)
                            for plane, half in enumerate((half_h, half_l)):
                                to = scratch["q1" if s == 0 else "k1"][ds(b * 2 + plane, 1)]
                                sp.dma_start(to.rearrange("a (c h) d s -> (h d) (a c) s", c=4)[:, :, t * P:(t + 1) * P],
                                             half[s][:].bitcast(F32)).then_inc(at.stored, 16)
                        sp.wait_ge(at.stored, b * 256 + (t + 1) * 64 + 1)
                        sp.sem_inc(tile_stored, 1)
                    with sp.Fori(0, at.pairs) as gp:
                        load_heads(sp, at, b, gp)
                    sp.wait_ge(h2_ready, b * 4 + 4 + 1)
                    sp.dma_start(scratch["h2"][ds(b, 1)].rearrange("a p n -> (a p) n"),
                                 h2[:].rearrange("p t n -> p (t n)")).then_inc(h2_out, 16)
                sp.wait_ge(h2_out, B * 16 + 1)

            @block.gpsimd
            def _(pool):
                pool.sem_inc(spread, 1)
                pool.memset(power[:], -0.5).then_inc(pool_set, 1)
                pool.wait_ge(pool_set, 1)
                pool.wait_ge(consts, 9 * 16)
                with pool.Fori(0, B) as b:
                    pool.wait_ge(delta_ready, b + 1)
                    pool.wait_ge(h2_out, b * 16 + 1)
                    for t in range(NT):
                        pool.tensor_tensor(h2[:, t].rearrange("p (n s) -> p n s", s=SLICE),
                                           oh[:, t].unsqueeze(2).to_broadcast([P, NTILE, SLICE]),
                                           delta[:, t].unsqueeze(1).to_broadcast([P, NTILE, SLICE]), ALU.mult).then_inc(spread, 1)
                    pool.wait_ge(h_in, b * 16 + 16)
                    pool.wait_ge(spread, b * 5 + 4 + 1)
                    pool.tensor_tensor(h2[:], h2[:], h[:], ALU.add).then_inc(spread, 1)
                    norm_pool(pool, nm, power, b, 0)
                    for t in range(NT):
                        pool.wait_ge(qkv_taken, b * 8 + t * 2 + 1)
                        src = qk[:].rearrange("p (n two d) -> p n two d", two=2, d=DH1 // 2)
                        dst = qk_sin[:].rearrange("p (n two d) -> p n two d", two=2, d=DH1 // 2)
                        for half in range(2):
                            pool.tensor_tensor(dst[:, :, half], src[:, :, 1 - half],
                                               rope[:, 1, t, half * 16:(half + 1) * 16].unsqueeze(1).to_broadcast([P, 2 * H1, 16]),
                                               ALU.mult).then_inc(rot_ready, 1)
                        pool.wait_ge(rope_ready, b * 4 + t + 1)

            @block.scalar
            def _(act):
                act.wait_ge(ready, 2)
                with act.Fori(0, B) as b:
                    act.wait_ge(oht_psum, b + 1)
                    act.copy(oht[:], ps[0][0:NTILE, :]).then_inc(oht_ready, 1)
                    for t in range(NT):
                        act.wait_ge(look_psum, b * 4 + t + 1)
                        act.copy(look[:, t], ps[1 + t][:, 0:LOOKUP]).then_inc(look_ready, 1)

                    def turned(k):
                        for c in (0, 2):
                            act.wait_ge(xt_psum, b * 8 + k * 4 + c + 1)
                            act.copy(xt[:, c], ps[c][:]).then_inc(xt_even, 1)

                    turned(0)
                    for t in range(NT):
                        for s in range(2):
                            act.wait_ge(qkt_psum, b * 8 + t * 2 + s + 1)
                            if s == 0:
                                act.wait_ge(tile_stored, b * 4 + t + 1)
                            act.activation(half_h[s][:], ps[4 + s][:].rearrange("p (c n) -> p c n", c=4), ACT.Copy,
                                           scale=QK_SCALE[s]).then_inc(qhi_ready, 1)
                    over_pairs(act, at, lambda gp, first, steps: attend_act(act, at, ps, b, gp, first, steps))
                    turned(1)

            @block.vector
            def _(dve):
                dve.sem_inc(h2_ready, 1)
                dve.wait_ge(consts, 9 * 16)
                dve.tensor_copy(ident_b[:], ident).then_inc(ready, 1)
                dve.tensor_copy(mask_b[:], causal).then_inc(ready, 1)
                dve.wait_ge(best_t, 2)
                dve.tensor_reduce(lookup[:, 2 * NCELL:2 * NCELL + 1], ps[1][0:NTILE, 0:P], AX.X, ALU.max,
                                  negate=True).then_inc(lookup_ready, 1)
                dve.tensor_reduce(lookup[:, 2 * NCELL + 1:2 * NCELL + 2], ps[0][0:NTILE, 0:P], AX.X, ALU.max).then_inc(lookup_ready, 1)
                with dve.Fori(0, B) as b:
                    steps = [0]
                    link = chain(dve, dve_chain, b * DVE_STEPS, steps)
                    dve.wait_ge(spread, b * 5 + 1)
                    dve.tensor_copy(xs[:], keep["slice"][:, ds(b * NT, NT)])
                    dve.tensor_copy(oh[:], keep["onehot"][:, ds(b * NT, NT)]).then_inc(oh_ready, 1)
                    dve.wait_ge(look_ready, b * 4 + 4)
                    least, most, scale = (look[:, :, 2 * NCELL + n] for n in range(3))
                    dve.wait_ge(oh_ready, b + 1)
                    dve.tensor_tensor(u[:], xs[:], least.unsqueeze(2).to_broadcast([P, NT, SLICE]), ALU.subtract)
                    link(dve.tensor_tensor(den[:], most, least, ALU.subtract))
                    link(dve.tensor_scalar(den[:], den[:], 1e-8, None, ALU.add))
                    link(dve.reciprocal(rden[:], den[:]))
                    link(dve.tensor_tensor(u[:], u[:], rden[:].unsqueeze(2).to_broadcast([P, NT, SLICE]), ALU.mult))
                    uf = u[:].rearrange("p t s -> p (t s)")
                    link(dve.tensor_scalar(uf, uf, 0.0, 1.0 - 1e-6, ALU.max, ALU.min))
                    link(dve.tensor_scalar(u16[:], uf, float(GRID), None, ALU.mult))
                    shape = [P, NT * SLICE, GRID]
                    link(dve.tensor_tensor(cells[:], u16[:].unsqueeze(2).to_broadcast(shape),
                                           small[:, NTILE + GRID:].unsqueeze(1).to_broadcast(shape), ALU.is_ge))
                    link(dve.tensor_reduce(cell[:], cells[:], AX.X, ALU.add))
                    link(dve.tensor_tensor(cells[:], cell[:].unsqueeze(2).to_broadcast(shape),
                                           small[:, NTILE:NTILE + GRID].unsqueeze(1).to_broadcast(shape), ALU.is_equal))
                    for n, pk in enumerate((picked, picked2)):
                        last = dve.tensor_tensor(pk[:].rearrange("p (t s) g -> p t (s g)", t=NT),
                                                 cells[:].rearrange("p (t s) g -> p t (s g)", t=NT),
                                                 look[:, :, n * NCELL:(n + 1) * NCELL], ALU.mult)
                    link(last)
                    for n, pk in enumerate((picked, picked2)):
                        last = dve.tensor_reduce(bs[:, n], pk[:], AX.X, ALU.add)
                    link(last)
                    link(dve.scalar_tensor_tensor(u16[:], cell[:], -1.0 / GRID, uf, ALU.mult, ALU.add))
                    link(dve.scalar_tensor_tensor(u16[:], u16[:], float(GRID), bs[:, 1], ALU.mult, ALU.mult))
                    link(dve.tensor_tensor(u16[:], u16[:], bs[:, 0], ALU.add))
                    dve.tensor_tensor(delta[:], u16[:].rearrange("p (t s) -> p t s", t=NT),
                                      scale.unsqueeze(2).to_broadcast([P, NT, SLICE]), ALU.mult).then_inc(delta_ready, 1)
                    dve.wait_ge(spread, b * 5 + 5 + 1)
                    norm_dve(dve, link, nm, h2, x, b, 0).then_inc(x_ready, 1)

                    def turned(k):
                        for c in (1, 3):
                            dve.wait_ge(xt_psum, b * 8 + k * 4 + c + 1)
                            dve.tensor_copy(xt[:, c], ps[c][:]).then_inc(xt_odd, 1)

                    turned(0)
                    for t in range(NT):
                        dve.wait_ge(qkv_psum, b * 4 + t + 1)
                        link(dve.tensor_tensor(qk[:, 0:D], ps[1][:], bqkv[:, 0:D], ALU.add))
                        dve.tensor_tensor(qk[:, D:], ps[2][:], bqkv[:, D:2 * D], ALU.add).then_inc(qkv_taken, 1)
                        dve.tensor_tensor(v[:, t], ps[3][:], bqkv[:, 2 * D:], ALU.add).then_inc(qkv_taken, 1)
                        dve.wait_ge(qkv_taken, b * 8 + t * 2 + 1)
                        link(dve.tensor_tensor(qk_cos[:].rearrange("p (n d) -> p n d", d=DH1),
                                               qk[:].rearrange("p (n d) -> p n d", d=DH1),
                                               rope[:, 0, t].unsqueeze(1).to_broadcast([P, 2 * H1, DH1]), ALU.mult))
                        dve.wait_ge(rot_ready, b * 8 + t * 2 + 2)
                        dve.tensor_tensor(qk_cos[:], qk_cos[:], qk_sin[:], ALU.add).then_inc(rope_ready, 1)
                        for s in range(2):
                            dve.wait_ge(qhi_ready, b * 8 + t * 2 + s + 1)
                            dve.scalar_tensor_tensor(half_l[s][:], ps[4 + s][:].rearrange("p (c n) -> p c n", c=4), QK_SCALE[s],
                                                     half_h[s][:].bitcast(F32), ALU.mult, ALU.subtract).then_inc(qlo_ready, 1)
                    over_pairs(dve, at, lambda gp, first, steps: attend_dve(dve, at, ps, x, b, gp, first, steps))
                    turned(1)
                    for t in range(NT):
                        dve.wait_ge(o_psum, b * 4 + t + 1)
                        link(dve.tensor_tensor(h2[:, t], ps[4 + t][:], h2[:, t], ALU.add))
                        dve.tensor_tensor(h2[:, t], h2[:, t], bout[:], ALU.add).then_inc(h2_ready, 1)
                    assert steps[0] == DVE_STEPS

            @block.tensor
            def _(pe):
                pe.wait_ge(consts, 9 * 16)
                for k in range(2):
                    pe.transpose(ps[k][0:NTILE, 0:P], keep["best"][:, k], ident).then_inc(best_t, 1)
                pe.wait_ge(lookup_ready, 2)
                pe.wait_ge(ready, 2)
                pe.sem_inc(at.qk_free, 2)
                with pe.Fori(0, B) as b:
                    pe.wait_ge(oh_ready, b + 1)
                    carry_wait(pe, pe_carried)
                    for t in range(NT):
                        last = pe.transpose(ps[0][0:NTILE, t * P:(t + 1) * P], oh[:, t], ident)
                    last.then_inc(oht_psum, 1)
                    pe.wait_ge(oht_ready, b + 1)
                    pe.wait_ge(h2_ready, b * 4 + 1)
                    for t in range(NT):
                        pe.matmul(ps[1 + t][:, 0:LOOKUP], oht[:, t * P:(t + 1) * P], lookup[:],
                                  start=True, stop=True).then_inc(look_psum, 1)

                    def turn_rows():
                        for c in range(NT):
                            for t in range(NT):
                                last = pe.transpose(ps[c][:, t * P:(t + 1) * P], x[:, t, c * P:(c + 1) * P], ident)
                            last.then_inc(xt_psum, 1)

                    def product(out, t, w):
                        for c in range(NT):
                            last = pe.matmul(out, xt[:, c, t * P:(t + 1) * P], w(c), start=(c == 0), stop=(c == NT - 1))
                        return last

                    pe.wait_ge(look_ready, b * 4 + 4)
                    pe.wait_ge(x_ready, b + 1)
                    turn_rows()
                    for t in range(NT):
                        if t == 0:
                            pe.wait_ge(xt_odd, b * 4 + 2)
                            pe.wait_ge(xt_even, b * 4 + 2)
                        else:
                            pe.wait_ge(qkv_taken, b * 8 + t * 2)
                        for s in range(3):
                            last = product(ps[1 + s][:], t, lambda c: wqkv[:, c, s * D:(s + 1) * D])
                        last.then_inc(qkv_psum, 1)
                        pe.wait_ge(rope_ready, b * 4 + t + 1)
                        for s in range(2):
                            if t > 0:
                                pe.wait_ge(qlo_ready, b * 8 + t * 2 + s - 1)
                            for c in range(NT):
                                last = pe.transpose(ps[4 + s][:, c * P:(c + 1) * P], qk_cos[:, s * D + c * P:s * D + (c + 1) * P], ident)
                            last.then_inc(qkt_psum, 1)
                    pe.wait_ge(qlo_ready, b * 8 + 8)
                    over_pairs(pe, at, lambda gp, first, steps: attend_pe(pe, at, ps, v, ident, ident_b[:], mask_b[:], b, gp, first, steps))
                    pe.wait_ge(at.normed, b * at.pairs * 2 + at.pairs * 2)
                    turn_rows()
                    pe.wait_ge(xt_odd, b * 4 + 4)
                    pe.wait_ge(xt_even, b * 4 + 4)
                    for t in range(NT):
                        product(ps[4 + t][:], t, lambda c: wout[:, c]).then_inc(o_psum, 1)


def phase_three(nc, a, scratch, out):
    with ExitStack() as ctx:
        def sb(name, shape, dt=F32):
            return ctx.enter_context(nc.sbuf_tensor("m_" + name, shape, dt))

        def sem(name):
            return ctx.enter_context(nc.semaphore("m_" + name))

        ps = [ctx.enter_context(nc.psum_tensor(f"m_ps{i}", [P, T], F32)) for i in range(8)]
        nm = Norm(ctx, nc, "m_ln", 1)
        nm.buffers(sb, "ln")
        ident = sb("ident", [P, 3, P])
        pick = sb("pick", [E, E * P])
        earlier = sb("earlier", [P, E, E])
        power = sb("power", [P, NT])
        euler = sb("euler", [P, NT, E])
        gate_w = sb("gate_w", [P, NT, E])
        w1 = sb("w1", [P, NT, E * HID])
        w2 = sb("w2", [P, 2 * E, D])
        s1 = sb("s1", [P, NT, D])
        s2 = sb("s2", [P, NT, D])
        b1 = sb("b1", [P, 2 * E + NT])
        b2 = sb("b2", [E + 1, D])
        h = [sb("h0", [P, NT, D]), sb("h1", [P, NT, D])]
        x = sb("x", [P, NT, D])
        y = sb("y", [P, NT, D])
        xt = sb("xt", [P, NT, T])
        logits = sb("logits", [P, NT, E])
        best = sb("best", [P, NT])
        above = sb("above", [P, NT * E, E])
        equal = sb("equal", [P, NT * E, E])
        rank = sb("rank", [P, NT * E])
        chosen = sb("chosen", [P, NT * E])
        shifted = sb("shifted", [P, NT, E])
        expo = sb("expo", [P, NT, E])
        total = sb("total", [P, NT])
        rtotal = sb("rtotal", [P, NT])
        gates = sb("gates", [P, NT, E])
        gates_t = sb("gates_t", [E + 1, T])
        act_out = [sb(f"act_out{i}", [P, T]) for i in range(3)]
        gated = [sb(f"gated{i}", [P, T]) for i in range(3)]

        consts = sem("consts")
        pool_set = sem("pool_set")
        pe_carried = sem("pe_carried")
        ones_set = sem("ones_set")
        h_in = sem("h_in")
        x_ready = sem("x_ready")
        xt_psum = sem("xt_psum")
        xt_even = sem("xt_even")
        xt_odd = sem("xt_odd")
        logit_psum = sem("logit_psum")
        shifted_ready = sem("shifted_ready")
        expo_ready = sem("expo_ready")
        gates_ready = sem("gates_ready")
        gates_psum = sem("gates_psum")
        gates_t_ready = sem("gates_t_ready")
        gate_psum = sem("gate_psum")
        hid_psum = sem("hid_psum")
        hid_ready = sem("hid_ready")
        gated_ready = sem("gated_ready")
        y_psum = sem("y_psum")
        hid_used = sem("hid_used")
        y_ready = sem("y_ready")
        y_out = sem("y_out")
        dve_chain = sem("dve_chain")
        DVE_STEPS = 12
        NH = 2 * E + NT
        NG = 2 * E

        with nc.Block() as block:
            @block.sync
            def _(sp):
                sp.sem_inc(y_out, 1)
                loads = [(ident[:], a["c_square"]), (pick[:], a["c_pick"]), (earlier[:].rearrange("p a b -> p (a b)"), a["c_earlier"].partition_broadcast(P)),
                         (gate_w[:], a["gate_w"]), (w1[:], a["w1"]), (w2[:], a["w2"]), (s1[:], a["s1"]), (s2[:], a["s2"]),
                         (b1[:], a["b1"]), (b2[0:E], a["b2"]), (b2[E:E + 1], a["sb2"])]
                for to, of in loads:
                    sp.dma_start(to, of).then_inc(consts, 16)
                assert len(loads) == 11
                with sp.Fori(0, B) as b:
                    sp.wait_ge(y_ready, b * 4 + 1)
                    sp.dma_start(h[0][:].rearrange("p t n -> p (t n)"),
                                 scratch["h2"][ds(b, 1)].rearrange("a p n -> (a p) n")).then_inc(h_in, 16)
                    sp.wait_ge(y_ready, b * 4 + 4 + 1)
                    sp.dma_start(out[ds(b, 1)].rearrange("a (t p) n -> p (a t) n", p=P), y[:]).then_inc(y_out, 16)
                sp.wait_ge(y_out, B * 16 + 1)

            @block.gpsimd
            def _(pool):
                pool.memset(power[:], -0.5).then_inc(pool_set, 1)
                pool.memset(euler[:], float(np.e)).then_inc(pool_set, 1)
                pool.wait_ge(pool_set, 2)
                with pool.Fori(0, B) as b:
                    norm_pool(pool, nm, power, b, 0)
                    pool.wait_ge(shifted_ready, b + 1)
                    pool.tensor_tensor(expo[:], euler[:], shifted[:], ALU.pow).then_inc(expo_ready, 1)

            @block.scalar
            def _(act):
                act.wait_ge(consts, 11 * 16)
                with act.Fori(0, B) as b:
                    for c in (0, 2):
                        act.wait_ge(xt_psum, b * 4 + c + 1)
                        act.copy(xt[:, c], ps[4 + c][:]).then_inc(xt_even, 1)
                    for n in range(NH):
                        act.wait_ge(hid_psum, b * NH + n + 1)
                        if n >= 3:
                            act.wait_ge(hid_used, b * NH + n - 2)
                        act.activation(act_out[n % 3][:], ps[4 + n % 2][:], ACT.Gelu, bias=b1[:, n:n + 1],
                                       scale=1.0).then_inc(hid_ready, 1)

            @block.vector
            def _(dve):
                dve.sem_inc(y_ready, 1)
                dve.memset(gates_t[:], 1.0).then_inc(ones_set, 1)
                dve.wait_ge(ones_set, 1)
                dve.wait_ge(consts, 11 * 16)
                with dve.Fori(0, B) as b:
                    steps = [0]
                    link = chain(dve, dve_chain, b * DVE_STEPS, steps)
                    dve.wait_ge(h_in, b * 16 + 16)
                    norm_dve(dve, link, nm, h[0], x, b, 0).then_inc(x_ready, 1)
                    for c in (1, 3):
                        dve.wait_ge(xt_psum, b * 4 + c + 1)
                        dve.tensor_copy(xt[:, c], ps[4 + c][:]).then_inc(xt_odd, 1)
                    dve.wait_ge(logit_psum, b + 1)
                    link(dve.tensor_copy(logits[:], ps[4][:, 0:NT * E].rearrange("p (t e) -> p t e", t=NT)))
                    link(dve.tensor_reduce(best[:], logits[:], AX.X, ALU.max))
                    dve.tensor_tensor(shifted[:], logits[:], best[:].unsqueeze(2).to_broadcast([P, NT, E]),
                                      ALU.subtract).then_inc(shifted_ready, 1)
                    mine = logits[:].unsqueeze(3).to_broadcast([P, NT, E, E])
                    theirs = logits[:].unsqueeze(2).to_broadcast([P, NT, E, E])
                    dve.tensor_tensor(above[:].rearrange("p (t e) f -> p t e f", t=NT), theirs, mine, ALU.is_gt)
                    link(dve.tensor_tensor(equal[:].rearrange("p (t e) f -> p t e f", t=NT), theirs, mine, ALU.is_equal))
                    link(dve.tensor_tensor(equal[:].rearrange("p (t e) f -> p t (e f)", t=NT),
                                           equal[:].rearrange("p (t e) f -> p t (e f)", t=NT),
                                           earlier[:].rearrange("p e f -> p (e f)").unsqueeze(1).to_broadcast([P, NT, E * E]), ALU.mult))
                    link(dve.tensor_tensor(above[:], above[:], equal[:], ALU.add))
                    link(dve.tensor_reduce(rank[:], above[:], AX.X, ALU.add))
                    link(dve.tensor_scalar(chosen[:], rank[:], 2.0, None, ALU.is_lt))
                    dve.wait_ge(expo_ready, b + 1)
                    link(dve.tensor_tensor(gates[:].rearrange("p t e -> p (t e)"), expo[:].rearrange("p t e -> p (t e)"), chosen[:], ALU.mult))
                    link(dve.tensor_reduce(total[:], gates[:], AX.X, ALU.add))
                    link(dve.reciprocal(rtotal[:], total[:]))
                    dve.tensor_tensor(gates[:], gates[:], rtotal[:].unsqueeze(2).to_broadcast([P, NT, E]), ALU.mult).then_inc(gates_ready, 1)
                    dve.wait_ge(gates_psum, b + 1)
                    dve.tensor_copy(gates_t[0:E, :], ps[5][0:E, :]).then_inc(gates_t_ready, 1)
                    for n in range(NG):
                        dve.wait_ge(gate_psum, b * E + n // 2 + 1)
                        dve.wait_ge(hid_ready, b * NH + n + 1)
                        if n >= 3:
                            dve.wait_ge(hid_used, b * NH + n - 2)
                        dve.tensor_tensor(gated[n % 3][:], ps[6 + n // 2 % 2][:], act_out[n % 3][:], ALU.mult).then_inc(gated_ready, 1)
                    dve.wait_ge(y_out, b * 16 + 1)
                    dve.wait_ge(y_psum, b + 1)
                    for t in range(NT):
                        dve.tensor_tensor(y[:, t], ps[t][:], h[0][:, t], ALU.add).then_inc(y_ready, 1)
                    assert steps[0] == DVE_STEPS

            @block.tensor
            def _(pe):
                pe.wait_ge(ones_set, 1)
                pe.wait_ge(consts, 11 * 16)
                with pe.Fori(0, B) as b:
                    pe.wait_ge(x_ready, b + 1)
                    for c in range(NT):
                        for t in range(NT):
                            last = pe.transpose(ps[4 + c][:, t * P:(t + 1) * P], x[:, t, c * P:(c + 1) * P], ident[:, 0])
                        last.then_inc(xt_psum, 1)
                    pe.wait_ge(xt_even, b * 2 + 2)
                    pe.wait_ge(xt_odd, b * 2 + 2)
                    for t in range(NT):
                        for c in range(NT):
                            last = pe.matmul(ps[4][:, t * E:(t + 1) * E], xt[:, c, t * P:(t + 1) * P], gate_w[:, c],
                                             start=(c == 0), stop=(c == NT - 1))
                    last.then_inc(logit_psum, 1)
                    pe.wait_ge(gates_ready, b + 1)
                    carry_wait(pe, pe_carried)
                    for t in range(NT):
                        last = pe.transpose(ps[5][0:E, t * P:(t + 1) * P], gates[:, t], ident[:, 0])
                    last.then_inc(gates_psum, 1)
                    pe.wait_ge(gates_t_ready, b + 1)
                    pe.wait_ge(y_ready, b * 4 + 1)

                    def hidden(n):
                        if n % 2 == 0 and n < NG:
                            if n >= 4:
                                pe.wait_ge(gated_ready, b * NG + n - 2)
                            pe.matmul(ps[6 + n // 2 % 2][:], pick[:, n // 2 * P:(n // 2 + 1) * P], gates_t[0:E, :],
                                      start=True, stop=True).then_inc(gate_psum, 1)
                        if n >= 2:
                            pe.wait_ge(hid_ready, b * NH + n - 1)
                        for c in range(NT):
                            w = w1[:, c, n * P:(n + 1) * P] if n < NG else s1[:, c, (n - NG) * P:(n - NG + 1) * P]
                            last = pe.matmul(ps[4 + n % 2][:], w, xt[:, c], start=(c == 0), stop=(c == NT - 1))
                        last.then_inc(hid_psum, 1)

                    def output(n):
                        if n < NG:
                            pe.wait_ge(gated_ready, b * NG + n + 1)
                        else:
                            pe.wait_ge(hid_ready, b * NH + n + 1)
                        for t in range(NT):
                            left = (gated if n < NG else act_out)[n % 3][:, t * P:(t + 1) * P]
                            right = w2[:, n] if n < NG else s2[:, n - NG]
                            last = pe.matmul(ps[t][:], left, right, start=False, stop=(n == NH - 1))
                        last.then_inc(hid_used, 1)
                        return last

                    for t in range(NT):
                        pe.matmul(ps[t][:], gates_t[:, t * P:(t + 1) * P], b2[:], start=True, stop=False)
                    hidden(0)
                    for n in range(1, NH):
                        hidden(n)
                        output(n - 1)
                    output(NH - 1)
                    pe.matmul(ps[7][:, 0:P], ident[:, 0], ident[:, 0], start=True, stop=True).then_inc(y_psum, 1)


def program(nc, a, out):
    def dram(name, shape):
        return nc.dram_tensor(name, shape, F32).ap()

    scratch = {
        "q0": dram("q0", (2 * B, H0, DH0, T)), "k0": dram("k0", (2 * B, H0 // G0, DH0, T)),
        "q1": dram("q1", (2 * B, H1, DH1, T)), "k1": dram("k1", (2 * B, H1, DH1, T)),
        "h1": dram("h1", (B, P, NT * D)), "h2": dram("h2", (B, P, NT * D)),
    }
    with ExitStack() as ctx:
        keep = {n: ctx.enter_context(nc.sbuf_tensor("keep_" + n, s, F32)) for n, s in (
            ("onehot", [P, B * NT, NTILE]),
            ("slice", [P, B * NT, SLICE]),
            ("best", [P, 2, NTILE]),
        )}
        phase_one(nc, keep, a, scratch)
        phase_two(nc, keep, a, scratch)
    phase_three(nc, a, scratch, out)


def layout(i):
    def rows(w):
        return w.reshape(-1, P, w.shape[-1]).transpose(1, 0, 2)

    n = np.arange(3 * D)
    s, head, d = n // D, n % D // DH1, n % DH1
    order = head * 3 * DH1 + s * DH1 + d
    return {
        "ids": i["x"].reshape(B * NT, P).T.astype(np.uint32),
        "table": i["L0_tok_emb_table"],
        "convw": i["L0_tok_conv_w"].transpose(1, 2, 0),
        "convb": i["L0_tok_conv_b"],
        "spos": np.stack([i["L0_tok_spos0"], i["L0_tok_spos1"]], 1),
        "wq": rows(i["L0_attn_wq"].T), "wk": rows(i["L0_attn_wk"].T),
        "wv": rows(i["L0_attn_wv"].T), "wo": rows(i["L0_attn_wo"].T),
        "gamma": i["L0_ffn_ln_gamma"], "beta": i["L0_ffn_ln_beta"],
        "slopes_rows": i["L0_ffn_spline_slopes"].reshape(NT, P, GRID).transpose(1, 0, 2),
        "splines": np.concatenate([i["L0_ffn_spline_bases"].reshape(NTILE, -1),
                                   i["L0_ffn_spline_slopes"].reshape(NTILE, -1)], 1),
        "output_scale": i["L0_ffn_output_scale"].reshape(NTILE, 1),
        "wqkv": rows(i["L1_attn_W_qkv"][order].T), "bqkv": i["L1_attn_b_qkv"][order],
        "wout": rows(i["L1_attn_W_out"].T), "bout": i["L1_attn_b_out"],
        "gate_w": rows(i["L1_ffn_gate_w"]),
        "w1": rows(i["L1_ffn_w1"].transpose(1, 0, 2).reshape(D, E * HID)),
        "w2": rows(i["L1_ffn_w2"].reshape(E * HID, D)),
        "s1": rows(i["L1_ffn_shared_w1"]), "s2": rows(i["L1_ffn_shared_w2"]),
        "b1": np.concatenate([i["L1_ffn_b1"].reshape(-1, P), i["L1_ffn_shared_b1"].reshape(-1, P)]).T,
        "b2": i["L1_ffn_b2"], "sb2": i["L1_ffn_shared_b2"].reshape(1, D),
    }


def kernel(**inputs):
    import concourse.bacc as bacc
    from concourse.bass_utils import run_bass_kernel_spmd

    given = {n: np.asarray(v) for n, v in inputs.items()}
    arrays = {f"in_{n}": np.ascontiguousarray(v) for n, v in {**layout(given), **host_constants()}.items()}
    nc = bacc.Bacc("TRN2", target_bir_lowering=False, num_devices=1)
    a = {n[3:]: nc.dram_tensor(n, v.shape, mybir.dt.from_np(v.dtype), kind="ExternalInput").ap() for n, v in arrays.items()}
    out = nc.dram_tensor("out", (B, D, T), F32, kind="ExternalOutput").ap()
    program(nc, a, out)
    return run_bass_kernel_spmd(nc, [arrays], core_ids=[0]).results[0]["out"]
```

```python
from contextlib import ExitStack

import numpy as np

import concourse.bass as bass
from concourse import mybir

F32 = mybir.dt.float32
F32R = mybir.dt.float32r
BF16 = mybir.dt.bfloat16
U32 = mybir.dt.uint32
ALU = mybir.AluOpType
ACT = mybir.ActivationFunctionType
AX = mybir.AxisListType
ds = bass.ds

P = 128
B = 8
T = 512
D = T
NT = T // P
E_CH = 128
TAPS = 3
EPS = 1e-5
NTILE, SLICE, GRID = 64, 8, 16
NCLUSTER = 8
BIG = 1e30
H0, G0, DH0 = 32, 4, 16
H1, DH1 = 16, 32
E, HID = 8, 256
LOOKUP = 2 * SLICE * GRID + 3


def host_constants():
    f = np.float32
    ident = np.eye(P, dtype=f)
    causal = np.where(np.arange(P)[None, :] > np.arange(P)[:, None], f(-BIG), f(0)).astype(f)
    depth = E_CH // 2
    angle = np.arange(T, dtype=f)[:, None] * (f(1) / f(10000.0) ** (np.arange(depth, dtype=f)[None] / f(depth)))
    pe = np.concatenate([np.sin(angle), np.cos(angle)], -1).astype(f)
    pe = pe.reshape(NT, P, E_CH).transpose(1, 0, 2)
    n = np.arange(NTILE)
    order = ((7 - n // NCLUSTER) * 256 + (7 - n % NCLUSTER)).astype(f)
    small = np.concatenate([order, np.arange(GRID, dtype=f), np.arange(1, GRID + 1, dtype=f)])
    theta = f(1) / f(10000.0) ** (np.arange(0, DH1, 2, dtype=f) / f(DH1))
    it = np.arange(T, dtype=f)[:, None] * theta[None]
    cos = np.concatenate([np.cos(it), np.cos(it)], -1)
    sin = np.concatenate([-np.sin(it), np.sin(it)], -1)
    rope = np.stack([cos, sin]).astype(f).reshape(2, NT, P, DH1).transpose(2, 0, 1, 3)
    pick = np.zeros((E, E, P), f)
    for e in range(E):
        pick[e, e] = 1
    earlier = (np.arange(E)[None, :] < np.arange(E)[:, None]).astype(f)
    return {
        "c_square": np.stack([ident, causal, np.ones((P, P), f)], 1),
        "c_pe": pe,
        "c_small": small,
        "c_rope": rope,
        "c_pick": pick.reshape(E, E * P),
        "c_earlier": earlier.reshape(-1),
    }


def flat(ap):
    return ap.rearrange("p a n -> p (a n)")


class Attention:

    def __init__(self, nc, ctx, name, heads, dh, shared_keys, q_planes, k_planes):
        self.dh, self.shared = dh, shared_keys
        self.rows = 3 * dh
        self.top = -(-self.rows // 32) * 32
        self.all = self.top + 3
        self.heads, self.groups, self.units = heads, heads // 4, heads * 4
        self.q_planes, self.k_planes = q_planes, k_planes
        self.nk = 1 if shared_keys else 4

        def sem(n):
            return ctx.enter_context(nc.semaphore(f"{name}_{n}"))

        self.pool_carried = sem("pool_carried")
        self.sp_carried = sem("sp_carried")
        self.set = sem("rows_filled")
        self.stored = sem("qk_stored")
        self.loaded = [sem(f"qk_loaded{i}") for i in range(4)]
        self.qk_free = sem("qk_free")
        self.v_set = sem("v_set")
        self.scores = sem("scores")
        self.max = sem("row_max")
        self.split = sem("split")
        self.max_psum = sem("max_psum")
        self.max_rows = sem("max_rows")
        self.scores_t = sem("scores_t")
        self.probs = sem("probs")
        self.pv = sem("pv")
        self.taken = sem("taken")
        self.rsums_ready = sem("rsums_ready")
        self.normed = sem("normed")

    def buffers(self, sb, name):
        self.q = [sb(f"{name}_q{i}", [self.all, 4, T], F32R) for i in range(4)]
        self.k = [sb(f"{name}_k{i}", [self.all, self.nk, T], F32R) for i in range(4)]
        self.v = [sb(f"{name}_v{i}", [P, NT, 32 if self.shared else P]) for i in range(2)]
        self.ones = sb(f"{name}_ones", [P, 32])
        self.mx = sb(f"{name}_mx", [P, 2, 16])
        self.parts = sb(f"{name}_parts", [P, 2, 16, 3], BF16)
        self.rest = sb(f"{name}_rest", [P, 16])
        self.pt = sb(f"{name}_pt", [P, 8, T])
        self.sums = sb(f"{name}_sums", [P, T])


SPLIT = 5
BANK_MAX, BANK_OUT, BANK_SUM = 5, 6, 7
MAX_T, MAX_COPY, EXP, PV, TAKE, RSUM, UPPER = 20, 21, 28, 33, 34, 35, 45
STEPS_AFTER = UPPER + 1


def attention_set(dve, at):
    link = chain(dve, at.set, 0, [0])

    def fill(of, rows):
        link(dve.tensor_copy(of[rows], at.sums[rows].unsqueeze(1).to_broadcast([of[rows].shape[0], of.shape[1], T])))

    if at.rows < at.top:
        link(dve.memset(at.sums[:], 0.0))
        for of in at.q + at.k:
            fill(of, slice(at.top - 32, at.top))
    link(dve.memset(at.sums[:], 1.0))
    for of in at.k:
        fill(of, slice(at.top, at.all))
    link(dve.tensor_copy(at.ones[:], at.sums[:, 0:32]))


def constant_rows(at):
    return 6 + (9 if at.rows < at.top else 0)


def load_heads(sp, at, b):
    rounds = at.groups // 4
    carry_wait(sp, at.sp_carried)
    with sp.Fori(0, rounds) as r:
        for slot in range(4):
            sp.wait_ge(at.qk_free, b * at.groups + r * 4 + slot + 1)
            for n, (qp, kp) in enumerate(((0, 0), (0, 1), (1, 0))):
                rows = slice(n * at.dh, (n + 1) * at.dh)
                sp.dma_start(at.q[slot][rows].bitcast(F32), at.q_planes[ds(b * 2 + qp, 1), ds(r * 16 + slot * 4, 4)]
                             .rearrange("a h d s -> d (a h) s")).then_inc(at.loaded[slot], 16)
                keys = r * 4 + slot if at.shared else r * 16 + slot * 4
                sp.dma_start(at.k[slot][rows].bitcast(F32), at.k_planes[ds(b * 2 + kp, 1), ds(keys, at.nk)]
                             .rearrange("a h d s -> d (a h) s")).then_inc(at.loaded[slot], 16)


def attend_pool(pool, at, v, b, out, lower):
    n = at.v[0].shape[2]
    for g in range(at.groups + 2):
        if g < at.groups:
            if g >= 2:
                pool.wait_ge(at.pv, b * at.units // 4 + (g - 1) * 4)
            carry_wait(pool, at.pool_carried)
            pool.tensor_copy(at.v[g % 2][:], v[:, :, g * n:(g + 1) * n]).then_inc(at.v_set, 1)
            pool.wait_ge(at.max, b * at.units + (g + 1) * 16)
            if g >= 2:
                pool.wait_ge(at.max_psum, b * at.heads + (g - 1) * 4)
            link = chain(pool, at.split, (b * at.groups + g) * SPLIT, [0])
            carry_wait(pool, at.pool_carried)
            mx, parts = at.mx[:, g % 2], at.parts[:, g % 2]
            link(pool.tensor_copy(parts[:, :, 0], mx))
            link(pool.tensor_tensor(at.rest[:], mx, parts[:, :, 0], ALU.subtract))
            carry_wait(pool, at.pool_carried)
            link(pool.tensor_copy(parts[:, :, 1], at.rest[:]))
            link(pool.tensor_tensor(at.rest[:], at.rest[:], parts[:, :, 1], ALU.subtract))
            carry_wait(pool, at.pool_carried)
            link(pool.tensor_copy(parts[:, :, 2], at.rest[:]))
        if g >= 2:
            pool.wait_ge(at.rsums_ready, (b * at.groups + g - 1) * NT)
            pool.wait_ge(at.taken, (b * at.groups + g - 1) * 2)
            pool.tensor_tensor(out(g - 2), out(g - 2), at.sums[:], ALU.mult).then_inc(at.normed, 1)
            lower(g - 2)


def attend_pe(pe, at, ps, ident_b, mask_b, b):
    for s in range(at.units + STEPS_AFTER):
        x = s
        if x < at.units:
            g, j, i = x // 16, x % 16 // 4, x % 4
            if x % 16 == 0:
                pe.wait_ge(at.loaded[g % 4], (b * (at.groups // 4) + g // 4 + 1) * 96)
            if x >= 2:
                pe.wait_ge(at.max, b * at.units + x - 1)
            keys = (i + 1) * P
            pe.matmul(ps[x % 2][:, 0:keys], at.q[g % 4][0:at.rows, j, i * P:keys],
                      at.k[g % 4][0:at.rows, 0 if at.shared else j, 0:keys], start=True, stop=False)
            pe.matmul(ps[x % 2][:, i * P:keys], ident_b, mask_b, start=False, stop=True).then_inc(at.scores, 1)
        x = s - MAX_T
        if 0 <= x < at.units and x % 16 in (0, 2, 4, 6):
            g, j = x // 16, x % 16 // 2
            if j == 0:
                pe.wait_ge(at.split, (b * at.groups + g + 1) * SPLIT)
            if g + j > 0:
                pe.wait_ge(at.max_rows, b * at.heads + g * 4 + j)
            for i in range(NT):
                turned = pe.matmul(ps[BANK_MAX][at.top:at.all, i * P:(i + 1) * P], at.parts[:, g % 2, j * 4 + i],
                                   ident_b, start=True, stop=True)
            turned.then_inc(at.max_psum, 1)
        x = s - EXP
        if 0 <= x < at.units:
            g, kt, j = x // 16, x % 16 // 4, x % 4
            if kt == 0:
                pe.wait_ge(at.max_rows, b * at.heads + g * 4 + j + 1)
            if x >= 3:
                pe.wait_ge(at.probs, b * at.units + x - 2)
            queries = (NT - kt) * P
            scores = pe.matmul(ps[2 + x % 3][:, 0:queries], at.k[g % 4][:, 0 if at.shared else j, kt * P:(kt + 1) * P],
                               at.q[g % 4][:, j, kt * P:], start=True, stop=False)
            if x % 16 == 15:
                scores.then_inc(at.qk_free, 1)
            pe.matmul(ps[2 + x % 3][:, 0:P], mask_b, ident_b, start=False, stop=True).then_inc(at.scores_t, 1)
        x = s - PV
        if 0 <= x < at.units and x % 4 == 0:
            g, kt = x // 16, x % 16 // 4
            if kt == 0:
                pe.wait_ge(at.v_set, b * at.groups + g + 1)
                if g > 0:
                    pe.wait_ge(at.taken, (b * at.groups + g) * 2)
            pe.wait_ge(at.probs, b * at.units + x + 4)
            for bank in (BANK_OUT, BANK_SUM):
                for j in range(4):
                    left = (at.ones[:] if bank == BANK_SUM else
                            at.v[g % 2][:, kt] if at.shared else at.v[g % 2][:, kt, j * 32:(j + 1) * 32])
                    product = pe.matmul(ps[bank][j * 32:(j + 1) * 32, kt * P:], left, at.pt[:, (x + j) % 8, kt * P:],
                                        start=(kt == 0), stop=(kt == NT - 1))
            product.then_inc(at.pv, 1)


def attend_dve(dve, at, ps, b):
    for s in range(at.units + STEPS_AFTER):
        x = s
        if x < at.units:
            if x % 16 == 0 and x >= 32:
                dve.wait_ge(at.split, (b * at.groups + x // 16 - 1) * SPLIT)
            dve.wait_ge(at.scores, b * at.units + x + 1)
            dve.tensor_reduce(at.mx[:, x // 16 % 2, x % 16:x % 16 + 1], ps[x % 2][:, 0:(x % 4 + 1) * P], AX.X, ALU.max,
                              negate=True).then_inc(at.max, 1)
        x = s - RSUM - 12
        if 0 <= x < at.units and x % 16 in (0, 2, 4, 6):
            g, i = x // 16, x % 16 // 2
            if i == 0:
                dve.wait_ge(at.taken, (b * at.groups + g) * 2 + 1)
            tile = at.sums[:, i * P:(i + 1) * P]
            dve.reciprocal(tile, tile).then_inc(at.rsums_ready, 1)


def attend_act(act, at, ps, b, out, out_free, upper):
    for s in range(at.units + STEPS_AFTER):
        x = s - MAX_COPY
        if 0 <= x < at.units and x % 16 in (0, 2, 4, 6):
            g, j = x // 16, x % 16 // 2
            act.wait_ge(at.max_psum, b * at.heads + g * 4 + j + 1)
            act.copy(at.q[g % 4][at.top:at.all, j], ps[BANK_MAX][at.top:at.all]).then_inc(at.max_rows, 1)
        x = s - EXP
        if 0 <= x < at.units:
            kt = x % 16 // 4
            act.wait_ge(at.scores_t, b * at.units + x + 1)
            if x >= 8:
                act.wait_ge(at.pv, b * at.units // 4 + x // 4 - 1)
            act.activation(at.pt[:, x % 8, kt * P:], ps[2 + x % 3][:, 0:(NT - kt) * P], ACT.Exp).then_inc(at.probs, 1)
        x = s - TAKE
        if 0 <= x < at.units and x % 16 == 12:
            g = x // 16
            act.wait_ge(at.pv, b * at.units // 4 + x // 4 + 1)
            if g >= 1:
                act.wait_ge(at.normed, b * at.groups + g)
            act.copy(at.sums[:], ps[BANK_SUM][:]).then_inc(at.taken, 1)
            if out_free and g >= 2:
                act.wait_ge(out_free, b * at.groups + g - 1)
            act.copy(out(g), ps[BANK_OUT][:]).then_inc(at.taken, 1)
        x = s - UPPER
        if 0 <= x < at.units and x % 16 == 12:
            upper(x // 16)


def carry_wait(eng, carried):
    eng.sem_inc(carried, 1)


class Norm:

    def __init__(self, ctx, nc, name, per):
        self.per = per
        self.carried = ctx.enter_context(nc.semaphore(f"{name}_carried"))
        self.var = ctx.enter_context(nc.semaphore(f"{name}_var"))
        self.rstd = ctx.enter_context(nc.semaphore(f"{name}_rstd"))

    def buffers(self, sb, name):
        self.stats = sb(f"{name}_stats", [P, NT, 6])
        self.mv = sb(f"{name}_mv", [P, NT, 2])
        self.ve = sb(f"{name}_ve", [P, NT])
        self.r = sb(f"{name}_r", [P, NT])


def norm_stats(dve, link, nm, x):
    for t in range(NT):
        last = dve.bn_stats(nm.stats[:, t], x[:, t])
    link(last)
    carry_wait(dve, nm.carried)
    for t in range(NT):
        last = dve.bn_aggr(nm.mv[:, t], nm.stats[:, t])
    link(last)
    dve.tensor_scalar(nm.ve[:], nm.mv[:, :, 1], EPS, None, ALU.add).then_inc(nm.var, 1)


def norm_apply(dve, nm, x, out, b, k):
    dve.wait_ge(nm.rstd, b * nm.per + k + 1)
    for t in range(NT):
        last = dve.tensor_scalar(out[:, t], x[:, t], nm.mv[:, t, 0:1], nm.r[:, t:t + 1], ALU.subtract, ALU.mult)
    return last


def norm_dve(dve, link, nm, x, out, b, k):
    norm_stats(dve, link, nm, x)
    return norm_apply(dve, nm, x, out, b, k)


def norm_pool(pool, nm, power, b, k):
    pool.wait_ge(nm.var, b * nm.per + k + 1)
    pool.tensor_tensor(nm.r[:], nm.ve[:], power[:, 0:NT], ALU.pow).then_inc(nm.rstd, 1)


def chain(eng, sem, base, done):
    def link(ins):
        done[0] += 1
        ins.then_inc(sem, 1)
        eng.wait_ge(sem, base + done[0])
    return link


def phase_one(nc, keep, a, scratch):
    with ExitStack() as ctx:
        def sb(name, shape, dt=F32):
            return ctx.enter_context(nc.sbuf_tensor("a_" + name, shape, dt))

        def sem(name):
            return ctx.enter_context(nc.semaphore("a_" + name))

        ps = [ctx.enter_context(nc.psum_tensor(f"a_ps{i}", [P, T], F32)) for i in range(8)]
        at = Attention(nc, ctx, "a_at", H0, DH0, True, scratch["q0"], scratch["k0"])
        at.buffers(sb, "at")
        nm = Norm(ctx, nc, "a_ln", 3)
        nm.buffers(sb, "ln")

        square = sb("square", [P, 3, P])
        ident, causal, ones = square[:, 0], square[:, 1], square[:, 2]
        ident_b = sb("ident_b", [P, P], BF16)
        mask_b = sb("mask_b", [P, P], BF16)
        pe_t = sb("pe", [P, NT, E_CH])
        small = sb("small", [P, NTILE + 2 * GRID])
        convw = sb("convw", [P, TAPS, P])
        convb = sb("convb", [P, P])
        spos = sb("spos", [P, 2, P])
        gamma = sb("gamma", [P, D])
        beta = sb("beta", [P, D])
        power = sb("power", [P, NT])
        ids = sb("ids", [P, B * NT], U32)
        ids_now = sb("ids_now", [P, NT], U32)
        wq = sb("wq", [P, NT, D], F32R)
        wk = sb("wk", [P, NT, P], F32R)
        wv = sb("wv", [P, NT, P], F32R)
        wo = sb("wo", [P, 2 * NT, D], F32R)
        wparts = [(wq, D), (wk, P), (wv, P), (wo, D)]
        asum = sb("asum", [P, 4])
        mean_abs = sb("mean_abs", [P, 4])
        wscale = sb("wscale", [P, 5])
        slopes = sb("slopes", [P, NT, GRID])
        ssum = sb("ssum", [P, NT])
        ssign = sb("ssign", [P, NT])
        sdiag = sb("sdiag", [P, NT, P])
        slope_sign = sb("slope_sign", [P, D])

        emb = sb("emb", [P, NT, E_CH])
        tok_both = sb("tok", [P, 2 * NT, E_CH])
        tok = [tok_both[:, 0:NT], tok_both[:, NT:]]
        tmx = sb("tmx", [P, NT])
        texp = sb("texp", [P, NT, E_CH])
        tsum = sb("tsum", [P, NT])
        trs = sb("trs", [P, NT])
        sel = sb("sel", [P, NT, E_CH])
        sel_t = sb("sel_t", [P, T])
        xpad = sb("xpad", [P, T + TAPS - 1])
        h = sb("h", [P, NT, D])
        hn = sb("hn", [P, NT, D])
        x = sb("x", [P, NT, D])
        oth = sb("oth", [P, 2 * NT, T], F32R)
        otl = sb("otl", [P, 2 * NT, T], F32R)
        xh, xl = oth[:, 0:NT], otl[:, 0:NT]
        o32 = [flat(emb), flat(texp)]
        qh = sb("qh", [P, NT + 1, T], F32R)
        ql = sb("ql", [P, NT + 1, T], F32R)
        v = sb("v", [P, NT, H0 // G0, 32])
        sg, xf = at.pt[:, 0:NT], at.pt[:, NT:]
        ts, key, oh = (tok_both[:, n * 2:n * 2 + 2].rearrange("p a c -> p (a c)").rearrange("p (t n) -> p t n", t=NT)
                       for n in range(3))
        cs = sb("cs", [P, NT * NCLUSTER])
        kmax = sb("kmax", [P, NT])
        pen = sel_t[:, 0:NT * NTILE].rearrange("p (t n) -> p t n", t=NT)
        xs = sb("xs", [P, NT, SLICE])
        ext = sb("ext", [P, 2, NT])
        cand = at.sums[:].rearrange("p (a t n) -> p a t n", a=2, t=NT)
        cmax = sel_t[:, NT * NTILE:(NT + 2) * NTILE].rearrange("p (k n) -> p k n", k=2)

        raw = [h[:], *(x[:, n].rearrange("p (c n) -> p c n", c=NT) for n in range(2)), at.pt[:]]

        consts = sem("consts")
        raw_in = sem("raw_in")
        ids_in = sem("ids_in")
        bf_ready = sem("bf_ready")
        pool_set = sem("pool_set")
        asum_ready = sem("asum_ready")
        mean_psum = sem("mean_psum")
        w_ready = sem("w_ready")
        sdiag_ready = sem("sdiag_ready")
        sign_psum = sem("sign_psum")
        ssum_ready = sem("ssum_ready")
        ssign_ready = sem("ssign_ready")
        pool_carried = sem("pool_carried")
        ids_set = sem("ids_set")
        emb_in = sem("emb_in")
        tok_ready = sem("tok_ready")
        tmx_ready = sem("tmx_ready")
        texp_ready = sem("texp_ready")
        sel_ready = sem("sel_ready")
        tok_t = sem("tok_t")
        selt_psum = sem("selt_psum")
        selt_ready = sem("selt_ready")
        xpad_ready = sem("xpad_ready")
        ext_psum = sem("ext_psum")
        conv_psum = sem("conv_psum")
        h_built = sem("h_built")
        x_ready = sem("x_ready")
        xt_psum = sem("xt_psum")
        hi_ready = sem("hi_ready")
        lo_ready = sem("lo_ready")
        q_psum = sem("q_psum")
        qhi_ready = sem("qhi_ready")
        qlo_ready = sem("qlo_ready")
        v_psum = sem("v_psum")
        v_ready = sem("v_ready")
        ohi_ready = sem("ohi_ready")
        olo_ready = sem("olo_ready")
        o_psum = sem("o_psum")
        xn_ready = sem("xn_ready")
        hn_ready = sem("hn_ready")
        hn_out = sem("hn_out")
        xn2_ready = sem("xn2_ready")
        xf_ready = sem("xf_ready")
        sg_ready = sem("sg_ready")
        h_used = sem("h_used")
        dve_chain = sem("dve_chain")
        DVE_STEPS = 24

        with nc.Block() as block:
            @block.sync
            def _(sp):
                sp.sem_inc(at.stored, 1)
                sp.sem_inc(hn_out, 1)
                sp.dma_start(ids[:], a["ids"]).then_inc(ids_in, 16)
                for w, of in zip(raw, ("wq", "wk", "wv", "wo")):
                    sp.dma_start(w, a[of]).then_inc(raw_in, 16)
                loads = [(square, a["c_square"]), (pe_t, a["c_pe"]), (convw, a["convw"]), (spos, a["spos"]),
                         (slopes, a["slopes_rows"]),
                         (small, a["c_small"].partition_broadcast(P)), (convb, a["convb"].partition_broadcast(P)),
                         (gamma, a["gamma"].partition_broadcast(P)), (beta, a["beta"].partition_broadcast(P))]
                for to, of in loads:
                    sp.dma_start(to[:], of).then_inc(consts, 16)
                assert len(loads) == 9
                sp.wait_ge(at.set, constant_rows(at))
                with sp.Fori(0, B) as b:
                    for m in range(NT + 1):
                        sp.wait_ge(qlo_ready, b * 5 + m + 1)
                        for plane, half in enumerate((qh, ql)):
                            to = (scratch["q0"][ds(b * 2 + plane, 1), m * 8:(m + 1) * 8] if m < NT
                                  else scratch["k0"][ds(b * 2 + plane, 1)])
                            sp.dma_start(to.rearrange("a h d s -> (a h d) s"), half[:, m].bitcast(F32)).then_inc(at.stored, 16)
                    sp.wait_ge(at.stored, b * 160 + 160 + 1)
                    load_heads(sp, at, b)
                    sp.wait_ge(hn_ready, b + 1)
                    sp.dma_start(scratch["h1"][ds(b, 1)].rearrange("a p n -> (a p) n"),
                                 hn[:].rearrange("p t n -> p (t n)")).then_inc(hn_out, 16)
                sp.wait_ge(hn_out, B * 16 + 1)

            @block.gpsimd
            def _(pool):
                pool.memset(power[:], -0.5).then_inc(pool_set, 1)
                pool.wait_ge(pool_set, 1)
                pool.wait_ge(ids_in, 16)
                pool.wait_ge(consts, 9 * 16)
                v_rows = v[:].rearrange("p t g d -> p t (g d)")
                with pool.Fori(0, B) as b:
                    pool.wait_ge(tok_ready, b * 2 + 1)
                    pool.tensor_copy(ids_now[:], ids[:, ds(b * NT, NT)]).then_inc(ids_set, 1)
                    pool.wait_ge(ids_set, b + 1)
                    carry_wait(pool, pool_carried)
                    for t in range(NT):
                        pool.indirect_dma_start(
                            out=emb[:, t], out_offset=None, in_=a["table"],
                            in_offset=bass.IndirectOffsetOnAxis(ap=ids_now[:, t:t + 1], axis=0)).then_inc(emb_in, 16)
                    norm_pool(pool, nm, power, b, 0)
                    pool.wait_ge(v_ready, b + 1)

                    def lower_of_group(g):
                        pool.wait_ge(ohi_ready, b * at.groups + g + 1)
                        pool.tensor_tensor(otl[:, g], o32[g % 2], oth[:, g].bitcast(F32),
                                           ALU.subtract).then_inc(olo_ready, 1)

                    attend_pool(pool, at, v_rows, b, lambda g: o32[g % 2], lower_of_group)
                    norm_pool(pool, nm, power, b, 1)
                    pool.wait_ge(xn_ready, b + 1)
                    pool.wait_ge(hn_out, b * 16 + 1)
                    pool.tensor_tensor(hn[:], h[:], x[:], ALU.add).then_inc(hn_ready, 1)
                    norm_pool(pool, nm, power, b, 2)
                    pool.wait_ge(xn2_ready, b + 1)
                    pool.tensor_tensor(xf, xf, gamma[:].unsqueeze(1).to_broadcast([P, NT, D]), ALU.mult).then_inc(xf_ready, 1)
                    pool.wait_ge(xf_ready, b * 2 + 1)
                    pool.tensor_tensor(xf, xf, beta[:].unsqueeze(1).to_broadcast([P, NT, D]), ALU.add).then_inc(xf_ready, 1)

            @block.scalar
            def _(act):
                act.wait_ge(asum_ready, 1)
                for (w, _), of in zip(wparts, raw):
                    act.activation(w[:], of, ACT.Sign).then_inc(w_ready, 1)
                act.wait_ge(ssum_ready, 1)
                act.activation(ssign[:], ssum[:], ACT.Sign).then_inc(ssign_ready, 1)
                act.wait_ge(bf_ready, 5)
                with act.Fori(0, B) as b:
                    for z in range(2):
                        act.wait_ge(tmx_ready, b * 2 + z + 1)
                        if z == 0:
                            act.wait_ge(h_used, b + 1)
                        for t in range(NT):
                            last = act.activation(texp[:, t], tok[z][:, t], ACT.Exp, bias=tmx[:, t:t + 1], scale=1.0,
                                                  accum_out=tsum[:, t:t + 1])
                        last.then_inc(texp_ready, 1)
                        act.wait_ge(tok_t, b * 2 + z + 1)
                        if z == 0:
                            act.copy(xpad[:, TAPS - 1:], ps[0][:]).then_inc(xpad_ready, 1)
                        act.copy(h[:, 2 * z], ps[0][:]).then_inc(h_built, 1)
                        act.wait_ge(ext_psum, b * 2 + z + 1)
                        act.copy(h[:, 2 * z + 1], ps[2][:]).then_inc(h_built, 1)

                    def upper():
                        for c in range(NT):
                            act.wait_ge(xt_psum, b * 4 + c + 1)
                            act.copy(xh[:, c], ps[c][:]).then_inc(hi_ready, 1)

                    upper()
                    act.wait_ge(at.stored, b * 160 + 1)
                    for m in range(NT + 1):
                        act.wait_ge(q_psum, b * 5 + m + 1)
                        act.activation(qh[:, m], ps[(4 + m) % 8][:], ACT.Copy,
                                       scale=wscale[:, 4:5] if m < NT else wscale[:, 1:2]).then_inc(qhi_ready, 1)

                    def upper_of_group(g):
                        act.wait_ge(at.normed, b * at.groups + g + 1)
                        act.copy(oth[:, g], o32[g % 2]).then_inc(ohi_ready, 1)

                    attend_act(act, at, ps, b, lambda g: o32[g % 2], olo_ready, upper_of_group)
                    act.wait_ge(xf_ready, b * 2 + 2)
                    act.activation(sg, xf, ACT.Sign).then_inc(sg_ready, 1)

            @block.vector
            def _(dve):
                attention_set(dve, at)
                dve.sem_inc(tok_ready, 1)
                dve.sem_inc(h_used, 1)
                dve.memset(xpad[:, 0:TAPS - 1], 0.0).then_inc(bf_ready, 1)
                dve.memset(keep["best"][:], -BIG)
                dve.memset(v[:], 0.0).then_inc(bf_ready, 1)
                dve.wait_ge(consts, 9 * 16)
                dve.tensor_copy(ident_b[:], ident).then_inc(bf_ready, 1)
                dve.tensor_copy(mask_b[:], causal).then_inc(bf_ready, 1)
                dve.wait_ge(raw_in, 64)
                for n, w in enumerate(raw):
                    last = dve.tensor_reduce(asum[:, n:n + 1], w, AX.XY, ALU.add, apply_absolute_value=True)
                last.then_inc(asum_ready, 1)
                dve.tensor_reduce(ssum[:], slopes[:], AX.X, ALU.add).then_inc(ssum_ready, 1)
                dve.wait_ge(mean_psum, 1)
                for n, (_, w) in enumerate(wparts):
                    last = dve.tensor_scalar(wscale[:, n:n + 1], ps[0][:, n:n + 1], 1.0 / (w * D), EPS, ALU.mult, ALU.max)
                last.then_inc(mean_psum, 1)
                dve.wait_ge(mean_psum, 2)
                dve.tensor_scalar(wscale[:, 4:5], wscale[:, 0:1], DH0 ** -0.5, None, ALU.mult).then_inc(bf_ready, 1)
                dve.wait_ge(bf_ready, 5)
                dve.wait_ge(ssign_ready, 1)
                for c in range(NT):
                    dve.tensor_scalar(sdiag[:, c], ident, ssign[:, c:c + 1], None, ALU.mult).then_inc(sdiag_ready, 1)
                dve.wait_ge(sign_psum, 1)
                dve.tensor_copy(slope_sign[:], ps[1][:]).then_inc(sign_psum, 1)
                dve.wait_ge(sign_psum, 2)
                with dve.Fori(0, B) as b:
                    steps = [0]
                    link = chain(dve, dve_chain, b * DVE_STEPS, steps)
                    for z in range(2):
                        if z == 0:
                            dve.wait_ge(emb_in, b * 64 + 64)
                            dve.scalar_tensor_tensor(tok[0][:], emb[:], float(np.sqrt(np.float32(E_CH))), pe_t[:],
                                                     ALU.mult, ALU.add).then_inc(tok_ready, 1)
                        else:
                            dve.wait_ge(conv_psum, b + 1)
                            dve.tensor_tensor(tok[1][:], ps[3][:].rearrange("p (t c) -> p t c", t=NT),
                                              convb[:].unsqueeze(1).to_broadcast([P, NT, P]), ALU.add).then_inc(tok_ready, 1)
                        dve.wait_ge(tok_ready, b * 2 + z + 1 + 1)
                        dve.tensor_reduce(tmx[:], tok[z][:], AX.X, ALU.max, negate=True).then_inc(tmx_ready, 1)
                        dve.wait_ge(texp_ready, b * 2 + z + 1)
                        link(dve.reciprocal(trs[:], tsum[:]))
                        dve.tensor_tensor(sel[:], texp[:], trs[:].unsqueeze(2).to_broadcast([P, NT, E_CH]),
                                          ALU.mult).then_inc(sel_ready, 1)
                        dve.wait_ge(selt_psum, b * 2 + z + 1)
                        dve.tensor_copy(sel_t[:], ps[1][:]).then_inc(selt_ready, 1)
                    dve.wait_ge(h_built, b * 4 + 4)
                    norm_dve(dve, link, nm, h, x, b, 0).then_inc(x_ready, 1)

                    def lower():
                        for c in range(NT):
                            dve.wait_ge(hi_ready, b * 4 + c + 1)
                            dve.tensor_tensor(xl[:, c], ps[c][:], xh[:, c].bitcast(F32), ALU.subtract).then_inc(lo_ready, 1)

                    lower()
                    for m in range(NT + 1):
                        dve.wait_ge(qhi_ready, b * 5 + m + 1)
                        dve.scalar_tensor_tensor(ql[:, m], ps[(4 + m) % 8][:], wscale[:, 4:5] if m < NT else wscale[:, 1:2],
                                                 qh[:, m].bitcast(F32), ALU.mult, ALU.subtract).then_inc(qlo_ready, 1)
                    dve.wait_ge(v_psum, b + 1)
                    dve.tensor_scalar(v[:, :, :, 0:DH0].rearrange("p t g d -> p (t g) d"),
                                      ps[1][:].rearrange("p (n d) -> p n d", d=DH0), wscale[:, 2:3], None,
                                      ALU.mult).then_inc(v_ready, 1)
                    attend_dve(dve, at, ps, b)
                    for t in range(NT):
                        dve.wait_ge(o_psum, b * 4 + t + 1)
                        last = dve.scalar_tensor_tensor(h[:, t], ps[4 + t][:], wscale[:, 3:4], h[:, t], ALU.mult, ALU.add)
                    link(last)
                    norm_dve(dve, link, nm, h, x, b, 1).then_inc(xn_ready, 1)
                    dve.wait_ge(xn_ready, b + 1)
                    norm_dve(dve, link, nm, x, xf, b, 2).then_inc(xn2_ready, 1)
                    dve.wait_ge(sg_ready, b + 1)
                    link(dve.tensor_tensor(sg, sg, slope_sign[:].unsqueeze(1).to_broadcast([P, NT, D]), ALU.mult))
                    link(dve.tensor_reduce(ts, sg.rearrange("p t (n s) -> p (t n) s", s=SLICE), AX.X, ALU.add))
                    link(dve.tensor_reduce(cs[:], ts.rearrange("p t (c n) -> p (t c) n", c=NCLUSTER), AX.X, ALU.add))
                    link(dve.tensor_scalar(cs[:], cs[:], 2048.0, None, ALU.mult))
                    link(dve.scalar_tensor_tensor(key, ts, 8.0, small[:, 0:NTILE].unsqueeze(1).to_broadcast([P, NT, NTILE]),
                                                  ALU.mult, ALU.add))
                    keyc = key.rearrange("p t (c n) -> p (t c) n", c=NCLUSTER)
                    link(dve.tensor_tensor(keyc, keyc, cs[:].unsqueeze(2).to_broadcast([P, NT * NCLUSTER, 8]), ALU.add))
                    link(dve.tensor_reduce(kmax[:], key, AX.X, ALU.max))
                    link(dve.tensor_tensor(oh, key, kmax[:].unsqueeze(2).to_broadcast([P, NT, NTILE]), ALU.is_equal))
                    dve.tensor_copy(keep["onehot"][:, ds(b * NT, NT)], oh)
                    link(dve.tensor_scalar(pen, oh, 1.0, BIG, ALU.subtract, ALU.mult))
                    link(dve.tensor_tensor(sg.rearrange("p t (n s) -> p (t n) s", s=SLICE),
                                           xf.rearrange("p t (n s) -> p (t n) s", s=SLICE),
                                           oh.rearrange("p t n -> p (t n)").unsqueeze(2).to_broadcast([P, NT * NTILE, SLICE]),
                                           ALU.mult))
                    link(dve.tensor_reduce(xs[:], sg.rearrange("p t (n s) -> p t s n", s=SLICE), AX.X, ALU.add))
                    dve.tensor_copy(keep["slice"][:, ds(b * NT, NT)], xs[:])
                    dve.tensor_reduce(ext[:, 0], xs[:], AX.X, ALU.max)
                    link(dve.tensor_reduce(ext[:, 1], xs[:], AX.X, ALU.min, negate=True))
                    for k in range(2):
                        last = dve.tensor_tensor(cand[:, k], oh, ext[:, k].unsqueeze(2).to_broadcast([P, NT, NTILE]), ALU.mult)
                    link(last)
                    for k in range(2):
                        last = dve.tensor_tensor(cand[:, k], cand[:, k], pen, ALU.add)
                    link(last)
                    for k in range(2):
                        last = dve.tensor_reduce(cmax[:, k], cand[:, k].rearrange("p t n -> p n t"), AX.X, ALU.max)
                    link(last)
                    dve.tensor_tensor(keep["best"][:], keep["best"][:], cmax, ALU.max).then_inc(h_used, 1)
                    dve.wait_ge(h_used, b + 1 + 1)
                    assert steps[0] == DVE_STEPS

            @block.tensor
            def _(pe):
                pe.wait_ge(asum_ready, 1)
                pe.wait_ge(consts, 9 * 16)
                pe.matmul(ps[0][:, 0:4], ones, asum[:], start=True, stop=True).then_inc(mean_psum, 1)
                for c in range(NT):
                    pe.wait_ge(sdiag_ready, c + 1)
                    last = pe.matmul(ps[1][:, c * P:(c + 1) * P], ones, sdiag[:, c], start=True, stop=True)
                last.then_inc(sign_psum, 1)
                pe.wait_ge(sign_psum, 2)
                pe.wait_ge(bf_ready, 5)
                pe.wait_ge(w_ready, 4)
                pe.sem_inc(at.qk_free, 4)
                with pe.Fori(0, B) as b:
                    def turn(to, of, ready):
                        for t in range(NT):
                            last = pe.transpose(to[:, t * P:(t + 1) * P], of[:, t], ident)
                        last.then_inc(ready, 1)

                    pe.wait_ge(h_used, b + 1)
                    for z in range(2):
                        pe.wait_ge(tok_ready, b * 2 + z + 1 + 1)
                        if z == 1:
                            pe.wait_ge(h_built, b * 4 + 2)
                        turn(ps[0], tok[z], tok_t)
                        if z == 0:
                            pe.wait_ge(xpad_ready, b + 1)
                            for t in range(NT):
                                for k in range(TAPS):
                                    last = pe.matmul(ps[3][:, t * P:(t + 1) * P], xpad[:, t * P + k:t * P + k + P],
                                                     convw[:, k], start=(k == 0), stop=(k == TAPS - 1))
                            last.then_inc(conv_psum, 1)
                        pe.wait_ge(sel_ready, b * 2 + z + 1)
                        turn(ps[1], sel, selt_psum)
                        pe.wait_ge(selt_ready, b * 2 + z + 1)
                        pe.matmul(ps[2][:], spos[:, z], sel_t[:], start=True, stop=True).then_inc(ext_psum, 1)

                    def product(out, left, right, chunks=NT):
                        for c in range(chunks):
                            if chunks == NT:
                                pe.wait_ge(lo_ready, b * 4 + c + 1)
                            for half, hf in enumerate((oth, otl)):
                                last = pe.matmul(out, left(hf, c), right(hf, c), start=(c + half == 0), stop=(c == chunks - 1 and half == 1))
                        return last

                    pe.wait_ge(x_ready, b + 1)
                    for c in range(NT):
                        for t in range(NT):
                            last = pe.transpose(ps[c][:, t * P:(t + 1) * P], x[:, t, c * P:(c + 1) * P], ident)
                        last.then_inc(xt_psum, 1)
                    for m in range(NT):
                        product(ps[4 + m][:], lambda hf, c: wq[:, c, m * P:(m + 1) * P],
                                lambda hf, c: hf[:, c]).then_inc(q_psum, 1)
                    product(ps[0][:], lambda hf, c: wk[:, c], lambda hf, c: hf[:, c]).then_inc(q_psum, 1)
                    for t in range(NT):
                        last = product(ps[1][:, t * P:(t + 1) * P], lambda hf, c: hf[:, c, t * P:(t + 1) * P],
                                       lambda hf, c: wv[:, c])
                    last.then_inc(v_psum, 1)
                    pe.wait_ge(qlo_ready, b * 5 + 5)
                    pe.wait_ge(v_ready, b + 1)
                    attend_pe(pe, at, ps, ident_b[:], mask_b[:], b)
                    pe.wait_ge(olo_ready, b * at.groups + at.groups)
                    for t in range(NT):
                        product(ps[4 + t][:], lambda hf, c: hf[:, c, t * P:(t + 1) * P],
                                lambda hf, c: wo[:, c], 2 * NT).then_inc(o_psum, 1)


def phase_two(nc, keep, a, scratch):
    with ExitStack() as ctx:
        def sb(name, shape, dt=F32):
            return ctx.enter_context(nc.sbuf_tensor("b_" + name, shape, dt))

        def sem(name):
            return ctx.enter_context(nc.semaphore("b_" + name))

        ps = [ctx.enter_context(nc.psum_tensor(f"b_ps{i}", [P, T], F32)) for i in range(8)]
        at = Attention(nc, ctx, "b_at", H1, DH1, False, scratch["q1"], scratch["k1"])
        at.buffers(sb, "at")
        nm = Norm(ctx, nc, "b_ln", 1)
        nm.buffers(sb, "ln")
        NCELL = SLICE * GRID
        QK_SCALE = [float(DH1) ** -0.5, 1.0]
        QKV_BANKS = [(1, 2, 3), (6, 7, 0)]

        square = sb("square", [P, 3, P])
        ident, causal = square[:, 0], square[:, 1]
        ident_b = sb("ident_b", [P, P], BF16)
        mask_b = sb("mask_b", [P, P], BF16)
        small = sb("small", [P, NTILE + 2 * GRID])
        rope = sb("rope", [P, 2, NT, DH1])
        power = sb("power", [P, NT])
        wqkv = sb("wqkv", [P, NT, 3 * D])
        wout = sb("wout", [P, NT, D])
        bqkv = sb("bqkv", [P, 3 * D])
        bout = sb("bout", [P, D])
        lookup = sb("lookup", [NTILE, LOOKUP])
        h = sb("h", [P, NT, D])
        h2 = sb("h2", [P, NT, D])
        x = sb("x", [P, NT, D])
        xt = sb("xt", [P, NT, T])
        oh = sb("oh", [P, NT, NTILE])
        oht = sb("oht", [NTILE, T])
        look = sb("look", [P, NT, LOOKUP])
        xs = sb("xs", [P, NT, SLICE])
        den = sb("den", [P, NT])
        rden = sb("rden", [P, NT])
        u = sb("u", [P, NT, SLICE])
        u16 = sb("u16", [P, NT * SLICE])
        cell = sb("cell", [P, NT * SLICE])
        cells = sb("cells", [P, NT * SLICE, GRID])
        picked = sb("picked", [P, NT * SLICE, GRID])
        picked2 = sb("picked2", [P, NT * SLICE, GRID])
        bs = sb("bs", [P, 2, NT * SLICE])
        delta = sb("delta", [P, NT, SLICE])
        v = sb("v", [P, NT, D])
        qk, qk_cos, qk_sin = (flat(at.pt[:, n * 2:n * 2 + 2]) for n in range(3))
        half_h = [sb(f"half_h{i}", [P, NT, P], F32R) for i in range(2)]
        half_l = [sb(f"half_l{i}", [P, NT, P], F32R) for i in range(2)]

        consts = sem("consts")
        pe_carried = sem("pe_carried")
        ready = sem("ready")
        pool_set = sem("pool_set")
        best_t = sem("best_t")
        lookup_ready = sem("lookup_ready")
        h_in = sem("h_in")
        oh_ready = sem("oh_ready")
        oht_psum = sem("oht_psum")
        oht_ready = sem("oht_ready")
        look_psum = sem("look_psum")
        look_ready = sem("look_ready")
        delta_ready = sem("delta_ready")
        spread = sem("spread")
        x_ready = sem("x_ready")
        xt_psum = sem("xt_psum")
        xt_even = sem("xt_even")
        xt_odd = sem("xt_odd")
        qkv_psum = sem("qkv_psum")
        qkv_taken = sem("qkv_taken")
        rot_ready = sem("rot_ready")
        rope_ready = sem("rope_ready")
        qkt_psum = sem("qkt_psum")
        qhi_ready = sem("qhi_ready")
        qlo_ready = sem("qlo_ready")
        o_psum = sem("o_psum")
        h2_ready = sem("h2_ready")
        h2_out = sem("h2_out")
        tile_stored = sem("tile_stored")
        dve_chain = sem("dve_chain")
        DVE_STEPS = 28

        with nc.Block() as block:
            @block.sync
            def _(sp):
                for credited in (at.stored, h2_out, tile_stored):
                    sp.sem_inc(credited, 1)
                loads = [(square[:], a["c_square"]), (rope[:], a["c_rope"]), (wqkv[:], a["wqkv"]), (wout[:], a["wout"]),
                         (lookup[:, 0:2 * NCELL], a["splines"]), (lookup[:, 2 * NCELL + 2:], a["output_scale"]),
                         (small[:], a["c_small"].partition_broadcast(P)), (bqkv[:], a["bqkv"].partition_broadcast(P)),
                         (bout[:], a["bout"].partition_broadcast(P))]
                for to, of in loads:
                    sp.dma_start(to, of).then_inc(consts, 16)
                assert len(loads) == 9
                sp.wait_ge(at.set, constant_rows(at))
                with sp.Fori(0, B) as b:
                    sp.wait_ge(h2_ready, b * 4 + 1)
                    sp.dma_start(h[:].rearrange("p t n -> p (t n)"),
                                 scratch["h1"][ds(b, 1)].rearrange("a p n -> (a p) n")).then_inc(h_in, 16)
                    for t in range(NT):
                        for s in range(2):
                            sp.wait_ge(qlo_ready, b * 8 + t * 2 + s + 1)
                            for plane, half in enumerate((half_h, half_l)):
                                to = scratch["q1" if s == 0 else "k1"][ds(b * 2 + plane, 1)]
                                sp.dma_start(to.rearrange("a (c h) d s -> (h d) (a c) s", c=4)[:, :, t * P:(t + 1) * P],
                                             half[s][:].bitcast(F32)).then_inc(at.stored, 16)
                        sp.wait_ge(at.stored, b * 256 + (t + 1) * 64 + 1)
                        sp.sem_inc(tile_stored, 1)
                    load_heads(sp, at, b)
                    sp.wait_ge(h2_ready, b * 4 + 4 + 1)
                    sp.dma_start(scratch["h2"][ds(b, 1)].rearrange("a p n -> (a p) n"),
                                 h2[:].rearrange("p t n -> p (t n)")).then_inc(h2_out, 16)
                sp.wait_ge(h2_out, B * 16 + 1)

            @block.gpsimd
            def _(pool):
                pool.sem_inc(spread, 1)
                pool.memset(power[:], -0.5).then_inc(pool_set, 1)
                pool.wait_ge(pool_set, 1)
                pool.wait_ge(consts, 9 * 16)
                with pool.Fori(0, B) as b:
                    pool.wait_ge(delta_ready, b + 1)
                    pool.wait_ge(h2_out, b * 16 + 1)
                    for t in range(NT):
                        pool.tensor_tensor(h2[:, t].rearrange("p (n s) -> p n s", s=SLICE),
                                           oh[:, t].unsqueeze(2).to_broadcast([P, NTILE, SLICE]),
                                           delta[:, t].unsqueeze(1).to_broadcast([P, NTILE, SLICE]), ALU.mult).then_inc(spread, 1)
                    pool.wait_ge(h_in, b * 16 + 16)
                    pool.wait_ge(spread, b * 5 + 4 + 1)
                    pool.tensor_tensor(h2[:], h2[:], h[:], ALU.add).then_inc(spread, 1)
                    norm_pool(pool, nm, power, b, 0)
                    for t in range(NT):
                        pool.wait_ge(qkv_taken, b * 8 + t * 2 + 1)
                        src = qk.rearrange("p (n two d) -> p n two d", two=2, d=DH1 // 2)
                        dst = qk_sin.rearrange("p (n two d) -> p n two d", two=2, d=DH1 // 2)
                        for half in range(2):
                            pool.tensor_tensor(dst[:, :, half], src[:, :, 1 - half],
                                               rope[:, 1, t, half * 16:(half + 1) * 16].unsqueeze(1).to_broadcast([P, 2 * H1, 16]),
                                               ALU.mult).then_inc(rot_ready, 1)
                        pool.wait_ge(rope_ready, b * 4 + t + 1)
                    pool.wait_ge(qkv_taken, b * 8 + 8)
                    attend_pool(pool, at, v, b, lambda g: xt[:, g], lambda g: None)

            @block.scalar
            def _(act):
                act.wait_ge(ready, 2)
                with act.Fori(0, B) as b:
                    act.wait_ge(oht_psum, b + 1)
                    act.copy(oht[:], ps[0][0:NTILE, :]).then_inc(oht_ready, 1)
                    for t in range(NT):
                        act.wait_ge(look_psum, b * 4 + t + 1)
                        act.copy(look[:, t], ps[1 + t][:, 0:LOOKUP]).then_inc(look_ready, 1)

                    for c in (0, 2):
                        act.wait_ge(xt_psum, b * 4 + c + 1)
                        act.copy(xt[:, c], ps[c][:]).then_inc(xt_even, 1)
                    for t in range(NT):
                        for s in range(2):
                            act.wait_ge(qkt_psum, b * 8 + t * 2 + s + 1)
                            if s == 0:
                                act.wait_ge(tile_stored, b * 4 + t + 1)
                            act.activation(half_h[s][:], ps[4 + s][:].rearrange("p (c n) -> p c n", c=4), ACT.Copy,
                                           scale=QK_SCALE[s]).then_inc(qhi_ready, 1)
                    attend_act(act, at, ps, b, lambda g: xt[:, g], None, lambda g: None)

            @block.vector
            def _(dve):
                attention_set(dve, at)
                dve.sem_inc(h2_ready, 1)
                dve.wait_ge(consts, 9 * 16)
                dve.tensor_copy(ident_b[:], ident).then_inc(ready, 1)
                dve.tensor_copy(mask_b[:], causal).then_inc(ready, 1)
                dve.wait_ge(best_t, 2)
                dve.tensor_reduce(lookup[:, 2 * NCELL:2 * NCELL + 1], ps[1][0:NTILE, 0:P], AX.X, ALU.max,
                                  negate=True).then_inc(lookup_ready, 1)
                dve.tensor_reduce(lookup[:, 2 * NCELL + 1:2 * NCELL + 2], ps[0][0:NTILE, 0:P], AX.X, ALU.max).then_inc(lookup_ready, 1)
                with dve.Fori(0, B) as b:
                    steps = [0]
                    link = chain(dve, dve_chain, b * DVE_STEPS, steps)
                    dve.wait_ge(spread, b * 5 + 1)
                    dve.tensor_copy(xs[:], keep["slice"][:, ds(b * NT, NT)])
                    dve.tensor_copy(oh[:], keep["onehot"][:, ds(b * NT, NT)]).then_inc(oh_ready, 1)
                    dve.wait_ge(look_ready, b * 4 + 4)
                    least, most, scale = (look[:, :, 2 * NCELL + n] for n in range(3))
                    dve.wait_ge(oh_ready, b + 1)
                    dve.tensor_tensor(u[:], xs[:], least.unsqueeze(2).to_broadcast([P, NT, SLICE]), ALU.subtract)
                    link(dve.tensor_tensor(den[:], most, least, ALU.subtract))
                    link(dve.tensor_scalar(den[:], den[:], 1e-8, None, ALU.add))
                    link(dve.reciprocal(rden[:], den[:]))
                    link(dve.tensor_tensor(u[:], u[:], rden[:].unsqueeze(2).to_broadcast([P, NT, SLICE]), ALU.mult))
                    uf = u[:].rearrange("p t s -> p (t s)")
                    link(dve.tensor_scalar(uf, uf, 0.0, 1.0 - 1e-6, ALU.max, ALU.min))
                    link(dve.tensor_scalar(u16[:], uf, float(GRID), None, ALU.mult))
                    shape = [P, NT * SLICE, GRID]
                    link(dve.tensor_tensor(cells[:], u16[:].unsqueeze(2).to_broadcast(shape),
                                           small[:, NTILE + GRID:].unsqueeze(1).to_broadcast(shape), ALU.is_ge))
                    link(dve.tensor_reduce(cell[:], cells[:], AX.X, ALU.add))
                    link(dve.tensor_tensor(cells[:], cell[:].unsqueeze(2).to_broadcast(shape),
                                           small[:, NTILE:NTILE + GRID].unsqueeze(1).to_broadcast(shape), ALU.is_equal))
                    for n, pk in enumerate((picked, picked2)):
                        last = dve.tensor_tensor(pk[:].rearrange("p (t s) g -> p t (s g)", t=NT),
                                                 cells[:].rearrange("p (t s) g -> p t (s g)", t=NT),
                                                 look[:, :, n * NCELL:(n + 1) * NCELL], ALU.mult)
                    link(last)
                    for n, pk in enumerate((picked, picked2)):
                        last = dve.tensor_reduce(bs[:, n], pk[:], AX.X, ALU.add)
                    link(last)
                    link(dve.scalar_tensor_tensor(u16[:], cell[:], -1.0 / GRID, uf, ALU.mult, ALU.add))
                    link(dve.scalar_tensor_tensor(u16[:], u16[:], float(GRID), bs[:, 1], ALU.mult, ALU.mult))
                    link(dve.tensor_tensor(u16[:], u16[:], bs[:, 0], ALU.add))
                    dve.tensor_tensor(delta[:], u16[:].rearrange("p (t s) -> p t s", t=NT),
                                      scale.unsqueeze(2).to_broadcast([P, NT, SLICE]), ALU.mult).then_inc(delta_ready, 1)
                    dve.wait_ge(spread, b * 5 + 5 + 1)
                    norm_dve(dve, link, nm, h2, x, b, 0).then_inc(x_ready, 1)

                    for c in (1, 3):
                        dve.wait_ge(xt_psum, b * 4 + c + 1)
                        dve.tensor_copy(xt[:, c], ps[c][:]).then_inc(xt_odd, 1)
                    for t in range(NT):
                        dve.wait_ge(qkv_psum, b * 4 + t + 1)
                        banks = QKV_BANKS[t % 2]
                        link(dve.tensor_tensor(qk[:, 0:D], ps[banks[0]][:], bqkv[:, 0:D], ALU.add))
                        dve.tensor_tensor(qk[:, D:], ps[banks[1]][:], bqkv[:, D:2 * D], ALU.add).then_inc(qkv_taken, 1)
                        dve.tensor_tensor(v[:, t], ps[banks[2]][:], bqkv[:, 2 * D:], ALU.add).then_inc(qkv_taken, 1)
                        dve.wait_ge(qkv_taken, b * 8 + t * 2 + 1)
                        link(dve.tensor_tensor(qk_cos.rearrange("p (n d) -> p n d", d=DH1),
                                               qk.rearrange("p (n d) -> p n d", d=DH1),
                                               rope[:, 0, t].unsqueeze(1).to_broadcast([P, 2 * H1, DH1]), ALU.mult))
                        dve.wait_ge(rot_ready, b * 8 + t * 2 + 2)
                        dve.tensor_tensor(qk_cos, qk_cos, qk_sin, ALU.add).then_inc(rope_ready, 1)
                        for s in range(2):
                            dve.wait_ge(qhi_ready, b * 8 + t * 2 + s + 1)
                            dve.scalar_tensor_tensor(half_l[s][:], ps[4 + s][:].rearrange("p (c n) -> p c n", c=4), QK_SCALE[s],
                                                     half_h[s][:].bitcast(F32), ALU.mult, ALU.subtract).then_inc(qlo_ready, 1)
                    attend_dve(dve, at, ps, b)
                    for t in range(NT):
                        dve.wait_ge(o_psum, b * 4 + t + 1)
                        link(dve.tensor_tensor(h2[:, t], ps[4 + t][:], h2[:, t], ALU.add))
                        dve.tensor_tensor(h2[:, t], h2[:, t], bout[:], ALU.add).then_inc(h2_ready, 1)
                    assert steps[0] == DVE_STEPS

            @block.tensor
            def _(pe):
                pe.wait_ge(consts, 9 * 16)
                for k in range(2):
                    pe.transpose(ps[k][0:NTILE, 0:P], keep["best"][:, k], ident).then_inc(best_t, 1)
                pe.wait_ge(lookup_ready, 2)
                pe.wait_ge(ready, 2)
                pe.sem_inc(at.qk_free, 4)
                with pe.Fori(0, B) as b:
                    pe.wait_ge(oh_ready, b + 1)
                    carry_wait(pe, pe_carried)
                    for t in range(NT):
                        last = pe.transpose(ps[0][0:NTILE, t * P:(t + 1) * P], oh[:, t], ident)
                    last.then_inc(oht_psum, 1)
                    pe.wait_ge(oht_ready, b + 1)
                    pe.wait_ge(h2_ready, b * 4 + 1)
                    for t in range(NT):
                        pe.matmul(ps[1 + t][:, 0:LOOKUP], oht[:, t * P:(t + 1) * P], lookup[:],
                                  start=True, stop=True).then_inc(look_psum, 1)

                    def product(out, t, w):
                        for c in range(NT):
                            last = pe.matmul(out, xt[:, c, t * P:(t + 1) * P], w(c), start=(c == 0), stop=(c == NT - 1))
                        return last

                    pe.wait_ge(look_ready, b * 4 + 4)
                    pe.wait_ge(x_ready, b + 1)
                    for c in range(NT):
                        for t in range(NT):
                            last = pe.transpose(ps[c][:, t * P:(t + 1) * P], x[:, t, c * P:(c + 1) * P], ident)
                        last.then_inc(xt_psum, 1)
                    def qkv(t):
                        if t >= 2:
                            pe.wait_ge(qkv_taken, b * 8 + t * 2 - 2)
                        for s in range(3):
                            last = product(ps[QKV_BANKS[t % 2][s]][:], t, lambda c: wqkv[:, c, s * D:(s + 1) * D])
                        last.then_inc(qkv_psum, 1)

                    pe.wait_ge(xt_odd, b * 2 + 2)
                    pe.wait_ge(xt_even, b * 2 + 2)
                    qkv(0)
                    for t in range(NT):
                        if t + 1 < NT:
                            qkv(t + 1)
                        pe.wait_ge(rope_ready, b * 4 + t + 1)
                        for s in range(2):
                            if t > 0:
                                pe.wait_ge(qlo_ready, b * 8 + t * 2 + s - 1)
                            for c in range(NT):
                                last = pe.transpose(ps[4 + s][:, c * P:(c + 1) * P], qk_cos[:, s * D + c * P:s * D + (c + 1) * P], ident)
                            last.then_inc(qkt_psum, 1)
                    pe.wait_ge(qlo_ready, b * 8 + 8)
                    attend_pe(pe, at, ps, ident_b[:], mask_b[:], b)
                    pe.wait_ge(at.normed, b * at.groups + at.groups)
                    for t in range(NT):
                        product(ps[4 + t][:], t, lambda c: wout[:, c]).then_inc(o_psum, 1)


def phase_three(nc, a, scratch, out):
    with ExitStack() as ctx:
        def sb(name, shape, dt=F32):
            return ctx.enter_context(nc.sbuf_tensor("m_" + name, shape, dt))

        def sem(name):
            return ctx.enter_context(nc.semaphore("m_" + name))

        ps = [ctx.enter_context(nc.psum_tensor(f"m_ps{i}", [P, T], F32)) for i in range(8)]
        nm = Norm(ctx, nc, "m_ln", 1)
        nm.buffers(sb, "ln")
        ident = sb("ident", [P, 3, P])
        pick = sb("pick", [E, E * P])
        earlier = sb("earlier", [P, E, E])
        power = sb("power", [P, NT])
        euler = sb("euler", [P, NT, E])
        gate_w = sb("gate_w", [P, NT, E])
        w1 = sb("w1", [P, NT, E * HID])
        w2 = sb("w2", [P, 2 * E, D])
        s1 = sb("s1", [P, NT, D])
        s2 = sb("s2", [P, NT, D])
        b1 = sb("b1", [P, 2 * E + NT])
        b2 = sb("b2", [E + 1, D])
        h = sb("h", [P, NT, D])
        x = sb("x", [P, NT, D])
        y = sb("y", [P, NT, D])
        xt = sb("xt", [P, NT, T])
        logits = sb("logits", [P, NT, E])
        best = sb("best", [P, NT])
        above = sb("above", [P, NT * E, E])
        equal = sb("equal", [P, NT * E, E])
        rank = sb("rank", [P, NT * E])
        chosen = sb("chosen", [P, NT * E])
        shifted = sb("shifted", [P, NT, E])
        expo = sb("expo", [P, NT, E])
        total = sb("total", [P, NT])
        rtotal = sb("rtotal", [P, NT])
        gates = sb("gates", [P, NT, E])
        gates_t = sb("gates_t", [E + 1, T])
        act_out = [sb(f"act_out{i}", [P, T]) for i in range(3)]
        gated = [sb(f"gated{i}", [P, T]) for i in range(3)]

        consts = sem("consts")
        pool_set = sem("pool_set")
        pe_carried = sem("pe_carried")
        pool_carried = sem("pool_carried")
        ones_set = sem("ones_set")
        h_in = sem("h_in")
        h_kept = sem("h_kept")
        x_ready = sem("x_ready")
        xt_psum = sem("xt_psum")
        xt_ready = sem("xt_ready")
        logit_psum = sem("logit_psum")
        shifted_ready = sem("shifted_ready")
        expo_ready = sem("expo_ready")
        gates_ready = sem("gates_ready")
        gates_psum = sem("gates_psum")
        gates_t_ready = sem("gates_t_ready")
        gate_psum = sem("gate_psum")
        hid_psum = sem("hid_psum")
        hid_ready = sem("hid_ready")
        gated_ready = sem("gated_ready")
        hid_used = sem("hid_used")
        y_ready = sem("y_ready")
        y_out = sem("y_out")
        dve_chain = sem("dve_chain")
        norm_chain = sem("norm_chain")
        DVE_STEPS = 10
        NH = 2 * E + NT
        NG = 2 * E
        GATES_AT = NT
        NORM_AT, APPLY_AT = NT + 4, NT + 6
        BANK_LOGITS, BANK_GATES = 6, 7

        def over_sequences(eng, body):
            with eng.Fori(0, B - 1) as b:
                body(b, True)
            body(B - 1, False)

        with nc.Block() as block:
            @block.sync
            def _(sp):
                sp.sem_inc(y_out, 1)
                loads = [(ident[:], a["c_square"]), (pick[:], a["c_pick"]), (earlier[:].rearrange("p a b -> p (a b)"), a["c_earlier"].partition_broadcast(P)),
                         (gate_w[:], a["gate_w"]), (w1[:], a["w1"]), (w2[:], a["w2"]), (s1[:], a["s1"]), (s2[:], a["s2"]),
                         (b1[:], a["b1"]), (b2[0:E], a["b2"]), (b2[E:E + 1], a["sb2"])]
                for to, of in loads:
                    sp.dma_start(to, of).then_inc(consts, 16)
                assert len(loads) == 11

                def load(b):
                    sp.dma_start(h[:].rearrange("p t n -> p (t n)"),
                                 scratch["h2"][ds(b, 1)].rearrange("a p n -> (a p) n")).then_inc(h_in, 16)

                def sequence(b, more):
                    if more:
                        sp.wait_ge(h_kept, b + 1)
                        load(b + 1)
                    sp.wait_ge(y_ready, b * 4 + 4 + 1)
                    sp.dma_start(out[ds(b, 1)].rearrange("a (t p) n -> p (a t) n", p=P), y[:]).then_inc(y_out, 16)

                load(0)
                over_sequences(sp, sequence)
                sp.wait_ge(y_out, B * 16 + 1)

            @block.gpsimd
            def _(pool):
                pool.memset(power[:], -0.5).then_inc(pool_set, 1)
                pool.memset(euler[:], float(np.e)).then_inc(pool_set, 1)
                pool.wait_ge(pool_set, 2)

                def sequence(b, more):
                    pool.wait_ge(x_ready, b + 1)
                    pool.wait_ge(y_out, b * 16 + 1)
                    carry_wait(pool, pool_carried)
                    pool.tensor_copy(y[:], h[:]).then_inc(h_kept, 1)
                    pool.wait_ge(shifted_ready, b + 1)
                    pool.tensor_tensor(expo[:], euler[:], shifted[:], ALU.pow).then_inc(expo_ready, 1)
                    if more:
                        norm_pool(pool, nm, power, b + 1, 0)

                norm_pool(pool, nm, power, 0, 0)
                over_sequences(pool, sequence)

            @block.scalar
            def _(act):
                act.wait_ge(consts, 11 * 16)

                def sequence(b, more):
                    for c in range(NT):
                        act.wait_ge(xt_psum, b * 4 + c + 1)
                        act.copy(xt[:, c], ps[4 + c][:]).then_inc(xt_ready, 1)
                    for n in range(NH):
                        act.wait_ge(hid_psum, b * NH + n + 1)
                        if n >= 3:
                            act.wait_ge(hid_used, b * NH + n - 2)
                        of = b1[:, (n + NG) % NH:(n + NG) % NH + 1]
                        act.activation(act_out[n % 3][:], ps[4 + n % 2][:], ACT.Gelu, bias=of, scale=1.0).then_inc(hid_ready, 1)

                over_sequences(act, sequence)

            @block.vector
            def _(dve):
                dve.sem_inc(y_ready, 1)
                dve.memset(gates_t[:], 1.0).then_inc(ones_set, 1)
                dve.wait_ge(ones_set, 1)
                dve.wait_ge(consts, 11 * 16)
                norm = chain(dve, norm_chain, 0, [0])
                dve.wait_ge(h_in, 16)
                norm_stats(dve, norm, nm, h)
                norm_apply(dve, nm, h, x, 0, 0).then_inc(x_ready, 1)

                def sequence(b, more):
                    steps = [0]
                    link = chain(dve, dve_chain, b * DVE_STEPS, steps)
                    dve.wait_ge(logit_psum, b + 1)
                    link(dve.tensor_copy(logits[:], ps[BANK_LOGITS][:, 0:NT * E].rearrange("p (t e) -> p t e", t=NT)))
                    link(dve.tensor_reduce(best[:], logits[:], AX.X, ALU.max))
                    dve.tensor_tensor(shifted[:], logits[:], best[:].unsqueeze(2).to_broadcast([P, NT, E]),
                                      ALU.subtract).then_inc(shifted_ready, 1)
                    mine = logits[:].unsqueeze(3).to_broadcast([P, NT, E, E])
                    theirs = logits[:].unsqueeze(2).to_broadcast([P, NT, E, E])
                    dve.tensor_tensor(above[:].rearrange("p (t e) f -> p t e f", t=NT), theirs, mine, ALU.is_gt)
                    link(dve.tensor_tensor(equal[:].rearrange("p (t e) f -> p t e f", t=NT), theirs, mine, ALU.is_equal))
                    link(dve.tensor_tensor(equal[:].rearrange("p (t e) f -> p t (e f)", t=NT),
                                           equal[:].rearrange("p (t e) f -> p t (e f)", t=NT),
                                           earlier[:].rearrange("p e f -> p (e f)").unsqueeze(1).to_broadcast([P, NT, E * E]), ALU.mult))
                    link(dve.tensor_tensor(above[:], above[:], equal[:], ALU.add))
                    link(dve.tensor_reduce(rank[:], above[:], AX.X, ALU.add))
                    link(dve.tensor_scalar(chosen[:], rank[:], 2.0, None, ALU.is_lt))
                    dve.wait_ge(expo_ready, b + 1)
                    link(dve.tensor_tensor(gates[:].rearrange("p t e -> p (t e)"), expo[:].rearrange("p t e -> p (t e)"), chosen[:], ALU.mult))
                    link(dve.tensor_reduce(total[:], gates[:], AX.X, ALU.add))
                    link(dve.reciprocal(rtotal[:], total[:]))
                    dve.tensor_tensor(gates[:], gates[:], rtotal[:].unsqueeze(2).to_broadcast([P, NT, E]), ALU.mult).then_inc(gates_ready, 1)
                    dve.wait_ge(gates_psum, b + 1)
                    dve.tensor_copy(gates_t[0:E, :], ps[BANK_GATES][0:E, :]).then_inc(gates_t_ready, 1)
                    for n in range(NT, NH):
                        dve.wait_ge(gate_psum, b * E + (n - NT) // 2 + 1)
                        dve.wait_ge(hid_ready, b * NH + n + 1)
                        if n >= NT + 3:
                            dve.wait_ge(hid_used, b * NH + n - 2)
                        dve.tensor_tensor(gated[n % 3][:], ps[6 + (n - NT) // 2 % 2][:], act_out[n % 3][:], ALU.mult).then_inc(gated_ready, 1)
                        if more and n == NORM_AT:
                            dve.wait_ge(h_in, b * 16 + 32)
                            norm_stats(dve, chain(dve, norm_chain, b * 2 + 2, [0]), nm, h)
                        if more and n == APPLY_AT:
                            norm_apply(dve, nm, h, x, b + 1, 0).then_inc(x_ready, 1)
                    dve.wait_ge(hid_used, b * NH + NH)
                    for t in range(NT):
                        dve.tensor_tensor(y[:, t], ps[t][:], y[:, t], ALU.add).then_inc(y_ready, 1)
                    assert steps[0] == DVE_STEPS

                over_sequences(dve, sequence)

            @block.tensor
            def _(pe):
                pe.wait_ge(ones_set, 1)
                pe.wait_ge(consts, 11 * 16)

                def sequence(b, more):
                    pe.wait_ge(x_ready, b + 1)
                    for c in range(NT):
                        for t in range(NT):
                            last = pe.transpose(ps[4 + c][:, t * P:(t + 1) * P], x[:, t, c * P:(c + 1) * P], ident[:, 0])
                        last.then_inc(xt_psum, 1)
                    pe.wait_ge(xt_ready, b * 4 + 4)
                    for t in range(NT):
                        for c in range(NT):
                            last = pe.matmul(ps[BANK_LOGITS][:, t * E:(t + 1) * E], xt[:, c, t * P:(t + 1) * P], gate_w[:, c],
                                             start=(c == 0), stop=(c == NT - 1))
                    last.then_inc(logit_psum, 1)

                    def turn_gates():
                        pe.wait_ge(gates_ready, b + 1)
                        carry_wait(pe, pe_carried)
                        for t in range(NT):
                            last = pe.transpose(ps[BANK_GATES][0:E, t * P:(t + 1) * P], gates[:, t], ident[:, 0])
                        last.then_inc(gates_psum, 1)

                    def hidden(n):
                        m = n - NT
                        if m >= 0 and m % 2 == 0:
                            if m >= 4:
                                pe.wait_ge(gated_ready, b * NG + m - 2)
                            pe.matmul(ps[6 + m // 2 % 2][:], pick[:, m // 2 * P:(m // 2 + 1) * P], gates_t[0:E, :],
                                      start=True, stop=True).then_inc(gate_psum, 1)
                        if n >= 2:
                            pe.wait_ge(hid_ready, b * NH + n - 1)
                        for c in range(NT):
                            w = w1[:, c, m * P:(m + 1) * P] if m >= 0 else s1[:, c, n * P:(n + 1) * P]
                            last = pe.matmul(ps[4 + n % 2][:], w, xt[:, c], start=(c == 0), stop=(c == NT - 1))
                        last.then_inc(hid_psum, 1)

                    def output(n):
                        m = n - NT
                        if m >= 0:
                            pe.wait_ge(gated_ready, b * NG + m + 1)
                        else:
                            pe.wait_ge(hid_ready, b * NH + n + 1)
                        if n == 0:
                            pe.wait_ge(y_ready, b * 4 + 1)
                        for t in range(NT):
                            left = (gated if m >= 0 else act_out)[n % 3][:, t * P:(t + 1) * P]
                            right = w2[:, m] if m >= 0 else s2[:, n]
                            last = pe.matmul(ps[t][:], left, right, start=(n == 0), stop=(n == NH - 1))
                        last.then_inc(hid_used, 1)

                    hidden(0)
                    for n in range(1, NH):
                        if n == GATES_AT - 1:
                            turn_gates()
                        if n == GATES_AT:
                            pe.wait_ge(gates_t_ready, b + 1)
                        hidden(n)
                        output(n - 1)
                        if n == GATES_AT:
                            for t in range(NT):
                                pe.matmul(ps[t][:], gates_t[:, t * P:(t + 1) * P], b2[:], start=False, stop=False)
                    output(NH - 1)

                over_sequences(pe, sequence)


def program(nc, a, out):
    def dram(name, shape):
        return nc.dram_tensor(name, shape, F32).ap()

    scratch = {
        "q0": dram("q0", (2 * B, H0, DH0, T)), "k0": dram("k0", (2 * B, H0 // G0, DH0, T)),
        "q1": dram("q1", (2 * B, H1, DH1, T)), "k1": dram("k1", (2 * B, H1, DH1, T)),
        "h1": dram("h1", (B, P, NT * D)), "h2": dram("h2", (B, P, NT * D)),
    }
    with ExitStack() as ctx:
        keep = {n: ctx.enter_context(nc.sbuf_tensor("keep_" + n, s, F32)) for n, s in (
            ("onehot", [P, B * NT, NTILE]),
            ("slice", [P, B * NT, SLICE]),
            ("best", [P, 2, NTILE]),
        )}
        phase_one(nc, keep, a, scratch)
        phase_two(nc, keep, a, scratch)
    phase_three(nc, a, scratch, out)


def layout(i):
    def rows(w):
        return w.reshape(-1, P, w.shape[-1]).transpose(1, 0, 2)

    n = np.arange(3 * D)
    s, head, d = n // D, n % D // DH1, n % DH1
    order = head * 3 * DH1 + s * DH1 + d
    wo_rows = np.zeros((H0, 32, D), i["L0_attn_wo"].dtype)
    wo_rows[:, 0:DH0] = i["L0_attn_wo"].T.reshape(H0, DH0, D)
    return {
        "ids": i["x"].reshape(B * NT, P).T.astype(np.uint32),
        "table": i["L0_tok_emb_table"],
        "convw": i["L0_tok_conv_w"].transpose(1, 2, 0),
        "convb": i["L0_tok_conv_b"],
        "spos": np.stack([i["L0_tok_spos0"], i["L0_tok_spos1"]], 1),
        "wq": rows(i["L0_attn_wq"].T), "wk": rows(i["L0_attn_wk"].T),
        "wv": rows(i["L0_attn_wv"].T), "wo": rows(wo_rows.reshape(2 * D, D)),
        "gamma": i["L0_ffn_ln_gamma"], "beta": i["L0_ffn_ln_beta"],
        "slopes_rows": i["L0_ffn_spline_slopes"].reshape(NT, P, GRID).transpose(1, 0, 2),
        "splines": np.concatenate([i["L0_ffn_spline_bases"].reshape(NTILE, -1),
                                   i["L0_ffn_spline_slopes"].reshape(NTILE, -1)], 1),
        "output_scale": i["L0_ffn_output_scale"].reshape(NTILE, 1),
        "wqkv": rows(i["L1_attn_W_qkv"][order].T), "bqkv": i["L1_attn_b_qkv"][order],
        "wout": rows(i["L1_attn_W_out"].T), "bout": i["L1_attn_b_out"],
        "gate_w": rows(i["L1_ffn_gate_w"]),
        "w1": rows(i["L1_ffn_w1"].transpose(1, 0, 2).reshape(D, E * HID)),
        "w2": rows(i["L1_ffn_w2"].reshape(E * HID, D)),
        "s1": rows(i["L1_ffn_shared_w1"]), "s2": rows(i["L1_ffn_shared_w2"]),
        "b1": np.concatenate([i["L1_ffn_b1"].reshape(-1, P), i["L1_ffn_shared_b1"].reshape(-1, P)]).T,
        "b2": i["L1_ffn_b2"], "sb2": i["L1_ffn_shared_b2"].reshape(1, D),
    }


def kernel(**inputs):
    import concourse.bacc as bacc
    from concourse.bass_utils import run_bass_kernel_spmd

    given = {n: np.asarray(v) for n, v in inputs.items()}
    arrays = {f"in_{n}": np.ascontiguousarray(v) for n, v in {**layout(given), **host_constants()}.items()}
    nc = bacc.Bacc("TRN2", target_bir_lowering=False, num_devices=1)
    a = {n[3:]: nc.dram_tensor(n, v.shape, mybir.dt.from_np(v.dtype), kind="ExternalInput").ap() for n, v in arrays.items()}
    out = nc.dram_tensor("out", (B, D, T), F32, kind="ExternalOutput").ap()
    program(nc, a, out)
    return run_bass_kernel_spmd(nc, [arrays], core_ids=[0]).results[0]["out"]
```

```python
from contextlib import ExitStack

import numpy as np

import concourse.bass as bass
from concourse import mybir

F32 = mybir.dt.float32
F32R = mybir.dt.float32r
BF16 = mybir.dt.bfloat16
U32 = mybir.dt.uint32
ALU = mybir.AluOpType
ACT = mybir.ActivationFunctionType
AX = mybir.AxisListType
ds = bass.ds

P = 128
B = 8
T = 512
D = T
NT = T // P
E_CH = 128
TAPS = 3
EPS = 1e-5
NTILE, SLICE, GRID = 64, 8, 16
NCLUSTER = 8
BIG = 1e30
H0, G0, DH0 = 32, 4, 16
H1, DH1 = 16, 32
E, HID = 8, 256
LOOKUP = 2 * SLICE * GRID + 3


def host_constants():
    f = np.float32
    ident = np.eye(P, dtype=f)
    causal = np.where(np.arange(P)[None, :] > np.arange(P)[:, None], f(-BIG), f(0)).astype(f)
    depth = E_CH // 2
    angle = np.arange(T, dtype=f)[:, None] * (f(1) / f(10000.0) ** (np.arange(depth, dtype=f)[None] / f(depth)))
    pe = np.concatenate([np.sin(angle), np.cos(angle)], -1).astype(f)
    pe = pe.reshape(NT, P, E_CH).transpose(1, 0, 2)
    n = np.arange(NTILE)
    order = ((7 - n // NCLUSTER) * 256 + (7 - n % NCLUSTER)).astype(f)
    small = np.concatenate([order, np.arange(GRID, dtype=f), np.arange(1, GRID + 1, dtype=f)])
    theta = f(1) / f(10000.0) ** (np.arange(0, DH1, 2, dtype=f) / f(DH1))
    it = np.arange(T, dtype=f)[:, None] * theta[None]
    cos = np.concatenate([np.cos(it), np.cos(it)], -1)
    sin = np.concatenate([-np.sin(it), np.sin(it)], -1)
    rope = np.stack([cos, sin]).astype(f).reshape(2, NT, P, DH1).transpose(2, 0, 1, 3)
    pick = np.zeros((E, E, P), f)
    for e in range(E):
        pick[e, e] = 1
    earlier = (np.arange(E)[None, :] < np.arange(E)[:, None]).astype(f)
    return {
        "c_square": np.stack([ident, causal, np.ones((P, P), f)], 1),
        "c_pe": pe,
        "c_small": small,
        "c_rope": rope,
        "c_pick": pick.reshape(E, E * P),
        "c_earlier": earlier.reshape(-1),
    }


def flat(ap):
    return ap.rearrange("p a n -> p (a n)")


class Attention:

    def __init__(self, nc, ctx, name, heads, dh, shared_keys, q_planes, k_planes, carried):
        self.dh, self.shared = dh, shared_keys
        self.rows = 3 * dh
        self.top = -(-self.rows // 32) * 32
        self.all = self.top + 3
        self.heads, self.groups, self.units = heads, heads // 4, heads * 4
        self.q_planes, self.k_planes = q_planes, k_planes
        self.nk = 1 if shared_keys else 4

        def sem(n):
            return ctx.enter_context(nc.semaphore(f"{name}_{n}"))

        self.pool_carried, self.sp_carried = carried["pool"], carried["sp"]
        self.set = sem("rows_filled")
        self.stored = sem("qk_stored")
        self.loaded = [sem(f"qk_loaded{i}") for i in range(4)]
        self.qk_free = sem("qk_free")
        self.v_set = sem("v_set")
        self.scores = sem("scores")
        self.max = sem("row_max")
        self.split = sem("split")
        self.max_psum = sem("max_psum")
        self.max_rows = sem("max_rows")
        self.scores_t = sem("scores_t")
        self.probs = sem("probs")
        self.pv = sem("pv")
        self.taken = sem("taken")
        self.rsums_ready = sem("rsums_ready")
        self.normed = sem("normed")

    def buffers(self, sb, name):
        self.q = [sb(f"{name}_q{i}", [self.all, 4, T], F32R) for i in range(4)]
        self.k = [sb(f"{name}_k{i}", [self.all, self.nk, T], F32R) for i in range(4)]
        self.v = [sb(f"{name}_v{i}", [P, NT, 32 if self.shared else P]) for i in range(2)]
        self.ones = sb(f"{name}_ones", [P, 32])
        self.mx = sb(f"{name}_mx", [P, 2, 16])
        self.parts = sb(f"{name}_parts", [P, 2, 16, 3], BF16)
        self.rest = sb(f"{name}_rest", [P, 16])
        self.pt = sb(f"{name}_pt", [P, 8, T])
        self.sums = sb(f"{name}_sums", [P, T])


SPLIT = 5
FEW, MANY = 2, 3
BANK_MAX, BANK_OUT, BANK_SUM = 5, 6, 7
FILL = 24


def score_bank(x):
    return x % (FEW + MANY) if x < FILL else x % FEW


def transposed_bank(at, x):
    return x % (FEW + MANY) if x >= at.units - EXP + MANY else FEW + x % MANY


def last_user(bank, x):
    return next((y for y in range(x - 1, -1, -1) if bank(y) == bank(x)), None)
MAX_T, MAX_COPY, EXP, PV, TAKE, RSUM, UPPER = 19, 20, 27, 32, 33, 34, 43
STEPS_AFTER = UPPER + 1
MAX_AT = (0, 2, 4, 7)
RSUM_AT = (0, 2, 4, 6)


def attention_set(dve, at):
    link = chain(dve, at.set, 0, [0])

    def fill(of, rows):
        link(dve.tensor_copy(of[rows], at.sums[rows].unsqueeze(1).to_broadcast([of[rows].shape[0], of.shape[1], T])))

    if at.rows < at.top:
        link(dve.memset(at.sums[:], 0.0))
        for of in at.q + at.k:
            fill(of, slice(at.top - 32, at.top))
    link(dve.memset(at.sums[:], 1.0))
    for of in at.k:
        fill(of, slice(at.top, at.all))
    link(dve.tensor_copy(at.ones[:], at.sums[:, 0:32]))


def constant_rows(at):
    return 6 + (9 if at.rows < at.top else 0)


def load_heads(sp, at, b, groups):
    carry_wait(sp, at.sp_carried)
    for g in groups:
        slot = g % 4
        sp.wait_ge(at.qk_free, b * at.groups + g + 1)
        for n, (qp, kp) in enumerate(((0, 0), (0, 1), (1, 0))):
            rows = slice(n * at.dh, (n + 1) * at.dh)
            sp.dma_start(at.q[slot][rows].bitcast(F32), at.q_planes[ds(b * 2 + qp, 1), g * 4:g * 4 + 4]
                         .rearrange("a h d s -> d (a h) s")).then_inc(at.loaded[slot], 16)
            keys = g if at.shared else g * 4
            sp.dma_start(at.k[slot][rows].bitcast(F32), at.k_planes[ds(b * 2 + kp, 1), keys:keys + at.nk]
                         .rearrange("a h d s -> d (a h) s")).then_inc(at.loaded[slot], 16)


def attend_pool(pool, at, v, b, out, lower):
    n = at.v[0].shape[2]
    for g in range(at.groups + 2):
        if g < at.groups:
            if g >= 2:
                pool.wait_ge(at.pv, b * at.units // 4 + (g - 1) * 4)
            carry_wait(pool, at.pool_carried)
            pool.tensor_copy(at.v[g % 2][:], v[:, :, g * n:(g + 1) * n]).then_inc(at.v_set, 1)
            pool.wait_ge(at.max, b * at.units + (g + 1) * 16)
            if g >= 2:
                pool.wait_ge(at.max_psum, b * at.heads + (g - 1) * 4)
            link = chain(pool, at.split, (b * at.groups + g) * SPLIT, [0])
            carry_wait(pool, at.pool_carried)
            mx, parts = at.mx[:, g % 2], at.parts[:, g % 2]
            link(pool.tensor_copy(parts[:, :, 0], mx))
            link(pool.tensor_tensor(at.rest[:], mx, parts[:, :, 0], ALU.subtract))
            carry_wait(pool, at.pool_carried)
            link(pool.tensor_copy(parts[:, :, 1], at.rest[:]))
            link(pool.tensor_tensor(at.rest[:], at.rest[:], parts[:, :, 1], ALU.subtract))
            carry_wait(pool, at.pool_carried)
            link(pool.tensor_copy(parts[:, :, 2], at.rest[:]))
        if g >= 2:
            pool.wait_ge(at.rsums_ready, (b * at.groups + g - 1) * NT)
            pool.wait_ge(at.taken, (b * at.groups + g - 1) * 2)
            pool.tensor_tensor(out(g - 2), out(g - 2), at.sums[:], ALU.mult).then_inc(at.normed, 1)
            lower(g - 2)


def attend_pe(pe, at, ps, ident_b, mask_b, b):

    def scores(x):
        g, j, i = x // 16, x % 16 // 4, x % 4
        if x % 16 == 0:
            pe.wait_ge(at.loaded[g % 4], (b * (at.groups // 4) + g // 4 + 1) * 96)
        before = last_user(score_bank, x)
        if before is not None:
            pe.wait_ge(at.max, b * at.units + before + 1)
        keys = (i + 1) * P
        bank = ps[score_bank(x)]
        pe.matmul(bank[:, 0:keys], at.q[g % 4][0:at.rows, j, i * P:keys],
                  at.k[g % 4][0:at.rows, 0 if at.shared else j, 0:keys], start=True, stop=False)
        pe.matmul(bank[:, i * P:keys], ident_b, mask_b, start=False, stop=True).then_inc(at.scores, 1)

    def max_rows(g, j):
        if j == 0:
            pe.wait_ge(at.split, (b * at.groups + g + 1) * SPLIT)
        if g + j > 0:
            pe.wait_ge(at.max_rows, b * at.heads + g * 4 + j)
        for i in range(NT):
            turned = pe.matmul(ps[BANK_MAX][at.top:at.all, i * P:(i + 1) * P], at.parts[:, g % 2, j * 4 + i],
                               ident_b, start=True, stop=True)
        turned.then_inc(at.max_psum, 1)

    def transposed(x):
        g, kt, j = x // 16, x % 16 // 4, x % 4
        bank = ps[transposed_bank(at, x)]
        if kt == 0:
            pe.wait_ge(at.max_rows, b * at.heads + g * 4 + j + 1)
        before = last_user(lambda y: transposed_bank(at, y), x)
        if before is not None:
            pe.wait_ge(at.probs, b * at.units + before + 1)
        if x == at.units - EXP + MANY:
            pe.wait_ge(at.max, b * at.units + at.units)
        less_max = pe.matmul(bank[:, 0:(NT - kt) * P], at.k[g % 4][:, 0 if at.shared else j, kt * P:(kt + 1) * P],
                             at.q[g % 4][:, j, kt * P:], start=True, stop=False)
        if x % 16 == 15:
            less_max.then_inc(at.qk_free, 1)
        pe.matmul(bank[:, 0:P], mask_b, ident_b, start=False, stop=True).then_inc(at.scores_t, 1)

    def products(x):
        g, kt = x // 16, x % 16 // 4
        if kt == 0:
            pe.wait_ge(at.v_set, b * at.groups + g + 1)
            if g > 0:
                pe.wait_ge(at.taken, (b * at.groups + g) * 2)
        pe.wait_ge(at.probs, b * at.units + x + 4)
        for bank in (BANK_OUT, BANK_SUM):
            for j in range(4):
                left = (at.ones[:] if bank == BANK_SUM else
                        at.v[g % 2][:, kt] if at.shared else at.v[g % 2][:, kt, j * 32:(j + 1) * 32])
                product = pe.matmul(ps[bank][j * 32:(j + 1) * 32, kt * P:], left, at.pt[:, (x + j) % 8, kt * P:],
                                    start=(kt == 0), stop=(kt == NT - 1))
        product.then_inc(at.pv, 1)

    for s in range(at.units + STEPS_AFTER):
        x = s - EXP
        if 0 <= x < at.units:
            transposed(x)
        if s < at.units:
            scores(s)
        x = s - MAX_T
        if 0 <= x < at.units and x % 16 in MAX_AT:
            max_rows(x // 16, MAX_AT.index(x % 16))
        x = s - PV
        if 0 <= x < at.units and x % 4 == 0:
            products(x)


def attend_dve(dve, at, ps, b, between=None):
    for s in range(at.units + STEPS_AFTER):
        if between:
            between(s)
        x = s
        if x < at.units:
            if x % 16 == 0 and x >= 32:
                dve.wait_ge(at.split, (b * at.groups + x // 16 - 1) * SPLIT)
            dve.wait_ge(at.scores, b * at.units + x + 1)
            dve.tensor_reduce(at.mx[:, x // 16 % 2, x % 16:x % 16 + 1], ps[score_bank(x)][:, 0:(x % 4 + 1) * P], AX.X, ALU.max,
                              negate=True).then_inc(at.max, 1)
        x = s - RSUM - 12
        if 0 <= x < at.units and x % 16 in RSUM_AT:
            g, i = x // 16, RSUM_AT.index(x % 16)
            if i == 0:
                dve.wait_ge(at.taken, (b * at.groups + g) * 2 + 1)
            tile = at.sums[:, i * P:(i + 1) * P]
            dve.reciprocal(tile, tile).then_inc(at.rsums_ready, 1)


def attend_act(act, at, ps, b, out, out_free, upper):
    for s in range(at.units + STEPS_AFTER):
        x = s - MAX_COPY
        if 0 <= x < at.units and x % 16 in MAX_AT:
            g, j = x // 16, MAX_AT.index(x % 16)
            act.wait_ge(at.max_psum, b * at.heads + g * 4 + j + 1)
            act.copy(at.q[g % 4][at.top:at.all, j], ps[BANK_MAX][at.top:at.all]).then_inc(at.max_rows, 1)
        x = s - EXP
        if 0 <= x < at.units:
            kt = x % 16 // 4
            act.wait_ge(at.scores_t, b * at.units + x + 1)
            if x >= 8:
                act.wait_ge(at.pv, b * at.units // 4 + x // 4 - 1)
            act.activation(at.pt[:, x % 8, kt * P:], ps[transposed_bank(at, x)][:, 0:(NT - kt) * P], ACT.Exp).then_inc(at.probs, 1)
        x = s - TAKE
        if 0 <= x < at.units and x % 16 == 12:
            g = x // 16
            act.wait_ge(at.pv, b * at.units // 4 + x // 4 + 1)
            if g >= 1:
                act.wait_ge(at.normed, b * at.groups + g)
            act.copy(at.sums[:], ps[BANK_SUM][:]).then_inc(at.taken, 1)
            if out_free and g >= 2:
                act.wait_ge(out_free, b * at.groups + g - 1)
            act.copy(out(g), ps[BANK_OUT][:]).then_inc(at.taken, 1)
        x = s - UPPER
        if 0 <= x < at.units and x % 16 == 12:
            upper(x // 16)


def carry_wait(eng, carried):
    eng.sem_inc(carried, 1)


class Norm:

    def __init__(self, ctx, nc, name, per, carried):
        self.per = per
        self.carried = carried["dve"]
        self.var = ctx.enter_context(nc.semaphore(f"{name}_var"))
        self.rstd = ctx.enter_context(nc.semaphore(f"{name}_rstd"))

    def buffers(self, sb, name):
        self.stats = sb(f"{name}_stats", [P, NT, 6])
        self.mv = sb(f"{name}_mv", [P, NT, 2])
        self.ve = sb(f"{name}_ve", [P, NT])
        self.r = sb(f"{name}_r", [P, NT])


def norm_stats(dve, link, nm, x):
    for t in range(NT):
        last = dve.bn_stats(nm.stats[:, t], x[:, t])
    link(last)
    carry_wait(dve, nm.carried)
    for t in range(NT):
        last = dve.bn_aggr(nm.mv[:, t], nm.stats[:, t])
    link(last)
    dve.tensor_scalar(nm.ve[:], nm.mv[:, :, 1], EPS, None, ALU.add).then_inc(nm.var, 1)


def norm_apply(dve, nm, x, out, b, k):
    dve.wait_ge(nm.rstd, b * nm.per + k + 1)
    for t in range(NT):
        last = dve.tensor_scalar(out[:, t], x[:, t], nm.mv[:, t, 0:1], nm.r[:, t:t + 1], ALU.subtract, ALU.mult)
    return last


def norm_dve(dve, link, nm, x, out, b, k):
    norm_stats(dve, link, nm, x)
    return norm_apply(dve, nm, x, out, b, k)


def norm_pool(pool, nm, power, b, k):
    pool.wait_ge(nm.var, b * nm.per + k + 1)
    pool.tensor_tensor(nm.r[:], nm.ve[:], power[:, 0:NT], ALU.pow).then_inc(nm.rstd, 1)


def chain(eng, sem, base, done):
    def link(ins):
        done[0] += 1
        ins.then_inc(sem, 1)
        eng.wait_ge(sem, base + done[0])
    return link


def phase_one(nc, carried, keep, a, scratch):
    with ExitStack() as ctx:
        def sb(name, shape, dt=F32):
            return ctx.enter_context(nc.sbuf_tensor("a_" + name, shape, dt))

        def sem(name):
            return ctx.enter_context(nc.semaphore("a_" + name))

        ps = [ctx.enter_context(nc.psum_tensor(f"a_ps{i}", [P, T], F32)) for i in range(8)]
        at = Attention(nc, ctx, "a_at", H0, DH0, True, scratch["q0"], scratch["k0"], carried)
        at.buffers(sb, "at")
        nm = Norm(ctx, nc, "a_ln", 1, carried)
        nm.buffers(sb, "ln")

        square = sb("square", [P, 3, P])
        ident, causal, ones = square[:, 0], square[:, 1], square[:, 2]
        ident_b = sb("ident_b", [P, P], BF16)
        mask_b = sb("mask_b", [P, P], BF16)
        pe_t = sb("pe", [P, NT, E_CH])
        convw = sb("convw", [P, TAPS, P])
        convb = sb("convb", [P, P])
        spos = sb("spos", [P, 2, P])
        power = sb("power", [P, NT])
        ids = sb("ids", [P, B * NT], U32)
        ids_now = sb("ids_now", [P, NT], U32)
        wq = sb("wq", [P, NT, D], F32R)
        wk = sb("wk", [P, NT, P], F32R)
        wv = sb("wv", [P, NT, P], F32R)
        wo = sb("wo", [P, 2 * NT, D], F32R)
        wparts = [(wq, D), (wk, P), (wv, P), (wo, D)]
        asum = sb("asum", [P, 4])
        mean_abs = sb("mean_abs", [P, 4])
        wscale = sb("wscale", [P, 5])
        slopes = sb("slopes", [P, NT, GRID])
        ssum = sb("ssum", [P, NT])
        ssign = sb("ssign", [P, NT])
        sdiag = sb("sdiag", [P, NT, P])
        slope_sign = keep["slope_sign"]

        emb = sb("emb", [P, NT, E_CH])
        tok_both = sb("tok", [P, 2 * NT, E_CH])
        tok = [tok_both[:, 0:NT], tok_both[:, NT:]]
        tmx = sb("tmx", [P, NT])
        texp = sb("texp", [P, NT, E_CH])
        tsum = sb("tsum", [P, NT])
        trs = sb("trs", [P, NT])
        sel = sb("sel", [P, NT, E_CH])
        sel_t = sb("sel_t", [P, T])
        xpad = sb("xpad", [P, T + TAPS - 1])
        built = sb("built", [P, NT, D])
        h = sb("h", [P, NT, D])
        x = sb("x", [P, NT, D])
        oth = sb("oth", [P, 2 * NT, T], F32R)
        otl = sb("otl", [P, 2 * NT, T], F32R)
        xh, xl = oth[:, 0:NT], otl[:, 0:NT]
        o32 = [sb("o32_0", [P, T]), sb("o32_1", [P, T])]
        qh = sb("qh", [P, NT + 1, T], F32R)
        ql = sb("ql", [P, NT + 1, T], F32R)
        v = sb("v", [P, NT, H0 // G0, 32])

        raw = [h[:], *(x[:, n].rearrange("p (c n) -> p c n", c=NT) for n in range(2)), at.pt[:]]

        consts = sem("consts")
        raw_in = sem("raw_in")
        first_stored = sem("first_stored")
        bf_ready = sem("bf_ready")
        pool_set = sem("pool_set")
        asum_ready = sem("asum_ready")
        mean_psum = sem("mean_psum")
        w_ready = sem("w_ready")
        sdiag_ready = sem("sdiag_ready")
        sign_psum = sem("sign_psum")
        ssign_ready = sem("ssign_ready")
        pool_carried = carried["pool"]
        ids_set = sem("ids_set")
        emb_in = sem("emb_in")
        tok_ready = sem("tok_ready")
        tmx_ready = sem("tmx_ready")
        texp_ready = sem("texp_ready")
        sel_ready = sem("sel_ready")
        tok_t = sem("tok_t")
        selt_psum = sem("selt_psum")
        selt_ready = sem("selt_ready")
        xpad_ready = sem("xpad_ready")
        ext_psum = sem("ext_psum")
        conv_psum = sem("conv_psum")
        h_built = sem("h_built")
        x_ready = sem("x_ready")
        xt_psum = sem("xt_psum")
        hi_ready = sem("hi_ready")
        lo_ready = sem("lo_ready")
        q_psum = sem("q_psum")
        qhi_ready = sem("qhi_ready")
        qlo_ready = sem("qlo_ready")
        v_psum = sem("v_psum")
        v_ready = sem("v_ready")
        ohi_ready = sem("ohi_ready")
        olo_ready = sem("olo_ready")
        o_psum = sem("o_psum")
        h_done = sem("h_done")
        h_set = sem("h_set")
        h_out = sem("h_out")
        dve_chain = sem("dve_chain")
        BUILD_STEPS, DVE_STEPS = 2, 4
        QK_ORDER = (NT, *range(NT))

        def over_sequences(eng, build, body):
            build(0)
            with eng.Fori(0, B - 1) as b:
                body(b, True)
            body(B - 1, False)

        with nc.Block() as block:
            @block.sync
            def _(sp):
                sp.sem_inc(at.stored, 1)
                sp.sem_inc(h_out, 1)
                for w, of in zip(raw, ("wq", "wk", "wv", "wo")):
                    sp.dma_start(w, a[of]).then_inc(raw_in, 16)
                loads = [(square, a["c_square"]), (pe_t, a["c_pe"]), (convw, a["convw"]), (spos, a["spos"]),
                         (slopes, a["slopes_rows"]),
                         (convb, a["convb"].partition_broadcast(P)), (ids, a["ids"])]
                for to, of in loads:
                    sp.dma_start(to[:], of).then_inc(consts, 16)
                assert len(loads) == 7
                sp.wait_ge(at.set, constant_rows(at))
                with sp.Fori(0, B) as b:
                    for n, m in enumerate(QK_ORDER):
                        sp.wait_ge(qlo_ready, b * 5 + n + 1)
                        for plane, half in enumerate((qh, ql)):
                            to = (scratch["q0"][ds(b * 2 + plane, 1), m * 8:(m + 1) * 8] if m < NT
                                  else scratch["k0"][ds(b * 2 + plane, 1)])
                            sp.dma_start(to.rearrange("a h d s -> (a h d) s"), half[:, m].bitcast(F32)) \
                              .then_inc(first_stored if n < 2 else at.stored, 16)
                        if n == 2:
                            sp.wait_ge(first_stored, b * 64 + 64)
                            load_heads(sp, at, b, (0, 1))
                    sp.wait_ge(at.stored, b * 96 + 96 + 1)
                    load_heads(sp, at, b, range(2, at.groups))
                    sp.wait_ge(h_done, b * 4 + 4 + 1)
                    sp.dma_start(scratch["h0"][ds(b, 1)].rearrange("a p n -> (a p) n"),
                                 h[:].rearrange("p t n -> p (t n)")).then_inc(h_out, 16)
                sp.wait_ge(h_out, B * 16 + 1)

            @block.gpsimd
            def _(pool):
                pool.memset(power[:], -0.5).then_inc(pool_set, 1)
                pool.wait_ge(pool_set, 1)
                pool.wait_ge(consts, 7 * 16)
                v_rows = v[:].rearrange("p t g d -> p t (g d)")

                def gather(s):
                    pool.wait_ge(tok_ready, s * 2 + 1)
                    pool.tensor_copy(ids_now[:], ids[:, ds(s * NT, NT)]).then_inc(ids_set, 1)
                    pool.wait_ge(ids_set, s + 1)
                    carry_wait(pool, pool_carried)
                    for t in range(NT):
                        pool.indirect_dma_start(
                            out=emb[:, t], out_offset=None, in_=a["table"],
                            in_offset=bass.IndirectOffsetOnAxis(ap=ids_now[:, t:t + 1], axis=0)).then_inc(emb_in, 16)

                def sequence(b, more):
                    norm_pool(pool, nm, power, b, 0)
                    if more:
                        gather(b + 1)
                    pool.wait_ge(v_ready, b + 1)

                    def lower_of_group(g):
                        pool.wait_ge(ohi_ready, b * at.groups + g + 1)
                        pool.tensor_tensor(otl[:, g], o32[g % 2][:], oth[:, g].bitcast(F32),
                                           ALU.subtract).then_inc(olo_ready, 1)

                    attend_pool(pool, at, v_rows, b, lambda g: o32[g % 2][:], lower_of_group)

                over_sequences(pool, gather, sequence)

            @block.scalar
            def _(act):
                act.wait_ge(asum_ready, 1)
                for (w, _), of in zip(wparts, raw):
                    act.activation(w[:], of, ACT.Sign).then_inc(w_ready, 1)
                act.wait_ge(asum_ready, 2)
                act.activation(ssign[:], ssum[:], ACT.Sign).then_inc(ssign_ready, 1)
                act.wait_ge(bf_ready, 5)

                def build(s):
                    for z in range(2):
                        act.wait_ge(tmx_ready, s * 2 + z + 1)
                        for t in range(NT):
                            last = act.activation(texp[:, t], tok[z][:, t], ACT.Exp, bias=tmx[:, t:t + 1], scale=1.0,
                                                  accum_out=tsum[:, t:t + 1])
                        last.then_inc(texp_ready, 1)
                        act.wait_ge(tok_t, s * 2 + z + 1)
                        if z == 0:
                            act.copy(xpad[:, TAPS - 1:], ps[0][:]).then_inc(xpad_ready, 1)
                        act.copy(built[:, 2 * z], ps[0][:]).then_inc(h_built, 1)
                        act.wait_ge(ext_psum, s * 2 + z + 1)
                        act.copy(built[:, 2 * z + 1], ps[2][:]).then_inc(h_built, 1)

                def sequence(b, more):
                    def upper():
                        for c in range(NT):
                            act.wait_ge(xt_psum, b * 4 + c + 1)
                            act.copy(xh[:, c], ps[c][:]).then_inc(hi_ready, 1)

                    upper()
                    act.wait_ge(at.stored, b * 96 + 1)
                    for n, m in enumerate(QK_ORDER):
                        act.wait_ge(q_psum, b * 5 + n + 1)
                        act.activation(qh[:, m], ps[(4 + m) % 8][:], ACT.Copy,
                                       scale=wscale[:, 4:5] if m < NT else wscale[:, 1:2]).then_inc(qhi_ready, 1)

                    def upper_of_group(g):
                        act.wait_ge(at.normed, b * at.groups + g + 1)
                        act.copy(oth[:, g], o32[g % 2][:]).then_inc(ohi_ready, 1)

                    act.wait_ge(h_out, b * 16 + 1)
                    act.copy(h[:], built[:]).then_inc(h_set, 1)
                    attend_act(act, at, ps, b, lambda g: o32[g % 2][:], olo_ready, upper_of_group)
                    if more:
                        build(b + 1)

                over_sequences(act, build, sequence)

            @block.vector
            def _(dve):
                attention_set(dve, at)
                dve.sem_inc(tok_ready, 1)
                dve.sem_inc(h_done, 1)
                dve.memset(xpad[:, 0:TAPS - 1], 0.0).then_inc(bf_ready, 1)
                dve.memset(v[:], 0.0).then_inc(bf_ready, 1)
                dve.wait_ge(consts, 7 * 16)
                dve.tensor_copy(ident_b[:], ident).then_inc(bf_ready, 1)
                dve.tensor_copy(mask_b[:], causal).then_inc(bf_ready, 1)
                dve.wait_ge(raw_in, 64)
                for n, w in enumerate(raw):
                    last = dve.tensor_reduce(asum[:, n:n + 1], w, AX.XY, ALU.add, apply_absolute_value=True)
                last.then_inc(asum_ready, 1)
                dve.tensor_reduce(ssum[:], slopes[:], AX.X, ALU.add).then_inc(asum_ready, 1)
                dve.wait_ge(mean_psum, 1)
                for n, (_, w) in enumerate(wparts):
                    last = dve.tensor_scalar(wscale[:, n:n + 1], ps[0][:, n:n + 1], 1.0 / (w * D), EPS, ALU.mult, ALU.max)
                last.then_inc(mean_psum, 1)
                dve.wait_ge(mean_psum, 2)
                dve.tensor_scalar(wscale[:, 4:5], wscale[:, 0:1], DH0 ** -0.5, None, ALU.mult).then_inc(bf_ready, 1)
                dve.wait_ge(bf_ready, 5)
                dve.wait_ge(ssign_ready, 1)
                for c in range(NT):
                    dve.tensor_scalar(sdiag[:, c], ident, ssign[:, c:c + 1], None, ALU.mult).then_inc(sdiag_ready, 1)
                dve.wait_ge(sign_psum, 1)
                dve.tensor_copy(slope_sign[:], ps[1][:]).then_inc(sign_psum, 1)
                dve.wait_ge(sign_psum, 2)

                def build(s, link):
                    for z in range(2):
                        if z == 0:
                            dve.wait_ge(emb_in, s * 64 + 64)
                            dve.scalar_tensor_tensor(tok[0][:], emb[:], float(np.sqrt(np.float32(E_CH))), pe_t[:],
                                                     ALU.mult, ALU.add).then_inc(tok_ready, 1)
                        else:
                            dve.wait_ge(conv_psum, s + 1)
                            dve.tensor_tensor(tok[1][:], ps[3][:].rearrange("p (t c) -> p t c", t=NT),
                                              convb[:].unsqueeze(1).to_broadcast([P, NT, P]), ALU.add).then_inc(tok_ready, 1)
                        dve.wait_ge(tok_ready, s * 2 + z + 1 + 1)
                        dve.tensor_reduce(tmx[:], tok[z][:], AX.X, ALU.max, negate=True).then_inc(tmx_ready, 1)
                        dve.wait_ge(texp_ready, s * 2 + z + 1)
                        link(dve.reciprocal(trs[:], tsum[:]))
                        dve.tensor_tensor(sel[:], texp[:], trs[:].unsqueeze(2).to_broadcast([P, NT, E_CH]),
                                          ALU.mult).then_inc(sel_ready, 1)
                        dve.wait_ge(selt_psum, s * 2 + z + 1)
                        dve.tensor_copy(sel_t[:], ps[1][:]).then_inc(selt_ready, 1)

                def sequence(b, more):
                    steps = [0]
                    link = chain(dve, dve_chain, b * DVE_STEPS + BUILD_STEPS, steps)
                    dve.wait_ge(h_built, b * 4 + 4)
                    norm_dve(dve, link, nm, built, x, b, 0).then_inc(x_ready, 1)

                    def lower():
                        for c in range(NT):
                            dve.wait_ge(hi_ready, b * 4 + c + 1)
                            dve.tensor_tensor(xl[:, c], ps[c][:], xh[:, c].bitcast(F32), ALU.subtract).then_inc(lo_ready, 1)

                    lower()
                    for n, m in enumerate(QK_ORDER):
                        dve.wait_ge(qhi_ready, b * 5 + n + 1)
                        dve.scalar_tensor_tensor(ql[:, m], ps[(4 + m) % 8][:], wscale[:, 4:5] if m < NT else wscale[:, 1:2],
                                                 qh[:, m].bitcast(F32), ALU.mult, ALU.subtract).then_inc(qlo_ready, 1)
                    dve.wait_ge(v_psum, b + 1)
                    dve.tensor_scalar(v[:, :, :, 0:DH0].rearrange("p t g d -> p (t g) d"),
                                      ps[1][:].rearrange("p (n d) -> p n d", d=DH0), wscale[:, 2:3], None,
                                      ALU.mult).then_inc(v_ready, 1)
                    attend_dve(dve, at, ps, b)
                    if more:
                        build(b + 1, link)
                    dve.wait_ge(h_set, b + 1)
                    for t in range(NT):
                        dve.wait_ge(o_psum, b * 4 + t + 1)
                        dve.scalar_tensor_tensor(h[:, t], ps[4 + t][:], wscale[:, 3:4], h[:, t], ALU.mult, ALU.add) \
                           .then_inc(h_done, 1)
                    assert not more or steps[0] == DVE_STEPS

                over_sequences(dve, lambda s: build(s, chain(dve, dve_chain, 0, [0])), sequence)

            @block.tensor
            def _(pe):
                pe.wait_ge(asum_ready, 1)
                pe.wait_ge(consts, 7 * 16)
                pe.matmul(ps[0][:, 0:4], ones, asum[:], start=True, stop=True).then_inc(mean_psum, 1)
                for c in range(NT):
                    pe.wait_ge(sdiag_ready, c + 1)
                    last = pe.matmul(ps[1][:, c * P:(c + 1) * P], ones, sdiag[:, c], start=True, stop=True)
                last.then_inc(sign_psum, 1)
                pe.wait_ge(sign_psum, 2)
                pe.wait_ge(bf_ready, 5)
                pe.wait_ge(w_ready, 4)
                pe.sem_inc(at.qk_free, 4)

                def turn(to, of, ready):
                    for t in range(NT):
                        last = pe.transpose(to[:, t * P:(t + 1) * P], of[:, t], ident)
                    last.then_inc(ready, 1)

                def tokens(s, z):
                    pe.wait_ge(tok_ready, s * 2 + z + 1 + 1)
                    if z == 1:
                        pe.wait_ge(h_built, s * 4 + 2)
                    turn(ps[0], tok[z], tok_t)

                def convolution(s):
                    pe.wait_ge(xpad_ready, s + 1)
                    for t in range(NT):
                        for k in range(TAPS):
                            last = pe.matmul(ps[3][:, t * P:(t + 1) * P], xpad[:, t * P + k:t * P + k + P],
                                             convw[:, k], start=(k == 0), stop=(k == TAPS - 1))
                    last.then_inc(conv_psum, 1)

                def selection(s, z):
                    pe.wait_ge(sel_ready, s * 2 + z + 1)
                    turn(ps[1], sel, selt_psum)
                    pe.wait_ge(selt_ready, s * 2 + z + 1)
                    pe.matmul(ps[2][:], spos[:, z], sel_t[:], start=True, stop=True).then_inc(ext_psum, 1)

                def build(s):
                    tokens(s, 0)
                    convolution(s)
                    selection(s, 0)
                    tokens(s, 1)
                    selection(s, 1)

                def sequence(b, more):
                    def product(out, left, right, chunks=NT):
                        for c in range(chunks):
                            if chunks == NT:
                                pe.wait_ge(lo_ready, b * 4 + c + 1)
                            for half, hf in enumerate((oth, otl)):
                                last = pe.matmul(out, left(hf, c), right(hf, c), start=(c + half == 0), stop=(c == chunks - 1 and half == 1))
                        return last

                    pe.wait_ge(x_ready, b + 1)
                    for c in range(NT):
                        for t in range(NT):
                            last = pe.transpose(ps[c][:, t * P:(t + 1) * P], x[:, t, c * P:(c + 1) * P], ident)
                        last.then_inc(xt_psum, 1)
                    pe.wait_ge(h_done, b * 4 + 1)
                    product(ps[0][:], lambda hf, c: wk[:, c], lambda hf, c: hf[:, c]).then_inc(q_psum, 1)
                    for m in range(NT):
                        product(ps[4 + m][:], lambda hf, c: wq[:, c, m * P:(m + 1) * P],
                                lambda hf, c: hf[:, c]).then_inc(q_psum, 1)
                    for t in range(NT):
                        last = product(ps[1][:, t * P:(t + 1) * P], lambda hf, c: hf[:, c, t * P:(t + 1) * P],
                                       lambda hf, c: wv[:, c])
                    last.then_inc(v_psum, 1)
                    pe.wait_ge(qlo_ready, b * 5 + 5)
                    pe.wait_ge(v_ready, b + 1)
                    attend_pe(pe, at, ps, ident_b[:], mask_b[:], b)
                    pe.wait_ge(olo_ready, b * at.groups + at.groups)
                    if more:
                        tokens(b + 1, 0)
                    for t in range(NT):
                        if more and t == 1:
                            convolution(b + 1)
                        if more and t == 2:
                            selection(b + 1, 0)
                        if more and t == 3:
                            tokens(b + 1, 1)
                        product(ps[4 + t][:], lambda hf, c: hf[:, c, t * P:(t + 1) * P],
                                lambda hf, c: wo[:, c], 2 * NT).then_inc(o_psum, 1)
                    if more:
                        selection(b + 1, 1)

                over_sequences(pe, build, sequence)


def phase_route(nc, carried, keep, a, scratch):
    with ExitStack() as ctx:
        def sb(name, shape, dt=F32):
            return ctx.enter_context(nc.sbuf_tensor("r_" + name, shape, dt))

        def sem(name):
            return ctx.enter_context(nc.semaphore("r_" + name))

        nm = Norm(ctx, nc, "r_ln", 2, carried)
        nm.buffers(sb, "ln")
        small = sb("small", [P, NTILE + 2 * GRID])
        gamma = sb("gamma", [P, D])
        beta = sb("beta", [P, D])
        power = sb("power", [P, NT])
        h = [sb(f"h{k}", [P, NT, D]) for k in range(2)]
        x = [sb(f"x{k}", [P, NT, D]) for k in range(2)]
        xf = [sb(f"xf{k}", [P, NT, D]) for k in range(2)]
        sg = [sb(f"sg{k}", [P, NT, D]) for k in range(2)]
        ts = sb("ts", [P, NT, NTILE])
        cs = sb("cs", [P, NT * NCLUSTER])
        key = sb("key", [P, NT, NTILE])
        kmax = sb("kmax", [P, NT])
        oh = sb("oh", [P, NT, NTILE])
        pen = sb("pen", [P, NT, NTILE])
        xs = sb("xs", [P, NT, SLICE])
        ext = sb("ext", [P, 2, NT])
        cand = sb("cand", [P, 2, NT, NTILE])
        cmax = sb("cmax", [P, 2, NTILE])
        slope_sign = keep["slope_sign"]

        consts = sem("consts")
        pool_set = sem("pool_set")
        h_in = [sem("h_in0"), sem("h_in1")]
        xn2_ready = sem("xn2_ready")
        hn_ready = sem("hn_ready")
        hn_out = [sem("hn_out0"), sem("hn_out1")]
        xf_ready = sem("xf_ready")
        sg_ready = sem("sg_ready")
        norm_chain = sem("norm_chain")
        dve_chain = sem("dve_chain")
        DVE_STEPS = 16
        PAIRS = B // 2

        def over_pairs(eng, prepare, finish):
            def pair(i, more):
                for k in range(2):
                    if k == 0:
                        prepare(i * 2 + 1, i, 1)
                    elif more:
                        prepare(i * 2 + 2, i + 1, 0)
                    finish(i * 2 + k, i, k)

            prepare(0, 0, 0)
            with eng.Fori(0, PAIRS - 1) as i:
                pair(i, True)
            pair(PAIRS - 1, False)

        def all_rows(row):
            return row[:].unsqueeze(1).to_broadcast([P, NT, D])

        with nc.Block() as block:
            @block.sync
            def _(sp):
                for k in range(2):
                    sp.sem_inc(hn_out[k], 1)
                loads = [(small, a["c_small"]), (gamma, a["gamma"]), (beta, a["beta"])]
                for to, of in loads:
                    sp.dma_start(to[:], of.partition_broadcast(P)).then_inc(consts, 16)
                assert len(loads) == 3

                def load(s, k):
                    sp.dma_start(h[k][:].rearrange("p t n -> p (t n)"),
                                 scratch["h0"][ds(s, 1)].rearrange("a p n -> (a p) n")).then_inc(h_in[k], 16)

                def pair(i, more):
                    for k in range(2):
                        sp.wait_ge(hn_ready, i * 2 + k + 1)
                        if more:
                            load(i * 2 + k + 2, k)
                        sp.dma_start(scratch["h1"][ds(i * 2 + k, 1)].rearrange("a p n -> (a p) n"),
                                     x[k][:].rearrange("p t n -> p (t n)")).then_inc(hn_out[k], 16)

                load(0, 0)
                load(1, 1)
                with sp.Fori(0, PAIRS - 1) as i:
                    pair(i, True)
                pair(PAIRS - 1, False)
                for k in range(2):
                    sp.wait_ge(hn_out[k], PAIRS * 16 + 1)

            @block.gpsimd
            def _(pool):
                pool.memset(power[:], -0.5).then_inc(pool_set, 1)
                pool.wait_ge(pool_set, 1)
                pool.wait_ge(consts, 3 * 16)

                def prepare(s, i, k):
                    norm_pool(pool, nm, power, s, 0)
                    norm_pool(pool, nm, power, s, 1)
                    pool.wait_ge(xn2_ready, s + 1)
                    pool.tensor_tensor(xf[k][:], xf[k][:], all_rows(gamma), ALU.mult).then_inc(xf_ready, 1)
                    pool.wait_ge(xf_ready, s * 2 + 1)
                    pool.tensor_tensor(xf[k][:], xf[k][:], all_rows(beta), ALU.add).then_inc(xf_ready, 1)
                    pool.tensor_tensor(x[k][:], h[k][:], x[k][:], ALU.add).then_inc(hn_ready, 1)

                over_pairs(pool, prepare, lambda s, i, k: None)

            @block.scalar
            def _(act):
                def prepare(s, i, k):
                    act.wait_ge(xf_ready, s * 2 + 2)
                    act.activation(sg[k][:], xf[k][:], ACT.Sign).then_inc(sg_ready, 1)

                over_pairs(act, prepare, lambda s, i, k: None)

            @block.vector
            def _(dve):
                dve.memset(keep["best"][:], -BIG)
                dve.wait_ge(consts, 3 * 16)

                def prepare(s, i, k):
                    link = chain(dve, norm_chain, s * 5, [0])
                    dve.wait_ge(h_in[k], i * 16 + 16)
                    norm_stats(dve, link, nm, h[k])
                    dve.wait_ge(hn_out[k], i * 16 + 1)
                    link(norm_apply(dve, nm, h[k], x[k], s, 0))
                    norm_stats(dve, link, nm, x[k])
                    norm_apply(dve, nm, x[k], xf[k], s, 1).then_inc(xn2_ready, 1)

                def choose(s, i, k):
                    steps = [0]
                    link = chain(dve, dve_chain, s * DVE_STEPS, steps)
                    dve.wait_ge(sg_ready, s + 1)
                    link(dve.tensor_tensor(sg[k][:], sg[k][:], slope_sign[:].unsqueeze(1).to_broadcast([P, NT, D]), ALU.mult))
                    link(dve.tensor_reduce(ts[:], sg[k][:].rearrange("p t (n s) -> p (t n) s", s=SLICE), AX.X, ALU.add))
                    link(dve.tensor_reduce(cs[:], ts[:].rearrange("p t (c n) -> p (t c) n", c=NCLUSTER), AX.X, ALU.add))
                    link(dve.tensor_scalar(cs[:], cs[:], 2048.0, None, ALU.mult))
                    link(dve.scalar_tensor_tensor(key[:], ts[:], 8.0, small[:, 0:NTILE].unsqueeze(1).to_broadcast([P, NT, NTILE]),
                                                  ALU.mult, ALU.add))
                    keyc = key[:].rearrange("p t (c n) -> p (t c) n", c=NCLUSTER)
                    link(dve.tensor_tensor(keyc, keyc, cs[:].unsqueeze(2).to_broadcast([P, NT * NCLUSTER, 8]), ALU.add))
                    link(dve.tensor_reduce(kmax[:], key[:], AX.X, ALU.max))
                    link(dve.tensor_tensor(oh[:], key[:], kmax[:].unsqueeze(2).to_broadcast([P, NT, NTILE]), ALU.is_equal))
                    dve.tensor_copy(keep["onehot"][:, ds(s * NT, NT)], oh[:])
                    link(dve.tensor_scalar(pen[:], oh[:], 1.0, BIG, ALU.subtract, ALU.mult))
                    link(dve.tensor_tensor(sg[k][:].rearrange("p t (n s) -> p (t n) s", s=SLICE),
                                           xf[k][:].rearrange("p t (n s) -> p (t n) s", s=SLICE),
                                           oh[:].rearrange("p t n -> p (t n)").unsqueeze(2).to_broadcast([P, NT * NTILE, SLICE]),
                                           ALU.mult))
                    link(dve.tensor_reduce(xs[:], sg[k][:].rearrange("p t (n s) -> p t s n", s=SLICE), AX.X, ALU.add))
                    dve.tensor_copy(keep["slice"][:, ds(s * NT, NT)], xs[:])
                    dve.tensor_reduce(ext[:, 0], xs[:], AX.X, ALU.max)
                    link(dve.tensor_reduce(ext[:, 1], xs[:], AX.X, ALU.min, negate=True))
                    for e in range(2):
                        last = dve.tensor_tensor(cand[:, e], oh[:], ext[:, e].unsqueeze(2).to_broadcast([P, NT, NTILE]), ALU.mult)
                    link(last)
                    for e in range(2):
                        last = dve.tensor_tensor(cand[:, e], cand[:, e], pen[:], ALU.add)
                    link(last)
                    for e in range(2):
                        last = dve.tensor_reduce(cmax[:, e], cand[:, e].rearrange("p t n -> p n t"), AX.X, ALU.max)
                    link(last)
                    link(dve.tensor_tensor(keep["best"][:], keep["best"][:], cmax[:], ALU.max))
                    assert steps[0] == DVE_STEPS, steps

                over_pairs(dve, prepare, choose)


def phase_two(nc, carried, keep, a, scratch):
    with ExitStack() as ctx:
        def sb(name, shape, dt=F32):
            return ctx.enter_context(nc.sbuf_tensor("b_" + name, shape, dt))

        def sem(name):
            return ctx.enter_context(nc.semaphore("b_" + name))

        ps = [ctx.enter_context(nc.psum_tensor(f"b_ps{i}", [P, T], F32)) for i in range(8)]
        at = Attention(nc, ctx, "b_at", H1, DH1, False, scratch["q1"], scratch["k1"], carried)
        at.buffers(sb, "at")
        nm = Norm(ctx, nc, "b_ln", 1, carried)
        nm.buffers(sb, "ln")
        NCELL = SLICE * GRID
        QK_SCALE = [float(DH1) ** -0.5, 1.0]
        QKV_BANKS = [(1, 2, 3), (6, 7, 0)]

        square = sb("square", [P, 3, P])
        ident, causal = square[:, 0], square[:, 1]
        ident_b = sb("ident_b", [P, P], BF16)
        mask_b = sb("mask_b", [P, P], BF16)
        small = sb("small", [P, NTILE + 2 * GRID])
        rope = sb("rope", [P, 2, NT, DH1])
        power = sb("power", [P, NT])
        wqkv = sb("wqkv", [P, NT, 3 * D])
        wout = sb("wout", [P, NT, D])
        bqkv = sb("bqkv", [P, 3 * D])
        bout = sb("bout", [P, D])
        lookup = sb("lookup", [NTILE, LOOKUP])
        h = sb("h", [P, NT, D])
        h2 = sb("h2", [P, NT, D])
        x = sb("x", [P, NT, D])
        xt = sb("xt", [P, NT, T])
        oh = sb("oh", [P, NT, NTILE])
        oht = sb("oht", [NTILE, T])
        look = sb("look", [P, NT, LOOKUP])
        xs = sb("xs", [P, NT, SLICE])
        den = sb("den", [P, NT])
        rden = sb("rden", [P, NT])
        u = sb("u", [P, NT, SLICE])
        u16 = sb("u16", [P, NT * SLICE])
        cell = sb("cell", [P, NT * SLICE])
        cells = sb("cells", [P, NT * SLICE, GRID])
        picked = sb("picked", [P, NT * SLICE, GRID])
        picked2 = sb("picked2", [P, NT * SLICE, GRID])
        bs = sb("bs", [P, 2, NT * SLICE])
        delta = sb("delta", [P, NT, SLICE])
        v = sb("v", [P, NT, D])
        qk, qk_cos, qk_sin = (flat(at.pt[:, n * 2:n * 2 + 2]) for n in range(3))
        half_h = [sb(f"half_h{i}", [P, NT, P], F32R) for i in range(2)]
        half_l = [sb(f"half_l{i}", [P, NT, P], F32R) for i in range(2)]

        consts = sem("consts")
        pe_carried = carried["pe"]
        ready = sem("ready")
        pool_set = sem("pool_set")
        best_t = sem("best_t")
        lookup_ready = sem("lookup_ready")
        h_in = sem("h_in")
        oh_ready = sem("oh_ready")
        oht_psum = sem("oht_psum")
        oht_ready = sem("oht_ready")
        look_psum = sem("look_psum")
        look_ready = sem("look_ready")
        delta_ready = sem("delta_ready")
        spread = sem("spread")
        x_ready = sem("x_ready")
        xt_psum = sem("xt_psum")
        xt_even = sem("xt_even")
        xt_odd = sem("xt_odd")
        qkv_psum = sem("qkv_psum")
        qkv_taken = sem("qkv_taken")
        rot_ready = sem("rot_ready")
        rope_ready = sem("rope_ready")
        qkt_psum = sem("qkt_psum")
        qhi_ready = sem("qhi_ready")
        qlo_ready = sem("qlo_ready")
        o_psum = sem("o_psum")
        h2_ready = sem("h2_ready")
        h2_out = sem("h2_out")
        tile_stored = sem("tile_stored")
        h2_set = sem("h2_set")
        head_chain = sem("head_chain")
        dve_chain = sem("dve_chain")
        HEAD_STEPS, DVE_STEPS = 16, 12
        STATS_AT, APPLY_AT = 40, 72
        LOOK_BANKS = (1, 2, 3, 6)

        def over_sequences(eng, body):
            with eng.Fori(0, B - 1) as b:
                body(b, True)
            body(B - 1, False)

        with nc.Block() as block:
            @block.sync
            def _(sp):
                for credited in (at.stored, h2_out, tile_stored):
                    sp.sem_inc(credited, 1)
                loads = [(square[:], a["c_square"]), (rope[:], a["c_rope"]), (wqkv[:], a["wqkv"]), (wout[:], a["wout"]),
                         (lookup[:, 0:2 * NCELL], a["splines"]), (lookup[:, 2 * NCELL + 2:], a["output_scale"]),
                         (small[:], a["c_small"].partition_broadcast(P)), (bqkv[:], a["bqkv"].partition_broadcast(P)),
                         (bout[:], a["bout"].partition_broadcast(P))]
                for to, of in loads:
                    sp.dma_start(to, of).then_inc(consts, 16)
                assert len(loads) == 9
                sp.wait_ge(at.set, constant_rows(at))

                def load(s):
                    sp.dma_start(h[:].rearrange("p t n -> p (t n)"),
                                 scratch["h1"][ds(s, 1)].rearrange("a p n -> (a p) n")).then_inc(h_in, 16)

                def sequence(b, more):
                    if more:
                        sp.wait_ge(h2_set, b + 1)
                        load(b + 1)
                    for t in range(NT):
                        for s in range(2):
                            sp.wait_ge(qlo_ready, b * 8 + t * 2 + s + 1)
                            for plane, half in enumerate((half_h, half_l)):
                                to = scratch["q1" if s == 0 else "k1"][ds(b * 2 + plane, 1)]
                                sp.dma_start(to.rearrange("a (c h) d s -> (h d) (a c) s", c=4)[:, :, t * P:(t + 1) * P],
                                             half[s][:].bitcast(F32)).then_inc(at.stored, 16)
                        sp.wait_ge(at.stored, b * 256 + (t + 1) * 64 + 1)
                        sp.sem_inc(tile_stored, 1)
                    load_heads(sp, at, b, range(at.groups))
                    sp.wait_ge(h2_ready, b * 4 + 4 + 1)
                    sp.dma_start(scratch["h2"][ds(b, 1)].rearrange("a p n -> (a p) n"),
                                 h2[:].rearrange("p t n -> p (t n)")).then_inc(h2_out, 16)

                load(0)
                over_sequences(sp, sequence)
                sp.wait_ge(h2_out, B * 16 + 1)

            @block.gpsimd
            def _(pool):
                pool.sem_inc(spread, 1)
                pool.memset(power[:], -0.5).then_inc(pool_set, 1)
                pool.wait_ge(pool_set, 1)
                pool.wait_ge(consts, 9 * 16)

                def head(s):
                    pool.wait_ge(delta_ready, s + 1)
                    for t in range(NT):
                        pool.tensor_tensor(x[:, t].rearrange("p (n s) -> p n s", s=SLICE),
                                           oh[:, t].unsqueeze(2).to_broadcast([P, NTILE, SLICE]),
                                           delta[:, t].unsqueeze(1).to_broadcast([P, NTILE, SLICE]), ALU.mult).then_inc(spread, 1)
                    pool.wait_ge(h_in, s * 16 + 16)
                    pool.wait_ge(spread, s * 5 + 4 + 1)
                    pool.tensor_tensor(h[:], x[:], h[:], ALU.add).then_inc(spread, 1)

                def sequence(b, more):
                    for t in range(NT):
                        pool.wait_ge(qkv_taken, b * 8 + t * 2 + 1)
                        src = qk.rearrange("p (n two d) -> p n two d", two=2, d=DH1 // 2)
                        dst = qk_sin.rearrange("p (n two d) -> p n two d", two=2, d=DH1 // 2)
                        for half in range(2):
                            pool.tensor_tensor(dst[:, :, half], src[:, :, 1 - half],
                                               rope[:, 1, t, half * 16:(half + 1) * 16].unsqueeze(1).to_broadcast([P, 2 * H1, 16]),
                                               ALU.mult).then_inc(rot_ready, 1)
                        pool.wait_ge(rope_ready, b * 4 + t + 1)
                    pool.wait_ge(qkv_taken, b * 8 + 8)
                    if more:
                        head(b + 1)
                    attend_pool(pool, at, v, b, lambda g: xt[:, g],
                                lambda g: norm_pool(pool, nm, power, b + 1, 0) if more and g == 0 else None)

                head(0)
                norm_pool(pool, nm, power, 0, 0)
                over_sequences(pool, sequence)

            @block.scalar
            def _(act):
                act.wait_ge(ready, 2)

                def head(s):
                    act.wait_ge(oht_psum, s + 1)
                    act.copy(oht[:], ps[0][0:NTILE, :]).then_inc(oht_ready, 1)
                    for t in range(NT):
                        act.wait_ge(look_psum, s * 4 + t + 1)
                        act.copy(look[:, t], ps[LOOK_BANKS[t]][:, 0:LOOKUP]).then_inc(look_ready, 1)

                def sequence(b, more):
                    for c in (0, 2):
                        act.wait_ge(xt_psum, b * 4 + c + 1)
                        act.copy(xt[:, c], ps[c][:]).then_inc(xt_even, 1)
                    act.wait_ge(h2_out, b * 16 + 1)
                    act.copy(h2[:], h[:]).then_inc(h2_set, 1)
                    for t in range(NT):
                        for s in range(2):
                            act.wait_ge(qkt_psum, b * 8 + t * 2 + s + 1)
                            if s == 0:
                                act.wait_ge(tile_stored, b * 4 + t + 1)
                            act.activation(half_h[s][:], ps[4 + s][:].rearrange("p (c n) -> p c n", c=4), ACT.Copy,
                                           scale=QK_SCALE[s]).then_inc(qhi_ready, 1)
                    if more:
                        head(b + 1)
                    attend_act(act, at, ps, b, lambda g: xt[:, g], None, lambda g: None)

                head(0)
                over_sequences(act, sequence)

            @block.vector
            def _(dve):
                attention_set(dve, at)
                dve.sem_inc(h2_ready, 1)
                dve.wait_ge(consts, 9 * 16)
                dve.tensor_copy(ident_b[:], ident).then_inc(ready, 1)
                dve.tensor_copy(mask_b[:], causal).then_inc(ready, 1)
                dve.wait_ge(best_t, 2)
                dve.tensor_reduce(lookup[:, 2 * NCELL:2 * NCELL + 1], ps[1][0:NTILE, 0:P], AX.X, ALU.max,
                                  negate=True).then_inc(lookup_ready, 1)
                dve.tensor_reduce(lookup[:, 2 * NCELL + 1:2 * NCELL + 2], ps[0][0:NTILE, 0:P], AX.X, ALU.max).then_inc(lookup_ready, 1)

                def choice(s):
                    dve.wait_ge(spread, s * 5 + 1)
                    dve.tensor_copy(xs[:], keep["slice"][:, ds(s * NT, NT)])
                    dve.tensor_copy(oh[:], keep["onehot"][:, ds(s * NT, NT)]).then_inc(oh_ready, 1)

                def head(s, link):
                    dve.wait_ge(look_ready, s * 4 + 4)
                    least, most, scale = (look[:, :, 2 * NCELL + n] for n in range(3))
                    dve.wait_ge(oh_ready, s + 1)
                    dve.tensor_tensor(u[:], xs[:], least.unsqueeze(2).to_broadcast([P, NT, SLICE]), ALU.subtract)
                    link(dve.tensor_tensor(den[:], most, least, ALU.subtract))
                    link(dve.tensor_scalar(den[:], den[:], 1e-8, None, ALU.add))
                    link(dve.reciprocal(rden[:], den[:]))
                    link(dve.tensor_tensor(u[:], u[:], rden[:].unsqueeze(2).to_broadcast([P, NT, SLICE]), ALU.mult))
                    uf = u[:].rearrange("p t s -> p (t s)")
                    link(dve.tensor_scalar(uf, uf, 0.0, 1.0 - 1e-6, ALU.max, ALU.min))
                    link(dve.tensor_scalar(u16[:], uf, float(GRID), None, ALU.mult))
                    shape = [P, NT * SLICE, GRID]
                    link(dve.tensor_tensor(cells[:], u16[:].unsqueeze(2).to_broadcast(shape),
                                           small[:, NTILE + GRID:].unsqueeze(1).to_broadcast(shape), ALU.is_ge))
                    link(dve.tensor_reduce(cell[:], cells[:], AX.X, ALU.add))
                    link(dve.tensor_tensor(cells[:], cell[:].unsqueeze(2).to_broadcast(shape),
                                           small[:, NTILE:NTILE + GRID].unsqueeze(1).to_broadcast(shape), ALU.is_equal))
                    for n, pk in enumerate((picked, picked2)):
                        last = dve.tensor_tensor(pk[:].rearrange("p (t s) g -> p t (s g)", t=NT),
                                                 cells[:].rearrange("p (t s) g -> p t (s g)", t=NT),
                                                 look[:, :, n * NCELL:(n + 1) * NCELL], ALU.mult)
                    link(last)
                    for n, pk in enumerate((picked, picked2)):
                        last = dve.tensor_reduce(bs[:, n], pk[:], AX.X, ALU.add)
                    link(last)
                    link(dve.scalar_tensor_tensor(u16[:], cell[:], -1.0 / GRID, uf, ALU.mult, ALU.add))
                    link(dve.scalar_tensor_tensor(u16[:], u16[:], float(GRID), bs[:, 1], ALU.mult, ALU.mult))
                    link(dve.tensor_tensor(u16[:], u16[:], bs[:, 0], ALU.add))
                    dve.tensor_tensor(delta[:], u16[:].rearrange("p (t s) -> p t s", t=NT),
                                      scale.unsqueeze(2).to_broadcast([P, NT, SLICE]), ALU.mult).then_inc(delta_ready, 1)

                def sequence(b, more):
                    steps, head_steps = [0], [0]
                    link = chain(dve, dve_chain, b * DVE_STEPS, steps)
                    head_link = chain(dve, head_chain, (b + 1) * HEAD_STEPS, head_steps)
                    if more:
                        choice(b + 1)
                    for c in (1, 3):
                        dve.wait_ge(xt_psum, b * 4 + c + 1)
                        dve.tensor_copy(xt[:, c], ps[c][:]).then_inc(xt_odd, 1)
                    for t in range(NT):
                        dve.wait_ge(qkv_psum, b * 4 + t + 1)
                        banks = QKV_BANKS[t % 2]
                        link(dve.tensor_tensor(qk[:, 0:D], ps[banks[0]][:], bqkv[:, 0:D], ALU.add))
                        dve.tensor_tensor(qk[:, D:], ps[banks[1]][:], bqkv[:, D:2 * D], ALU.add).then_inc(qkv_taken, 1)
                        dve.tensor_tensor(v[:, t], ps[banks[2]][:], bqkv[:, 2 * D:], ALU.add).then_inc(qkv_taken, 1)
                        dve.wait_ge(qkv_taken, b * 8 + t * 2 + 1)
                        link(dve.tensor_tensor(qk_cos.rearrange("p (n d) -> p n d", d=DH1),
                                               qk.rearrange("p (n d) -> p n d", d=DH1),
                                               rope[:, 0, t].unsqueeze(1).to_broadcast([P, 2 * H1, DH1]), ALU.mult))
                        dve.wait_ge(rot_ready, b * 8 + t * 2 + 2)
                        dve.tensor_tensor(qk_cos, qk_cos, qk_sin, ALU.add).then_inc(rope_ready, 1)
                        for s in range(2):
                            dve.wait_ge(qhi_ready, b * 8 + t * 2 + s + 1)
                            dve.scalar_tensor_tensor(half_l[s][:], ps[4 + s][:].rearrange("p (c n) -> p c n", c=4), QK_SCALE[s],
                                                     half_h[s][:].bitcast(F32), ALU.mult, ALU.subtract).then_inc(qlo_ready, 1)
                    if more:
                        head(b + 1, head_link)

                    def between(s):
                        if more and s == STATS_AT:
                            dve.wait_ge(spread, b * 5 + 10 + 1)
                            norm_stats(dve, head_link, nm, h)
                        if more and s == APPLY_AT:
                            norm_apply(dve, nm, h, x, b + 1, 0).then_inc(x_ready, 1)

                    attend_dve(dve, at, ps, b, between)
                    dve.wait_ge(h2_set, b + 1)
                    for t in range(NT):
                        dve.wait_ge(o_psum, b * 4 + t + 1)
                        link(dve.tensor_tensor(h2[:, t], ps[4 + t][:], h2[:, t], ALU.add))
                        dve.tensor_tensor(h2[:, t], h2[:, t], bout[:], ALU.add).then_inc(h2_ready, 1)
                    assert steps[0] == DVE_STEPS, steps
                    assert not more or head_steps[0] == HEAD_STEPS, head_steps

                choice(0)
                first_link = chain(dve, head_chain, 0, [0])
                head(0, first_link)
                dve.wait_ge(spread, 5 + 1)
                norm_stats(dve, first_link, nm, h)
                norm_apply(dve, nm, h, x, 0, 0).then_inc(x_ready, 1)
                over_sequences(dve, sequence)

            @block.tensor
            def _(pe):
                pe.wait_ge(consts, 9 * 16)
                for k in range(2):
                    pe.transpose(ps[k][0:NTILE, 0:P], keep["best"][:, k], ident).then_inc(best_t, 1)
                pe.wait_ge(lookup_ready, 2)
                pe.wait_ge(ready, 2)
                pe.sem_inc(at.qk_free, 4)

                def head(s):
                    pe.wait_ge(oh_ready, s + 1)
                    carry_wait(pe, pe_carried)
                    for t in range(NT):
                        last = pe.transpose(ps[0][0:NTILE, t * P:(t + 1) * P], oh[:, t], ident)
                    last.then_inc(oht_psum, 1)
                    pe.wait_ge(oht_ready, s + 1)
                    for t in range(NT):
                        pe.matmul(ps[LOOK_BANKS[t]][:, 0:LOOKUP], oht[:, t * P:(t + 1) * P], lookup[:],
                                  start=True, stop=True).then_inc(look_psum, 1)
                    pe.wait_ge(look_ready, s * 4 + 4)

                def sequence(b, more):
                    def product(out, t, w):
                        for c in range(NT):
                            last = pe.matmul(out, xt[:, c, t * P:(t + 1) * P], w(c), start=(c == 0), stop=(c == NT - 1))
                        return last

                    pe.wait_ge(x_ready, b + 1)
                    for c in range(NT):
                        for t in range(NT):
                            last = pe.transpose(ps[c][:, t * P:(t + 1) * P], x[:, t, c * P:(c + 1) * P], ident)
                        last.then_inc(xt_psum, 1)
                    def qkv(t):
                        if t >= 2:
                            pe.wait_ge(qkv_taken, b * 8 + t * 2 - 2)
                        for s in range(3):
                            last = product(ps[QKV_BANKS[t % 2][s]][:], t, lambda c: wqkv[:, c, s * D:(s + 1) * D])
                        last.then_inc(qkv_psum, 1)

                    pe.wait_ge(xt_odd, b * 2 + 2)
                    pe.wait_ge(xt_even, b * 2 + 2)
                    pe.wait_ge(h2_ready, b * 4 + 1)
                    qkv(0)
                    for t in range(NT):
                        if t + 1 < NT:
                            qkv(t + 1)
                        pe.wait_ge(rope_ready, b * 4 + t + 1)
                        for s in range(2):
                            if t > 0:
                                pe.wait_ge(qlo_ready, b * 8 + t * 2 + s - 1)
                            for c in range(NT):
                                last = pe.transpose(ps[4 + s][:, c * P:(c + 1) * P], qk_cos[:, s * D + c * P:s * D + (c + 1) * P], ident)
                            last.then_inc(qkt_psum, 1)
                    if more:
                        pe.wait_ge(qkv_taken, b * 8 + 8)
                        head(b + 1)
                    pe.wait_ge(qlo_ready, b * 8 + 8)
                    attend_pe(pe, at, ps, ident_b[:], mask_b[:], b)
                    pe.wait_ge(at.normed, b * at.groups + at.groups)
                    for t in range(NT):
                        product(ps[4 + t][:], t, lambda c: wout[:, c]).then_inc(o_psum, 1)

                head(0)
                over_sequences(pe, sequence)


def phase_three(nc, carried, a, scratch, out):
    with ExitStack() as ctx:
        def sb(name, shape, dt=F32):
            return ctx.enter_context(nc.sbuf_tensor("m_" + name, shape, dt))

        def sem(name):
            return ctx.enter_context(nc.semaphore("m_" + name))

        ps = [ctx.enter_context(nc.psum_tensor(f"m_ps{i}", [P, T], F32)) for i in range(8)]
        nm = Norm(ctx, nc, "m_ln", 1, carried)
        nm.buffers(sb, "ln")
        ident = sb("ident", [P, 3, P])
        pick = sb("pick", [E, E * P])
        earlier = sb("earlier", [P, E, E])
        power = sb("power", [P, NT])
        euler = sb("euler", [P, NT, E])
        gate_w = sb("gate_w", [P, NT, E])
        w1 = sb("w1", [P, NT, E * HID])
        w2 = sb("w2", [P, 2 * E, D])
        s1 = sb("s1", [P, NT, D])
        s2 = sb("s2", [P, NT, D])
        b1 = sb("b1", [P, 2 * E + NT])
        b2 = sb("b2", [E + 1, D])
        h = sb("h", [P, NT, D])
        x = sb("x", [P, NT, D])
        y = sb("y", [P, NT, D])
        xt = sb("xt", [P, NT, T])
        logits = sb("logits", [P, NT, E])
        best = sb("best", [P, NT])
        above = sb("above", [P, NT * E, E])
        equal = sb("equal", [P, NT * E, E])
        rank = sb("rank", [P, NT * E])
        chosen = sb("chosen", [P, NT * E])
        shifted = sb("shifted", [P, NT, E])
        expo = sb("expo", [P, NT, E])
        total = sb("total", [P, NT])
        rtotal = sb("rtotal", [P, NT])
        gates = sb("gates", [P, NT, E])
        gates_t = sb("gates_t", [E + 1, T])
        act_out = [sb(f"act_out{i}", [P, T]) for i in range(3)]
        gated = [sb(f"gated{i}", [P, T]) for i in range(3)]

        consts = sem("consts")
        experts_in = sem("experts_in")
        pool_set = sem("pool_set")
        pe_carried = carried["pe"]
        pool_carried = carried["pool"]
        ones_set = sem("ones_set")
        h_in = sem("h_in")
        h_kept = sem("h_kept")
        x_ready = sem("x_ready")
        xt_psum = sem("xt_psum")
        xt_ready = sem("xt_ready")
        logit_psum = sem("logit_psum")
        shifted_ready = sem("shifted_ready")
        expo_ready = sem("expo_ready")
        gates_ready = sem("gates_ready")
        gates_psum = sem("gates_psum")
        gates_t_ready = sem("gates_t_ready")
        gate_psum = sem("gate_psum")
        hid_psum = sem("hid_psum")
        hid_ready = sem("hid_ready")
        gated_ready = sem("gated_ready")
        hid_used = sem("hid_used")
        y_ready = sem("y_ready")
        y_out = sem("y_out")
        dve_chain = sem("dve_chain")
        norm_chain = sem("norm_chain")
        DVE_STEPS = 10
        NH = 2 * E + NT
        NG = 2 * E
        GATES_AT = NT
        NORM_AT, APPLY_AT = NT + 4, NT + 6
        BANK_LOGITS, BANK_GATES = 6, 7

        def over_sequences(eng, body):
            with eng.Fori(0, B - 1) as b:
                body(b, True)
            body(B - 1, False)

        with nc.Block() as block:
            @block.sync
            def _(sp):
                sp.sem_inc(y_out, 1)
                loads = [(ident[:], a["c_square"]), (pick[:], a["c_pick"]), (earlier[:].rearrange("p a b -> p (a b)"), a["c_earlier"].partition_broadcast(P)),
                         (gate_w[:], a["gate_w"]), (s1[:], a["s1"]), (s2[:], a["s2"]),
                         (b1[:], a["b1"]), (b2[0:E], a["b2"]), (b2[E:E + 1], a["sb2"])]
                for to, of in loads:
                    sp.dma_start(to, of).then_inc(consts, 16)
                assert len(loads) == 9

                def load(b):
                    sp.dma_start(h[:].rearrange("p t n -> p (t n)"),
                                 scratch["h2"][ds(b, 1)].rearrange("a p n -> (a p) n")).then_inc(h_in, 16)

                def sequence(b, more):
                    if more:
                        sp.wait_ge(h_kept, b + 1)
                        load(b + 1)
                    sp.wait_ge(y_ready, b * 4 + 4 + 1)
                    sp.dma_start(out[ds(b, 1)].rearrange("a (t p) n -> p (a t) n", p=P), y[:]).then_inc(y_out, 16)

                load(0)
                sp.dma_start(w1[:], a["w1"]).then_inc(experts_in, 16)
                sp.dma_start(w2[:], a["w2"]).then_inc(experts_in, 16)
                over_sequences(sp, sequence)
                sp.wait_ge(y_out, B * 16 + 1)

            @block.gpsimd
            def _(pool):
                pool.memset(power[:], -0.5).then_inc(pool_set, 1)
                pool.memset(euler[:], float(np.e)).then_inc(pool_set, 1)
                pool.wait_ge(pool_set, 2)

                def sequence(b, more):
                    pool.wait_ge(x_ready, b + 1)
                    pool.wait_ge(y_out, b * 16 + 1)
                    carry_wait(pool, pool_carried)
                    pool.tensor_copy(y[:], h[:]).then_inc(h_kept, 1)
                    pool.wait_ge(shifted_ready, b + 1)
                    pool.tensor_tensor(expo[:], euler[:], shifted[:], ALU.pow).then_inc(expo_ready, 1)
                    if more:
                        norm_pool(pool, nm, power, b + 1, 0)

                norm_pool(pool, nm, power, 0, 0)
                over_sequences(pool, sequence)

            @block.scalar
            def _(act):
                act.wait_ge(consts, 9 * 16)

                def sequence(b, more):
                    for c in range(NT):
                        act.wait_ge(xt_psum, b * 4 + c + 1)
                        act.copy(xt[:, c], ps[4 + c][:]).then_inc(xt_ready, 1)
                    for n in range(NH):
                        act.wait_ge(hid_psum, b * NH + n + 1)
                        if n >= 3:
                            act.wait_ge(hid_used, b * NH + n - 2)
                        of = b1[:, (n + NG) % NH:(n + NG) % NH + 1]
                        act.activation(act_out[n % 3][:], ps[4 + n % 2][:], ACT.Gelu, bias=of, scale=1.0).then_inc(hid_ready, 1)

                over_sequences(act, sequence)

            @block.vector
            def _(dve):
                dve.sem_inc(y_ready, 1)
                dve.memset(gates_t[:], 1.0).then_inc(ones_set, 1)
                dve.wait_ge(ones_set, 1)
                dve.wait_ge(consts, 9 * 16)
                norm = chain(dve, norm_chain, 0, [0])
                dve.wait_ge(h_in, 16)
                norm_stats(dve, norm, nm, h)
                norm_apply(dve, nm, h, x, 0, 0).then_inc(x_ready, 1)

                def sequence(b, more):
                    steps = [0]
                    link = chain(dve, dve_chain, b * DVE_STEPS, steps)
                    dve.wait_ge(logit_psum, b + 1)
                    link(dve.tensor_copy(logits[:], ps[BANK_LOGITS][:, 0:NT * E].rearrange("p (t e) -> p t e", t=NT)))
                    link(dve.tensor_reduce(best[:], logits[:], AX.X, ALU.max))
                    dve.tensor_tensor(shifted[:], logits[:], best[:].unsqueeze(2).to_broadcast([P, NT, E]),
                                      ALU.subtract).then_inc(shifted_ready, 1)
                    mine = logits[:].unsqueeze(3).to_broadcast([P, NT, E, E])
                    theirs = logits[:].unsqueeze(2).to_broadcast([P, NT, E, E])
                    dve.tensor_tensor(above[:].rearrange("p (t e) f -> p t e f", t=NT), theirs, mine, ALU.is_gt)
                    link(dve.tensor_tensor(equal[:].rearrange("p (t e) f -> p t e f", t=NT), theirs, mine, ALU.is_equal))
                    link(dve.tensor_tensor(equal[:].rearrange("p (t e) f -> p t (e f)", t=NT),
                                           equal[:].rearrange("p (t e) f -> p t (e f)", t=NT),
                                           earlier[:].rearrange("p e f -> p (e f)").unsqueeze(1).to_broadcast([P, NT, E * E]), ALU.mult))
                    link(dve.tensor_tensor(above[:], above[:], equal[:], ALU.add))
                    link(dve.tensor_reduce(rank[:], above[:], AX.X, ALU.add))
                    link(dve.tensor_scalar(chosen[:], rank[:], 2.0, None, ALU.is_lt))
                    dve.wait_ge(expo_ready, b + 1)
                    link(dve.tensor_tensor(gates[:].rearrange("p t e -> p (t e)"), expo[:].rearrange("p t e -> p (t e)"), chosen[:], ALU.mult))
                    link(dve.tensor_reduce(total[:], gates[:], AX.X, ALU.add))
                    link(dve.reciprocal(rtotal[:], total[:]))
                    dve.tensor_tensor(gates[:], gates[:], rtotal[:].unsqueeze(2).to_broadcast([P, NT, E]), ALU.mult).then_inc(gates_ready, 1)
                    dve.wait_ge(gates_psum, b + 1)
                    dve.tensor_copy(gates_t[0:E, :], ps[BANK_GATES][0:E, :]).then_inc(gates_t_ready, 1)
                    for n in range(NT, NH):
                        dve.wait_ge(gate_psum, b * E + (n - NT) // 2 + 1)
                        dve.wait_ge(hid_ready, b * NH + n + 1)
                        if n >= NT + 3:
                            dve.wait_ge(hid_used, b * NH + n - 2)
                        dve.tensor_tensor(gated[n % 3][:], ps[6 + (n - NT) // 2 % 2][:], act_out[n % 3][:], ALU.mult).then_inc(gated_ready, 1)
                        if more and n == NORM_AT:
                            dve.wait_ge(h_in, b * 16 + 32)
                            norm_stats(dve, chain(dve, norm_chain, b * 2 + 2, [0]), nm, h)
                        if more and n == APPLY_AT:
                            norm_apply(dve, nm, h, x, b + 1, 0).then_inc(x_ready, 1)
                    dve.wait_ge(hid_used, b * NH + NH)
                    for t in range(NT):
                        dve.tensor_tensor(y[:, t], ps[t][:], y[:, t], ALU.add).then_inc(y_ready, 1)
                    assert steps[0] == DVE_STEPS

                over_sequences(dve, sequence)

            @block.tensor
            def _(pe):
                pe.wait_ge(ones_set, 1)
                pe.wait_ge(consts, 9 * 16)

                def sequence(b, more):
                    pe.wait_ge(x_ready, b + 1)
                    for c in range(NT):
                        for t in range(NT):
                            last = pe.transpose(ps[4 + c][:, t * P:(t + 1) * P], x[:, t, c * P:(c + 1) * P], ident[:, 0])
                        last.then_inc(xt_psum, 1)
                    pe.wait_ge(xt_ready, b * 4 + 4)
                    for t in range(NT):
                        for c in range(NT):
                            last = pe.matmul(ps[BANK_LOGITS][:, t * E:(t + 1) * E], xt[:, c, t * P:(t + 1) * P], gate_w[:, c],
                                             start=(c == 0), stop=(c == NT - 1))
                    last.then_inc(logit_psum, 1)

                    def turn_gates():
                        pe.wait_ge(gates_ready, b + 1)
                        carry_wait(pe, pe_carried)
                        for t in range(NT):
                            last = pe.transpose(ps[BANK_GATES][0:E, t * P:(t + 1) * P], gates[:, t], ident[:, 0])
                        last.then_inc(gates_psum, 1)

                    def hidden(n):
                        m = n - NT
                        if m >= 0 and m % 2 == 0:
                            if m >= 4:
                                pe.wait_ge(gated_ready, b * NG + m - 2)
                            pe.matmul(ps[6 + m // 2 % 2][:], pick[:, m // 2 * P:(m // 2 + 1) * P], gates_t[0:E, :],
                                      start=True, stop=True).then_inc(gate_psum, 1)
                        if n >= 2:
                            pe.wait_ge(hid_ready, b * NH + n - 1)
                        for c in range(NT):
                            w = w1[:, c, m * P:(m + 1) * P] if m >= 0 else s1[:, c, n * P:(n + 1) * P]
                            last = pe.matmul(ps[4 + n % 2][:], w, xt[:, c], start=(c == 0), stop=(c == NT - 1))
                        last.then_inc(hid_psum, 1)

                    def output(n):
                        m = n - NT
                        if m >= 0:
                            pe.wait_ge(gated_ready, b * NG + m + 1)
                        else:
                            pe.wait_ge(hid_ready, b * NH + n + 1)
                        if n == 0:
                            pe.wait_ge(y_ready, b * 4 + 1)
                        for t in range(NT):
                            left = (gated if m >= 0 else act_out)[n % 3][:, t * P:(t + 1) * P]
                            right = w2[:, m] if m >= 0 else s2[:, n]
                            last = pe.matmul(ps[t][:], left, right, start=(n == 0), stop=(n == NH - 1))
                        last.then_inc(hid_used, 1)

                    hidden(0)
                    for n in range(1, NH):
                        if n == GATES_AT - 1:
                            turn_gates()
                        if n == GATES_AT:
                            pe.wait_ge(gates_t_ready, b + 1)
                            pe.wait_ge(experts_in, 32)
                        hidden(n)
                        output(n - 1)
                        if n == GATES_AT:
                            for t in range(NT):
                                pe.matmul(ps[t][:], gates_t[:, t * P:(t + 1) * P], b2[:], start=False, stop=False)
                    output(NH - 1)

                over_sequences(pe, sequence)


def program(nc, a, out):
    def dram(name, shape):
        return nc.dram_tensor(name, shape, F32).ap()

    scratch = {
        "q0": dram("q0", (2 * B, H0, DH0, T)), "k0": dram("k0", (2 * B, H0 // G0, DH0, T)),
        "q1": dram("q1", (2 * B, H1, DH1, T)), "k1": dram("k1", (2 * B, H1, DH1, T)),
        "h0": dram("h0", (B, P, NT * D)), "h1": dram("h1", (B, P, NT * D)), "h2": dram("h2", (B, P, NT * D)),
    }
    with ExitStack() as ctx:
        carried = {n: ctx.enter_context(nc.semaphore("carried_" + n)) for n in ("pe", "dve", "pool", "sp")}
        keep_ctx = ctx.enter_context(ExitStack())
        keep = {n: keep_ctx.enter_context(nc.sbuf_tensor("keep_" + n, s, F32)) for n, s in (
            ("onehot", [P, B * NT, NTILE]),
            ("slice", [P, B * NT, SLICE]),
            ("best", [P, 2, NTILE]),
            ("slope_sign", [P, D]),
        )}
        phase_one(nc, carried, keep, a, scratch)
        phase_route(nc, carried, keep, a, scratch)
        phase_two(nc, carried, keep, a, scratch)
        keep_ctx.close()
        phase_three(nc, carried, a, scratch, out)


def layout(i):
    def rows(w):
        return w.reshape(-1, P, w.shape[-1]).transpose(1, 0, 2)

    n = np.arange(3 * D)
    s, head, d = n // D, n % D // DH1, n % DH1
    order = head * 3 * DH1 + s * DH1 + d
    wo_rows = np.zeros((H0, 32, D), i["L0_attn_wo"].dtype)
    wo_rows[:, 0:DH0] = i["L0_attn_wo"].T.reshape(H0, DH0, D)
    return {
        "ids": i["x"].reshape(B * NT, P).T.astype(np.uint32),
        "table": i["L0_tok_emb_table"],
        "convw": i["L0_tok_conv_w"].transpose(1, 2, 0),
        "convb": i["L0_tok_conv_b"],
        "spos": np.stack([i["L0_tok_spos0"], i["L0_tok_spos1"]], 1),
        "wq": rows(i["L0_attn_wq"].T), "wk": rows(i["L0_attn_wk"].T),
        "wv": rows(i["L0_attn_wv"].T), "wo": rows(wo_rows.reshape(2 * D, D)),
        "gamma": i["L0_ffn_ln_gamma"], "beta": i["L0_ffn_ln_beta"],
        "slopes_rows": i["L0_ffn_spline_slopes"].reshape(NT, P, GRID).transpose(1, 0, 2),
        "splines": np.concatenate([i["L0_ffn_spline_bases"].reshape(NTILE, -1),
                                   i["L0_ffn_spline_slopes"].reshape(NTILE, -1)], 1),
        "output_scale": i["L0_ffn_output_scale"].reshape(NTILE, 1),
        "wqkv": rows(i["L1_attn_W_qkv"][order].T), "bqkv": i["L1_attn_b_qkv"][order],
        "wout": rows(i["L1_attn_W_out"].T), "bout": i["L1_attn_b_out"],
        "gate_w": rows(i["L1_ffn_gate_w"]),
        "w1": rows(i["L1_ffn_w1"].transpose(1, 0, 2).reshape(D, E * HID)),
        "w2": rows(i["L1_ffn_w2"].reshape(E * HID, D)),
        "s1": rows(i["L1_ffn_shared_w1"]), "s2": rows(i["L1_ffn_shared_w2"]),
        "b1": np.concatenate([i["L1_ffn_b1"].reshape(-1, P), i["L1_ffn_shared_b1"].reshape(-1, P)]).T,
        "b2": i["L1_ffn_b2"], "sb2": i["L1_ffn_shared_b2"].reshape(1, D),
    }


def kernel(**inputs):
    import concourse.bacc as bacc
    from concourse.bass_utils import run_bass_kernel_spmd

    given = {n: np.asarray(v) for n, v in inputs.items()}
    arrays = {f"in_{n}": np.ascontiguousarray(v) for n, v in {**layout(given), **host_constants()}.items()}
    nc = bacc.Bacc("TRN2", target_bir_lowering=False, num_devices=1)
    a = {n[3:]: nc.dram_tensor(n, v.shape, mybir.dt.from_np(v.dtype), kind="ExternalInput").ap() for n, v in arrays.items()}
    out = nc.dram_tensor("out", (B, D, T), F32, kind="ExternalOutput").ap()
    program(nc, a, out)
    return run_bass_kernel_spmd(nc, [arrays], core_ids=[0]).results[0]["out"]
```
